# Optimizing a Trainium2 kernel written in Bass

```python
import numpy as np
import jax
import jax.numpy as jnp

def _softmax(x, axis=-1):
    return jax.nn.softmax(x, axis=axis)

def _gelu(x):
    return jax.nn.gelu(x, approximate=True)

def _silu(x):
    return jax.nn.silu(x)

def _sigmoid(x):
    return jax.nn.sigmoid(x)

def _layernorm(x, axis=-1, eps=1e-05):
    m = jnp.mean(x, axis=axis, keepdims=True)
    v = jnp.var(x, axis=axis, keepdims=True)
    return (x - m) / jnp.sqrt(v + eps)

def _scatter_add(tgt, idx, src, axis=0):
    return tgt.at[idx].add(src)

def _segment_sum(src, seg, n):
    return jax.ops.segment_sum(src, seg, n)
kernel_name = 'mk_seq_postln_d4_jaxref_r8_652be7'

def setup_inputs(seed: int=0):
    np.random.seed(seed)
    _w = jnp.asarray

    def _L0_attn_setup():
        import jax, jax.numpy as jnp
        import numpy as np
        N_EMBD = 128
        N_HEADS = 16
        HEAD_DIM = N_EMBD // N_HEADS
        NUM_BUCKETS = 32
        MAX_DISTANCE = 64

        def _relative_position_bucket(relative_position):
            rp = jnp.maximum(-relative_position, 0)
            max_exact = NUM_BUCKETS // 2
            is_small = rp < max_exact
            rp_f = jnp.maximum(rp, 1).astype(jnp.float32)
            large = max_exact + (jnp.log(rp_f / max_exact) / np.log(MAX_DISTANCE / max_exact) * (NUM_BUCKETS - max_exact)).astype(jnp.int32)
            large = jnp.minimum(large, NUM_BUCKETS - 1)
            return jnp.where(is_small, rp, large)
        key = jax.random.key(seed)
        ks = jax.random.split(key, 10)
        B, S = (2, 256)
        std = 1.0 / np.sqrt(N_EMBD)
        inp = {'hidden_states': jax.random.normal(ks[0], (B, S, N_EMBD), dtype=jnp.float32), 'Wq': jax.random.normal(ks[1], (N_EMBD, N_EMBD), dtype=jnp.float32) * std, 'bq': jnp.zeros((N_EMBD,), jnp.float32), 'Wk': jax.random.normal(ks[2], (N_EMBD, N_EMBD), dtype=jnp.float32) * std, 'bk': jnp.zeros((N_EMBD,), jnp.float32), 'Wv': jax.random.normal(ks[3], (N_EMBD, N_EMBD), dtype=jnp.float32) * std, 'bv': jnp.zeros((N_EMBD,), jnp.float32), 'Wo': jax.random.normal(ks[4], (N_EMBD, N_EMBD), dtype=jnp.float32) * std, 'bo': jnp.zeros((N_EMBD,), jnp.float32), 'rel_bias': jax.random.normal(ks[5], (NUM_BUCKETS, N_HEADS), dtype=jnp.float32) * 0.1}
        return inp
    _L0_attn_in = _L0_attn_setup()

    def _L0_ffn_setup():
        import jax, jax.numpy as jnp
        import numpy as np
        THRESH_FACTOR = 0.7

        def ternary_quantize(w):
            delta = THRESH_FACTOR * jnp.mean(jnp.abs(w))
            return jnp.where(w > delta, 1.0, jnp.where(w < -delta, -1.0, 0.0)).astype(w.dtype)
        key = jax.random.key(seed)
        k1, k2, k3 = jax.random.split(key, 3)
        B, S, D_IN, D_OUT = (8, 512, 128, 128)
        inp = {'input': jax.random.normal(k1, (B, S, D_IN), dtype=jnp.float32), 'weight': jax.random.normal(k2, (D_OUT, D_IN), dtype=jnp.float32) * (1.0 / np.sqrt(D_IN)), 'alpha': jnp.ones((1,), dtype=jnp.float32), 'bias': jax.random.normal(k3, (D_OUT,), dtype=jnp.float32) * (1.0 / np.sqrt(D_IN))}
        return inp
    _L0_ffn_in = _L0_ffn_setup()

    def _L1_attn_setup():
        import jax, jax.numpy as jnp
        import numpy as np
        from jax import lax
        B, T, D, H, K = (2, 256, 128, 16, 4)
        HD = D // H
        CONV_DIM = 3 * D

        def _l2norm(x, eps=1e-06):
            return x * lax.rsqrt(jnp.sum(x * x, axis=-1, keepdims=True) + eps)

        def _forward(x, W_qkv, conv_w, W_z, W_b, W_a, dt_bias, A_log, W_out):
            b_, t_, d_ = x.shape
            mixed = jnp.einsum('btd,cd->btc', x, W_qkv)
            c = mixed.transpose(0, 2, 1)
            c = lax.conv_general_dilated(c, conv_w, window_strides=(1,), padding=[(K - 1, 0)], dimension_numbers=('NCH', 'OIH', 'NCH'), feature_group_count=CONV_DIM)
            mixed = jax.nn.silu(c).transpose(0, 2, 1)
            q, k, v = jnp.split(mixed, [d_, 2 * d_], axis=-1)
            q = q.reshape(b_, t_, H, HD)
            k = k.reshape(b_, t_, H, HD)
            v = v.reshape(b_, t_, H, HD)
            z = jnp.einsum('btd,ed->bte', x, W_z).reshape(b_, t_, H, HD)
            beta = jax.nn.sigmoid(jnp.einsum('btd,hd->bth', x, W_b))
            g = -jnp.exp(A_log) * jax.nn.softplus(jnp.einsum('btd,hd->bth', x, W_a) + dt_bias)
            q = _l2norm(q) * HD ** (-0.5)
            k = _l2norm(k)
            qs = q.transpose(1, 0, 2, 3)
            ks_ = k.transpose(1, 0, 2, 3)
            vs = v.transpose(1, 0, 2, 3)
            bs = beta.transpose(1, 0, 2)
            gs = g.transpose(1, 0, 2)

            def step(S, inp):
                q_t, k_t, v_t, b_t, g_t = inp
                S = S * jnp.exp(g_t)[..., None, None]
                S = S + jnp.einsum('bhd,bhv->bhdv', k_t, v_t * b_t[..., None])
                o_t = jnp.einsum('bhd,bhdv->bhv', q_t, S)
                return (S, o_t)
            S0 = jnp.zeros((b_, H, HD, HD), x.dtype)
            _, out = lax.scan(step, S0, (qs, ks_, vs, bs, gs))
            out = out.transpose(1, 0, 2, 3)
            var = jnp.mean(out * out, axis=-1, keepdims=True)
            out = out * lax.rsqrt(var + 1e-06) * jax.nn.silu(z)
            out = out.reshape(b_, t_, d_)
            return jnp.einsum('btd,ed->bte', out, W_out)
        key = jax.random.key(seed)
        ks = jax.random.split(key, 8)
        s = 0.02
        return {'x': jax.random.normal(ks[0], (B, T, D), jnp.float32), 'W_qkv': jax.random.normal(ks[1], (CONV_DIM, D), jnp.float32) * s, 'conv_w': jax.random.normal(ks[2], (CONV_DIM, 1, K), jnp.float32) * 0.25, 'W_z': jax.random.normal(ks[3], (D, D), jnp.float32) * s, 'W_b': jax.random.normal(ks[4], (H, D), jnp.float32) * s, 'W_a': jax.random.normal(ks[5], (H, D), jnp.float32) * s, 'dt_bias': jnp.ones((H,), jnp.float32), 'A_log': jnp.log(jnp.arange(1, H + 1, dtype=jnp.float32)), 'W_out': jax.random.normal(ks[6], (D, D), jnp.float32) * s}
    _L1_attn_in = _L1_attn_setup()

    def _L1_ffn_setup():
        import jax, jax.numpy as jnp
        import numpy as np
        B, S, D = (2, 256, 128)
        I = 64
        E = 16
        TOP_K = 2

        def _mlp(x, wg, wu, wd):
            return jnp.einsum('bsi,id->bsd', jax.nn.silu(x @ wg) * (x @ wu), wd)
        key = jax.random.key(seed)
        ks = jax.random.split(key, 10)
        sc_d = 1.0 / np.sqrt(D)
        sc_i = 1.0 / np.sqrt(I)
        return {'x': jax.random.normal(ks[0], (B, S, D), dtype=jnp.float32), 'gate_w': jax.random.normal(ks[1], (D, E), dtype=jnp.float32) * sc_d, 'gate_b': jnp.zeros((E,), dtype=jnp.float32), 'shared_wg': jax.random.normal(ks[2], (D, I), dtype=jnp.float32) * sc_d, 'shared_wu': jax.random.normal(ks[3], (D, I), dtype=jnp.float32) * sc_d, 'shared_wd': jax.random.normal(ks[4], (I, D), dtype=jnp.float32) * sc_i, 'experts_wg': jax.random.normal(ks[5], (E, D, I), dtype=jnp.float32) * sc_d, 'experts_wu': jax.random.normal(ks[6], (E, D, I), dtype=jnp.float32) * sc_d, 'experts_wd': jax.random.normal(ks[7], (E, I, D), dtype=jnp.float32) * sc_i}
    _L1_ffn_in = _L1_ffn_setup()

    def _L2_attn_setup():
        import jax, jax.numpy as jnp
        import numpy as np
        N_HEAD = 16
        key = jax.random.key(seed)
        k1, k2, k3, k4 = jax.random.split(key, 4)
        B, T, C = (2, 256, 128)
        x = jax.random.normal(k1, (B, T, C), dtype=jnp.float32)
        W_attn = jax.random.normal(k2, (C, 2 * C), dtype=jnp.float32) * 0.02
        b_attn = jax.random.normal(k3, (2 * C,), dtype=jnp.float32) * 0.02
        head_weights = jax.random.normal(k4, (N_HEAD, C), dtype=jnp.float32) * (1.0 / np.sqrt(C))
        return {'x': x, 'W_attn': W_attn, 'b_attn': b_attn, 'head_weights': head_weights}
    _L2_attn_in = _L2_attn_setup()

    def _L2_ffn_setup():
        import jax, jax.numpy as jnp
        import numpy as np
        from math import sqrt
        B, S, D, H, E, K, FF = (2, 128, 128, 16, 8, 2, 512)
        HD = D // H
        EPS = 1e-05

        def _rope_cache(seq_len, hd):
            inv_freq = 1.0 / 10000.0 ** (jnp.arange(0, hd, 2, dtype=jnp.float32) / hd)
            t = jnp.arange(seq_len, dtype=jnp.float32)
            freqs = t[:, None] * inv_freq[None, :]
            emb = jnp.concatenate([freqs, freqs], axis=-1)
            return (jnp.cos(emb), jnp.sin(emb))

        def _rotate_half(x):
            x1, x2 = jnp.split(x, 2, axis=-1)
            return jnp.concatenate([-x2, x1], axis=-1)

        def _layernorm(x, g, b):
            m = jnp.mean(x, axis=-1, keepdims=True)
            v = jnp.var(x, axis=-1, keepdims=True)
            return (x - m) * jax.lax.rsqrt(v + EPS) * g + b

        def _forward(x, Wq, bq, Wk, bk, Wv, bv, Wo, bo, Wg, bg, W1, b1, W2, b2, g1, be1, g2, be2):
            bsz, seq, d = x.shape
            q = (x @ Wq + bq).reshape(bsz, seq, H, HD).transpose(0, 2, 1, 3)
            k = (x @ Wk + bk).reshape(bsz, seq, H, HD).transpose(0, 2, 1, 3)
            v = (x @ Wv + bv).reshape(bsz, seq, H, HD).transpose(0, 2, 1, 3)
            cos, sin = _rope_cache(seq, HD)
            cos = cos[None, None]
            sin = sin[None, None]
            q = q * cos + _rotate_half(q) * sin
            k = k * cos + _rotate_half(k) * sin
            scores = jnp.einsum('bhqd,bhkd->bhqk', q, k) / sqrt(HD)
            attn = jax.nn.softmax(scores, axis=-1)
            ao = jnp.einsum('bhqk,bhkd->bhqd', attn, v)
            ao = ao.transpose(0, 2, 1, 3).reshape(bsz, seq, d)
            attn_out = ao @ Wo + bo
            x1 = _layernorm(x + attn_out, g1, be1)
            gate_logits = x1 @ Wg + bg
            gate_probs = jax.nn.softmax(gate_logits, axis=-1)
            topk_p, topk_i = jax.lax.top_k(gate_probs, K)
            topk_p = topk_p / jnp.sum(topk_p, axis=-1, keepdims=True)
            comb = jnp.sum(jax.nn.one_hot(topk_i, E, dtype=x.dtype) * topk_p[..., None], axis=-2)
            h = jax.nn.gelu(jnp.einsum('bsd,edf->bsef', x1, W1) + b1, approximate=False)
            y = jnp.einsum('bsef,efd->bsed', h, W2) + b2
            moe_out = jnp.einsum('bse,bsed->bsd', comb, y)
            return _layernorm(x1 + moe_out, g2, be2)
        key = jax.random.key(seed)
        ks = jax.random.split(key, 20)
        std = 0.02
        p = lambda k, sh: jax.random.normal(k, sh, dtype=jnp.float32) * std
        return {'x': jax.random.normal(ks[0], (B, S, D), dtype=jnp.float32), 'Wq': p(ks[1], (D, D)), 'bq': jnp.zeros((D,), jnp.float32), 'Wk': p(ks[2], (D, D)), 'bk': jnp.zeros((D,), jnp.float32), 'Wv': p(ks[3], (D, D)), 'bv': jnp.zeros((D,), jnp.float32), 'Wo': p(ks[4], (D, D)), 'bo': jnp.zeros((D,), jnp.float32), 'Wg': p(ks[5], (D, E)), 'bg': jnp.zeros((E,), jnp.float32), 'W1': p(ks[6], (E, D, FF)), 'b1': jnp.zeros((E, FF), jnp.float32), 'W2': p(ks[7], (E, FF, D)), 'b2': jnp.zeros((E, D), jnp.float32), 'g1': jnp.ones((D,), jnp.float32), 'be1': jnp.zeros((D,), jnp.float32), 'g2': jnp.ones((D,), jnp.float32), 'be2': jnp.zeros((D,), jnp.float32)}
    _L2_ffn_in = _L2_ffn_setup()

    def _L3_attn_setup():
        import jax, jax.numpy as jnp
        import numpy as np
        H, HD, D = (16, 64, 128)
        SCALE = HD ** (-0.5)
        TEMP = 1.0
        EPS = 1e-05
        key = jax.random.key(seed)
        ks = jax.random.split(key, 10)
        B, N = (2, 256)
        lim = 1.0 / np.sqrt(D)

        def lin(k, out_d, in_d):
            k1, k2 = jax.random.split(k)
            W = jax.random.uniform(k1, (out_d, in_d), jnp.float32, -lim, lim)
            b = jax.random.uniform(k2, (out_d,), jnp.float32, -lim, lim)
            return (W, b)
        Wq, bq = lin(ks[0], H * HD, D)
        Wk, bk = lin(ks[1], H * HD, D)
        Wv, bv = lin(ks[2], H * HD, D)
        Wo, bo = lin(ks[3], D, H * HD)
        return {'x': jax.random.normal(ks[4], (B, N, D), jnp.float32), 'adaptive_scale': jnp.ones((H,), jnp.float32), 'Wq': Wq, 'bq': bq, 'Wk': Wk, 'bk': bk, 'Wv': Wv, 'bv': bv, 'Wo': Wo, 'bo': bo, 'gamma': jnp.ones((D,), jnp.float32), 'beta': jnp.zeros((D,), jnp.float32)}
    _L3_attn_in = _L3_attn_setup()

    def _L3_ffn_setup():
        import jax, jax.numpy as jnp
        import numpy as np
        ALPHA = 1.5
        TEMP = 1.0
        N_ITER = 25
        THRESH = 1e-09

        def entmax_bisect(X, alpha=ALPHA, n_iter=N_ITER):
            d = X.shape[-1]
            inv_am1 = 1.0 / (alpha - 1.0)
            Xs = X * (alpha - 1.0)
            max_val = jnp.max(Xs, axis=-1, keepdims=True)
            tau_lo = max_val - 1.0
            tau_hi = max_val - (1.0 / d) ** (alpha - 1.0)
            f_lo = jnp.sum(jnp.maximum(Xs - tau_lo, 0.0) ** inv_am1, axis=-1, keepdims=True) - 1.0

            def body(i, carry):
                tau_lo, dm, _ = carry
                dm = dm * 0.5
                tau_m = tau_lo + dm
                f_m = jnp.sum(jnp.maximum(Xs - tau_m, 0.0) ** inv_am1, axis=-1, keepdims=True) - 1.0
                tau_lo = jnp.where(f_m * f_lo >= 0.0, tau_m, tau_lo)
                return (tau_lo, dm, tau_m)
            dm0 = tau_hi - tau_lo
            _, _, tau_m = jax.lax.fori_loop(0, n_iter, body, (tau_lo, dm0, tau_lo))
            p = jnp.maximum(Xs - tau_m, 0.0) ** inv_am1
            return p / jnp.sum(p, axis=-1, keepdims=True)
        key = jax.random.key(seed)
        ks = jax.random.split(key, 8)
        B, S, D, E = (2, 128, 128, 8)
        F = 4 * D
        return {'x': jax.random.normal(ks[0], (B, S, D), jnp.float32), 'Wr': jax.random.normal(ks[1], (D, E), jnp.float32) * 0.02, 'br': jnp.zeros((E,), jnp.float32), 'W1': jax.random.normal(ks[2], (E, D, F), jnp.float32) * 0.02, 'b1': jnp.zeros((E, F), jnp.float32), 'W2': jax.random.normal(ks[3], (E, F, D), jnp.float32) * 0.02, 'b2': jnp.zeros((E, D), jnp.float32)}
    _L3_ffn_in = _L3_ffn_setup()
    _d = {'L0_attn_hidden_states': _L0_attn_in['hidden_states'], 'L0_attn_Wq': _L0_attn_in['Wq'], 'L0_attn_bq': _L0_attn_in['bq'], 'L0_attn_Wk': _L0_attn_in['Wk'], 'L0_attn_bk': _L0_attn_in['bk'], 'L0_attn_Wv': _L0_attn_in['Wv'], 'L0_attn_bv': _L0_attn_in['bv'], 'L0_attn_Wo': _L0_attn_in['Wo'], 'L0_attn_bo': _L0_attn_in['bo'], 'L0_attn_rel_bias': _L0_attn_in['rel_bias'], 'L0_ffn_weight': _L0_ffn_in['weight'], 'L0_ffn_alpha': _L0_ffn_in['alpha'], 'L0_ffn_bias': _L0_ffn_in['bias'], 'L1_attn_W_qkv': _L1_attn_in['W_qkv'], 'L1_attn_conv_w': _L1_attn_in['conv_w'], 'L1_attn_W_z': _L1_attn_in['W_z'], 'L1_attn_W_b': _L1_attn_in['W_b'], 'L1_attn_W_a': _L1_attn_in['W_a'], 'L1_attn_dt_bias': _L1_attn_in['dt_bias'], 'L1_attn_A_log': _L1_attn_in['A_log'], 'L1_attn_W_out': _L1_attn_in['W_out'], 'L1_ffn_gate_w': _L1_ffn_in['gate_w'], 'L1_ffn_gate_b': _L1_ffn_in['gate_b'], 'L1_ffn_shared_wg': _L1_ffn_in['shared_wg'], 'L1_ffn_shared_wu': _L1_ffn_in['shared_wu'], 'L1_ffn_shared_wd': _L1_ffn_in['shared_wd'], 'L1_ffn_experts_wg': _L1_ffn_in['experts_wg'], 'L1_ffn_experts_wu': _L1_ffn_in['experts_wu'], 'L1_ffn_experts_wd': _L1_ffn_in['experts_wd'], 'L2_attn_W_attn': _L2_attn_in['W_attn'], 'L2_attn_b_attn': _L2_attn_in['b_attn'], 'L2_attn_head_weights': _L2_attn_in['head_weights'], 'L2_ffn_Wq': _L2_ffn_in['Wq'], 'L2_ffn_bq': _L2_ffn_in['bq'], 'L2_ffn_Wk': _L2_ffn_in['Wk'], 'L2_ffn_bk': _L2_ffn_in['bk'], 'L2_ffn_Wv': _L2_ffn_in['Wv'], 'L2_ffn_bv': _L2_ffn_in['bv'], 'L2_ffn_Wo': _L2_ffn_in['Wo'], 'L2_ffn_bo': _L2_ffn_in['bo'], 'L2_ffn_Wg': _L2_ffn_in['Wg'], 'L2_ffn_bg': _L2_ffn_in['bg'], 'L2_ffn_W1': _L2_ffn_in['W1'], 'L2_ffn_b1': _L2_ffn_in['b1'], 'L2_ffn_W2': _L2_ffn_in['W2'], 'L2_ffn_b2': _L2_ffn_in['b2'], 'L2_ffn_g1': _L2_ffn_in['g1'], 'L2_ffn_be1': _L2_ffn_in['be1'], 'L2_ffn_g2': _L2_ffn_in['g2'], 'L2_ffn_be2': _L2_ffn_in['be2'], 'L3_attn_adaptive_scale': _L3_attn_in['adaptive_scale'], 'L3_attn_Wq': _L3_attn_in['Wq'], 'L3_attn_bq': _L3_attn_in['bq'], 'L3_attn_Wk': _L3_attn_in['Wk'], 'L3_attn_bk': _L3_attn_in['bk'], 'L3_attn_Wv': _L3_attn_in['Wv'], 'L3_attn_bv': _L3_attn_in['bv'], 'L3_attn_Wo': _L3_attn_in['Wo'], 'L3_attn_bo': _L3_attn_in['bo'], 'L3_attn_gamma': _L3_attn_in['gamma'], 'L3_attn_beta': _L3_attn_in['beta'], 'L3_ffn_Wr': _L3_ffn_in['Wr'], 'L3_ffn_br': _L3_ffn_in['br'], 'L3_ffn_W1': _L3_ffn_in['W1'], 'L3_ffn_b1': _L3_ffn_in['b1'], 'L3_ffn_W2': _L3_ffn_in['W2'], 'L3_ffn_b2': _L3_ffn_in['b2']}
    _x0 = _d['L0_attn_hidden_states']
    _d['L0_attn_hidden_states'] = jax.random.normal(jax.random.fold_in(jax.random.key(seed), 1), (4, 1024, 128), dtype=_x0.dtype)
    del _x0
    return _d

def reference(L0_attn_hidden_states, L0_attn_Wq, L0_attn_bq, L0_attn_Wk, L0_attn_bk, L0_attn_Wv, L0_attn_bv, L0_attn_Wo, L0_attn_bo, L0_attn_rel_bias, L0_ffn_weight, L0_ffn_alpha, L0_ffn_bias, L1_attn_W_qkv, L1_attn_conv_w, L1_attn_W_z, L1_attn_W_b, L1_attn_W_a, L1_attn_dt_bias, L1_attn_A_log, L1_attn_W_out, L1_ffn_gate_w, L1_ffn_gate_b, L1_ffn_shared_wg, L1_ffn_shared_wu, L1_ffn_shared_wd, L1_ffn_experts_wg, L1_ffn_experts_wu, L1_ffn_experts_wd, L2_attn_W_attn, L2_attn_b_attn, L2_attn_head_weights, L2_ffn_Wq, L2_ffn_bq, L2_ffn_Wk, L2_ffn_bk, L2_ffn_Wv, L2_ffn_bv, L2_ffn_Wo, L2_ffn_bo, L2_ffn_Wg, L2_ffn_bg, L2_ffn_W1, L2_ffn_b1, L2_ffn_W2, L2_ffn_b2, L2_ffn_g1, L2_ffn_be1, L2_ffn_g2, L2_ffn_be2, L3_attn_adaptive_scale, L3_attn_Wq, L3_attn_bq, L3_attn_Wk, L3_attn_bk, L3_attn_Wv, L3_attn_bv, L3_attn_Wo, L3_attn_bo, L3_attn_gamma, L3_attn_beta, L3_ffn_Wr, L3_ffn_br, L3_ffn_W1, L3_ffn_b1, L3_ffn_W2, L3_ffn_b2):

    def _L0_attn_ref(hidden_states, Wq, bq, Wk, bk, Wv, bv, Wo, bo, rel_bias):
        import jax, jax.numpy as jnp
        import numpy as np
        N_EMBD = 128
        N_HEADS = 16
        HEAD_DIM = N_EMBD // N_HEADS
        NUM_BUCKETS = 32
        MAX_DISTANCE = 64

        def _relative_position_bucket(relative_position):
            rp = jnp.maximum(-relative_position, 0)
            max_exact = NUM_BUCKETS // 2
            is_small = rp < max_exact
            rp_f = jnp.maximum(rp, 1).astype(jnp.float32)
            large = max_exact + (jnp.log(rp_f / max_exact) / np.log(MAX_DISTANCE / max_exact) * (NUM_BUCKETS - max_exact)).astype(jnp.int32)
            large = jnp.minimum(large, NUM_BUCKETS - 1)
            return jnp.where(is_small, rp, large)
        B, S, _ = hidden_states.shape

        def shape(x):
            return x.reshape(B, S, N_HEADS, HEAD_DIM).transpose(0, 2, 1, 3)
        scale = 1.0 / np.sqrt(HEAD_DIM)
        q = shape(hidden_states @ Wq + bq)
        k = shape(hidden_states @ Wk + bk)
        v = shape(hidden_states @ Wv + bv)
        scores = jnp.einsum('bhqd,bhkd->bhqk', q * scale, k)
        ctx = jnp.arange(S)[:, None]
        mem = jnp.arange(S)[None, :]
        bucket = _relative_position_bucket(mem - ctx)
        position_bias = rel_bias[bucket].transpose(2, 0, 1)[None]
        scores = scores + position_bias * 8.0
        attn = jax.nn.softmax(scores.astype(jnp.float32), axis=-1).astype(scores.dtype)
        ctx_out = jnp.einsum('bhqk,bhkd->bhqd', attn, v)
        ctx_out = ctx_out.transpose(0, 2, 1, 3).reshape(B, S, N_EMBD)
        return ctx_out @ Wo + bo

    def _L0_ffn_ref(input, weight, alpha, bias):
        import jax, jax.numpy as jnp
        import numpy as np
        THRESH_FACTOR = 0.7

        def ternary_quantize(w):
            delta = THRESH_FACTOR * jnp.mean(jnp.abs(w))
            return jnp.where(w > delta, 1.0, jnp.where(w < -delta, -1.0, 0.0)).astype(w.dtype)
        w_ternary = ternary_quantize(weight)
        w_eff = w_ternary * alpha
        out = jnp.einsum('bsd,od->bso', input, w_eff) + bias
        return out

    def _L1_attn_ref(x, W_qkv, conv_w, W_z, W_b, W_a, dt_bias, A_log, W_out):
        import jax, jax.numpy as jnp
        import numpy as np
        from jax import lax
        B, T, D, H, K = (2, 256, 128, 16, 4)
        HD = D // H
        CONV_DIM = 3 * D

        def _l2norm(x, eps=1e-06):
            return x * lax.rsqrt(jnp.sum(x * x, axis=-1, keepdims=True) + eps)

        def _forward(x, W_qkv, conv_w, W_z, W_b, W_a, dt_bias, A_log, W_out):
            b_, t_, d_ = x.shape
            mixed = jnp.einsum('btd,cd->btc', x, W_qkv)
            c = mixed.transpose(0, 2, 1)
            c = lax.conv_general_dilated(c, conv_w, window_strides=(1,), padding=[(K - 1, 0)], dimension_numbers=('NCH', 'OIH', 'NCH'), feature_group_count=CONV_DIM)
            mixed = jax.nn.silu(c).transpose(0, 2, 1)
            q, k, v = jnp.split(mixed, [d_, 2 * d_], axis=-1)
            q = q.reshape(b_, t_, H, HD)
            k = k.reshape(b_, t_, H, HD)
            v = v.reshape(b_, t_, H, HD)
            z = jnp.einsum('btd,ed->bte', x, W_z).reshape(b_, t_, H, HD)
            beta = jax.nn.sigmoid(jnp.einsum('btd,hd->bth', x, W_b))
            g = -jnp.exp(A_log) * jax.nn.softplus(jnp.einsum('btd,hd->bth', x, W_a) + dt_bias)
            q = _l2norm(q) * HD ** (-0.5)
            k = _l2norm(k)
            qs = q.transpose(1, 0, 2, 3)
            ks_ = k.transpose(1, 0, 2, 3)
            vs = v.transpose(1, 0, 2, 3)
            bs = beta.transpose(1, 0, 2)
            gs = g.transpose(1, 0, 2)

            def step(S, inp):
                q_t, k_t, v_t, b_t, g_t = inp
                S = S * jnp.exp(g_t)[..., None, None]
                S = S + jnp.einsum('bhd,bhv->bhdv', k_t, v_t * b_t[..., None])
                o_t = jnp.einsum('bhd,bhdv->bhv', q_t, S)
                return (S, o_t)
            S0 = jnp.zeros((b_, H, HD, HD), x.dtype)
            _, out = lax.scan(step, S0, (qs, ks_, vs, bs, gs))
            out = out.transpose(1, 0, 2, 3)
            var = jnp.mean(out * out, axis=-1, keepdims=True)
            out = out * lax.rsqrt(var + 1e-06) * jax.nn.silu(z)
            out = out.reshape(b_, t_, d_)
            return jnp.einsum('btd,ed->bte', out, W_out)
        return _forward(x, W_qkv, conv_w, W_z, W_b, W_a, dt_bias, A_log, W_out)

    def _L1_ffn_ref(x, gate_w, gate_b, shared_wg, shared_wu, shared_wd, experts_wg, experts_wu, experts_wd):
        import jax, jax.numpy as jnp
        import numpy as np
        B, S, D = (2, 256, 128)
        I = 64
        E = 16
        TOP_K = 2

        def _mlp(x, wg, wu, wd):
            return jnp.einsum('bsi,id->bsd', jax.nn.silu(x @ wg) * (x @ wu), wd)
        router_logits = jax.nn.sigmoid(x @ gate_w + gate_b)
        expert_values, expert_indices = jax.lax.top_k(router_logits, k=TOP_K)
        expert_values = expert_values / jnp.sum(expert_values, axis=-1, keepdims=True)
        hg = jnp.einsum('bsd,edi->bsei', x, experts_wg)
        hu = jnp.einsum('bsd,edi->bsei', x, experts_wu)
        all_outputs = jnp.einsum('bsei,eid->bsed', jax.nn.silu(hg) * hu, experts_wd)
        selected = jnp.take_along_axis(all_outputs, expert_indices[..., None], axis=2)
        expert_weighted = jnp.sum(expert_values[..., None] * selected, axis=2)
        return x + _mlp(x, shared_wg, shared_wu, shared_wd) + expert_weighted

    def _L2_attn_ref(x, W_attn, b_attn, head_weights):
        import jax, jax.numpy as jnp
        import numpy as np
        N_HEAD = 16
        B, T, C = x.shape
        H = head_weights.shape[0]
        hs = C // H
        qk = x @ W_attn + b_attn
        q, k = jnp.split(qk, 2, axis=-1)
        q = q.reshape(B, T, H, hs).transpose(0, 2, 1, 3)
        k = k.reshape(B, T, H, hs).transpose(0, 2, 1, 3)
        att = jnp.einsum('bhtd,bhsd->bhts', q, k) * (1.0 / np.sqrt(hs))
        causal = jnp.tril(jnp.ones((T, T), dtype=bool))
        att = jnp.where(causal[None, None], att, -jnp.inf)
        att = jax.nn.softmax(att, axis=-1)
        y = jnp.einsum('bhts,bsc,hc->btc', att, x, head_weights)
        return y

    def _L2_ffn_ref(x, Wq, bq, Wk, bk, Wv, bv, Wo, bo, Wg, bg, W1, b1, W2, b2, g1, be1, g2, be2):
        import jax, jax.numpy as jnp
        import numpy as np
        from math import sqrt
        B, S, D, H, E, K, FF = (2, 128, 128, 16, 8, 2, 512)
        HD = D // H
        EPS = 1e-05

        def _rope_cache(seq_len, hd):
            inv_freq = 1.0 / 10000.0 ** (jnp.arange(0, hd, 2, dtype=jnp.float32) / hd)
            t = jnp.arange(seq_len, dtype=jnp.float32)
            freqs = t[:, None] * inv_freq[None, :]
            emb = jnp.concatenate([freqs, freqs], axis=-1)
            return (jnp.cos(emb), jnp.sin(emb))

        def _rotate_half(x):
            x1, x2 = jnp.split(x, 2, axis=-1)
            return jnp.concatenate([-x2, x1], axis=-1)

        def _layernorm(x, g, b):
            m = jnp.mean(x, axis=-1, keepdims=True)
            v = jnp.var(x, axis=-1, keepdims=True)
            return (x - m) * jax.lax.rsqrt(v + EPS) * g + b

        def _forward(x, Wq, bq, Wk, bk, Wv, bv, Wo, bo, Wg, bg, W1, b1, W2, b2, g1, be1, g2, be2):
            bsz, seq, d = x.shape
            q = (x @ Wq + bq).reshape(bsz, seq, H, HD).transpose(0, 2, 1, 3)
            k = (x @ Wk + bk).reshape(bsz, seq, H, HD).transpose(0, 2, 1, 3)
            v = (x @ Wv + bv).reshape(bsz, seq, H, HD).transpose(0, 2, 1, 3)
            cos, sin = _rope_cache(seq, HD)
            cos = cos[None, None]
            sin = sin[None, None]
            q = q * cos + _rotate_half(q) * sin
            k = k * cos + _rotate_half(k) * sin
            scores = jnp.einsum('bhqd,bhkd->bhqk', q, k) / sqrt(HD)
            attn = jax.nn.softmax(scores, axis=-1)
            ao = jnp.einsum('bhqk,bhkd->bhqd', attn, v)
            ao = ao.transpose(0, 2, 1, 3).reshape(bsz, seq, d)
            attn_out = ao @ Wo + bo
            x1 = _layernorm(x + attn_out, g1, be1)
            gate_logits = x1 @ Wg + bg
            gate_probs = jax.nn.softmax(gate_logits, axis=-1)
            topk_p, topk_i = jax.lax.top_k(gate_probs, K)
            topk_p = topk_p / jnp.sum(topk_p, axis=-1, keepdims=True)
            comb = jnp.sum(jax.nn.one_hot(topk_i, E, dtype=x.dtype) * topk_p[..., None], axis=-2)
            h = jax.nn.gelu(jnp.einsum('bsd,edf->bsef', x1, W1) + b1, approximate=False)
            y = jnp.einsum('bsef,efd->bsed', h, W2) + b2
            moe_out = jnp.einsum('bse,bsed->bsd', comb, y)
            return _layernorm(x1 + moe_out, g2, be2)
        return _forward(x, Wq, bq, Wk, bk, Wv, bv, Wo, bo, Wg, bg, W1, b1, W2, b2, g1, be1, g2, be2)

    def _L3_attn_ref(x, adaptive_scale, Wq, bq, Wk, bk, Wv, bv, Wo, bo, gamma, beta):
        import jax, jax.numpy as jnp
        import numpy as np
        H, HD, D = (16, 64, 128)
        SCALE = HD ** (-0.5)
        TEMP = 1.0
        EPS = 1e-05
        B, N, _ = x.shape
        Q = (x @ Wq.T + bq).reshape(B, N, H, HD)
        K = (x @ Wk.T + bk).reshape(B, N, H, HD)
        V = (x @ Wv.T + bv).reshape(B, N, H, HD)
        scores = jnp.einsum('bnhd,bmhd->bhnm', Q, K)
        scores = scores * (SCALE * adaptive_scale)[None, :, None, None] / TEMP
        w = jax.nn.softmax(scores, axis=-1)
        attn = jnp.einsum('bhnm,bmhd->bnhd', w, V).reshape(B, N, H * HD)
        y = x + (attn @ Wo.T + bo)
        mu = jnp.mean(y, axis=-1, keepdims=True)
        var = jnp.var(y, axis=-1, keepdims=True)
        return (y - mu) / jnp.sqrt(var + EPS) * gamma + beta

    def _L3_ffn_ref(x, Wr, br, W1, b1, W2, b2):
        import jax, jax.numpy as jnp
        import numpy as np
        ALPHA = 1.5
        TEMP = 1.0
        N_ITER = 25
        THRESH = 1e-09

        def entmax_bisect(X, alpha=ALPHA, n_iter=N_ITER):
            d = X.shape[-1]
            inv_am1 = 1.0 / (alpha - 1.0)
            Xs = X * (alpha - 1.0)
            max_val = jnp.max(Xs, axis=-1, keepdims=True)
            tau_lo = max_val - 1.0
            tau_hi = max_val - (1.0 / d) ** (alpha - 1.0)
            f_lo = jnp.sum(jnp.maximum(Xs - tau_lo, 0.0) ** inv_am1, axis=-1, keepdims=True) - 1.0

            def body(i, carry):
                tau_lo, dm, _ = carry
                dm = dm * 0.5
                tau_m = tau_lo + dm
                f_m = jnp.sum(jnp.maximum(Xs - tau_m, 0.0) ** inv_am1, axis=-1, keepdims=True) - 1.0
                tau_lo = jnp.where(f_m * f_lo >= 0.0, tau_m, tau_lo)
                return (tau_lo, dm, tau_m)
            dm0 = tau_hi - tau_lo
            _, _, tau_m = jax.lax.fori_loop(0, n_iter, body, (tau_lo, dm0, tau_lo))
            p = jnp.maximum(Xs - tau_m, 0.0) ** inv_am1
            return p / jnp.sum(p, axis=-1, keepdims=True)
        B, S, D = x.shape
        xt = x.reshape(B * S, D)
        logits = (xt @ Wr + br) / TEMP
        gates = entmax_bisect(logits)
        gates = jnp.where(gates > THRESH, gates, 0.0)
        h = jax.nn.relu(jnp.einsum('td,edf->etf', xt, W1) + b1[:, None, :])
        y = jnp.einsum('etf,efd->etd', h, W2) + b2[:, None, :]
        out = jnp.einsum('etd,te->td', y, gates)
        return out.reshape(B, S, D)
    x = L0_attn_hidden_states
    x = _layernorm(x + _L0_attn_ref(x, L0_attn_Wq, L0_attn_bq, L0_attn_Wk, L0_attn_bk, L0_attn_Wv, L0_attn_bv, L0_attn_Wo, L0_attn_bo, L0_attn_rel_bias), axis=-1)
    x = _layernorm(x + _L0_ffn_ref(x, L0_ffn_weight, L0_ffn_alpha, L0_ffn_bias), axis=-1)
    x = _layernorm(x + _L1_attn_ref(x, L1_attn_W_qkv, L1_attn_conv_w, L1_attn_W_z, L1_attn_W_b, L1_attn_W_a, L1_attn_dt_bias, L1_attn_A_log, L1_attn_W_out), axis=-1)
    x = _layernorm(x + _L1_ffn_ref(x, L1_ffn_gate_w, L1_ffn_gate_b, L1_ffn_shared_wg, L1_ffn_shared_wu, L1_ffn_shared_wd, L1_ffn_experts_wg, L1_ffn_experts_wu, L1_ffn_experts_wd), axis=-1)
    x = _layernorm(x + _L2_attn_ref(x, L2_attn_W_attn, L2_attn_b_attn, L2_attn_head_weights), axis=-1)
    x = _layernorm(x + _L2_ffn_ref(x, L2_ffn_Wq, L2_ffn_bq, L2_ffn_Wk, L2_ffn_bk, L2_ffn_Wv, L2_ffn_bv, L2_ffn_Wo, L2_ffn_bo, L2_ffn_Wg, L2_ffn_bg, L2_ffn_W1, L2_ffn_b1, L2_ffn_W2, L2_ffn_b2, L2_ffn_g1, L2_ffn_be1, L2_ffn_g2, L2_ffn_be2), axis=-1)
    x = _layernorm(x + _L3_attn_ref(x, L3_attn_adaptive_scale, L3_attn_Wq, L3_attn_bq, L3_attn_Wk, L3_attn_bk, L3_attn_Wv, L3_attn_bv, L3_attn_Wo, L3_attn_bo, L3_attn_gamma, L3_attn_beta), axis=-1)
    x = _layernorm(x + _L3_ffn_ref(x, L3_ffn_Wr, L3_ffn_br, L3_ffn_W1, L3_ffn_b1, L3_ffn_W2, L3_ffn_b2), axis=-1)
    return x

_drawn_inputs = setup_inputs


def setup_inputs(seed=0):
    import zlib

    import numpy as np

    out = dict(_drawn_inputs(seed))
    spreads = {'L0_attn_bq': (0.0, 0.328),
     'L0_attn_bk': (0.0, 2.0),
     'L0_attn_bv': (0.0, 0.1),
     'L0_attn_bo': (0.0, 0.1),
     'L1_attn_dt_bias': (1.0, 0.6),
     'L1_ffn_gate_b': (0.0, 0.1),
     'L2_ffn_bq': (0.0, 0.8),
     'L2_ffn_bk': (0.0, 0.8),
     'L2_ffn_bv': (0.0, 0.552),
     'L2_ffn_bo': (0.0, 0.1),
     'L2_ffn_bg': (0.0, 0.297),
     'L2_ffn_b1': (0.0, 0.8),
     'L2_ffn_b2': (0.0, 0.1),
     'L2_ffn_g1': (1.0, 0.2),
     'L2_ffn_be1': (0.0, 0.1),
     'L2_ffn_g2': (1.0, 0.2),
     'L2_ffn_be2': (0.0, 0.1),
     'L3_attn_adaptive_scale': (1.0, 0.6),
     'L3_attn_gamma': (1.0, 0.2),
     'L3_attn_beta': (0.0, 0.1),
     'L3_ffn_br': (0.0, 0.756),
     'L3_ffn_b1': (0.0, 0.609),
     'L3_ffn_b2': (0.0, 0.1)}
    factors = {'L1_attn_W_b': 8.0,
     'L1_attn_W_a': 23.212,
     'L1_attn_A_log': 5.548,
     'L2_attn_W_attn': 8.0,
     'L2_attn_b_attn': 8.0,
     'L2_ffn_Wq': 8.0,
     'L2_ffn_Wk': 8.0,
     'L2_ffn_Wv': 8.0,
     'L2_ffn_Wo': 4.015,
     'L2_ffn_W1': 3.031,
     'L2_ffn_W2': 2.76,
     'L3_attn_Wq': 2.86,
     'L3_attn_bq': 8.0,
     'L3_attn_Wk': 2.889,
     'L3_attn_bk': 64.0}
    for name, (base, spread) in spreads.items():
        noise = np.random.default_rng([zlib.crc32(name.encode()), seed]).standard_normal(out[name].shape)
        drawn = base * np.exp(spread * noise) if base else spread * noise
        out[name] = jnp.asarray(drawn.astype(out[name].dtype))
    for name, factor in factors.items():
        out[name] = (out[name] * factor).astype(out[name].dtype)
    return out
```

```python
from contextlib import ExitStack

import numpy as np
import concourse.bass as bass
from concourse import mybir

P = 128
T = 1024
C = 128
H = 16
NT = T // P
BANK = 512
HALF = T // BANK
LN_EPS = 1e-5

F32 = mybir.dt.float32
BF16 = mybir.dt.bfloat16
ALU = mybir.AluOpType
ACT = mybir.ActivationFunctionType
AX = mybir.AxisListType

SPLITS = 3
HD = C // H
STACK_QK = SPLITS * SPLITS * HD
STACK_FAR = SPLITS * NT
ROW_MAX = STACK_QK + STACK_FAR
STACK = ROW_MAX + 2
GROUP = 4
NEAR = 2 * P


class Count:

    def __init__(self, handle):
        self.handle, self.value, self.start = handle, 0, 0

    def at(self, n):
        return (self, self.start + n) if n > 0 else None


class Lane:

    def __init__(self):
        self.items, self.passed = [], {}

    def wait(self, *marks):
        for mark in marks:
            if mark is not None and self.passed.get(mark[0], 0) < mark[1]:
                self.passed[mark[0]] = mark[1]
                self.items.append((mark[0].handle, mark[1]))

    def __call__(self, method, *args, sig=None, step=1, **kw):
        self.items.append((method, args, kw, sig and sig.handle, step))
        if sig is None:
            return None
        sig.value += step
        return sig, sig.value

    def issue(self, engine):
        for item in self.items:
            if len(item) == 2:
                engine.wait_ge(*item)
                continue
            method, args, kw, sig, step = item
            instruction = method(*args, **kw)
            if sig is not None:
                instruction.then_inc(sig, step)


class Ring:

    def __init__(self, buffers):
        self.buffers, self.done, self.at = buffers, [[] for _ in buffers], -1

    def take(self):
        self.at = (self.at + 1) % len(self.buffers)
        return self.at, self.buffers[self.at], self.done[self.at]


class Core:
    pass


class Stage:

    def __init__(self, core, name):
        self.core, self.name, self.nc, self.ctx = core, name, core.nc, ExitStack()
        self.pe, self.act, self.dve, self.pool, self.sp = (Lane() for _ in range(5))
        self.counts = []

    def sbuf(self, name, shape, dtype=F32):
        return self.ctx.enter_context(self.nc.sbuf_tensor(f"{self.name}_{name}", shape, dtype))

    def psum(self, name, n):
        return self.ctx.enter_context(self.nc.psum_tensor(f"{self.name}_{name}", [P, n, BANK], F32))

    def sem(self, name):
        count = self.core.counts.pop() if self.core.counts else self.core.new_count()
        count.start = count.value
        self.counts.append(count)
        return count

    def load(self, out, in_, count):
        return self.sp(self.nc.sync.dma_start, out, in_, sig=count, step=16)

    def run(self):
        nc = self.nc
        with nc.Block() as block:
            @block.tensor
            def _(e):
                self.pe.issue(e)

            @block.scalar
            def _(e):
                self.act.issue(e)

            @block.vector
            def _(e):
                self.dve.issue(e)

            @block.gpsimd
            def _(e):
                self.pool.issue(e)

            @block.sync
            def _(e):
                self.sp.issue(e)
        self.core.counts += reversed(self.counts)
        self.ctx.close()


def banks4(bank):
    return bank.rearrange("p (n c) -> p n c", c=C)


def spread(ap, n):
    return ap[:, None, :].broadcast_to([ap.shape[0], n, ap.shape[1]])


def along(ap, n):
    return ap[:, :, None].broadcast_to([ap.shape[0], ap.shape[1], n])


class Norm:

    def __init__(self, st, tag=""):
        self.st = st
        self.stats = st.sbuf(f"stats{tag}", [P, NT, 6])
        self.mv = st.sbuf(f"mv{tag}", [P, NT, 2])
        self.std = st.sbuf(f"std{tag}", [P, NT])
        self.rstd = st.sbuf(f"rstd{tag}", [P, NT])
        self.n_stats = st.sem(f"n_stats{tag}")
        self.n_mv = st.sem(f"n_mv{tag}")
        self.n_std = st.sem(f"n_std{tag}")
        self.n_rstd = st.sem(f"n_rstd{tag}")
        self.n_out = st.sem(f"n_out{tag}")
        self.last = None

    def __call__(self, src, dst, after):
        st, nc, n = self.st, self.st.nc, src.shape[1]
        for i in range(n):
            st.dve.wait(*after, self.last)
            seen = st.dve(nc.vector.bn_stats, self.stats[:, i, :], src[:, i, :], sig=self.n_stats)
        for i in range(n):
            st.dve.wait((seen[0], seen[1] - n + 1 + i))
            mv = st.dve(nc.vector.bn_aggr, self.mv[:, i, :], self.stats[:, i, :], sig=self.n_mv)
        st.act.wait(mv, st.core.eps_ready)
        std = st.act(nc.scalar.activation, self.std[:, 0:n], self.mv[:, 0:n, 1], ACT.Sqrt,
                     bias=st.core.eps[:, 0:1], sig=self.n_std)
        st.dve.wait(std)
        rstd = st.dve(nc.vector.reciprocal, self.rstd[:, 0:n], self.std[:, 0:n],
                      sig=self.n_rstd)
        for i in range(n):
            st.dve.wait(rstd)
            out = st.dve(nc.vector.tensor_scalar, dst[:, i, :], src[:, i, :], self.mv[:, i, 0:1],
                         self.rstd[:, i:i + 1], ALU.subtract, ALU.mult,
                         sig=self.n_out)
        self.last = out
        return out


class Turn:

    def __init__(self, st, banks, tag=""):
        self.st, self.banks = st, banks
        self.turned = st.sem(f"turned{tag}")
        self.kept = st.sem(f"kept{tag}")

    def __call__(self, src, dst, after, copy_on="act"):
        st, nc = self.st, self.st.nc
        slot, bank, free = self.banks.take()
        for i in range(4):
            st.pe.wait(*after, *free, st.core.ident_ready)
            t = st.pe(nc.tensor.transpose, banks4(bank)[:, i, :], src[:, i, :], st.core.ident[:, :], sig=self.turned if i == 3 else None)
        if copy_on == "act":
            st.act.wait(t)
            kept = st.act(nc.scalar.copy, dst, bank, sig=self.kept)
        else:
            st.dve.wait(t)
            kept = st.dve(nc.vector.tensor_copy, dst, bank, sig=self.kept)
        self.banks.done[slot] = [kept]
        return kept


class Parts:

    def __init__(self, st, tag):
        self.st = st
        self.rest = st.sbuf(f"rest_{tag}", [P, T])
        self.parts = st.sbuf(f"parts_{tag}", [P, SPLITS, T], BF16)
        self.cast = st.sem(f"cast_{tag}")
        self.less = st.sem(f"less_{tag}")
        self.stored = st.sem(f"stored_{tag}")
        self.last = self.last_less = None

    def __call__(self, value, dram, after):
        st, nc = self.st, self.st.nc
        src, ready = value, after
        for s in range(SPLITS):
            st.act.wait(*ready, self.last)
            cast = st.act(nc.scalar.copy, self.parts[:, s, :], src,
                          sig=self.cast)
            if s < SPLITS - 1:
                st.dve.wait(cast)
                less = st.dve(nc.vector.tensor_tensor, self.rest[:, :], src, self.parts[:, s, :],
                              ALU.subtract, sig=self.less)
                src, ready = self.rest[:, :], [less]
                if s == 0:
                    self.last_less = less
        st.sp.wait(cast)
        self.last = st.load(dram.rearrange("s c t -> c s t"), self.parts[:, :, :], self.stored)
        return self.last


class SmallHeads:

    SLOTS = 3

    def __init__(self, st, per_unit, q_dram, k_dram, far_dram, near=None, strip=None, causal=False):
        self.st, self.q_dram, self.k_dram, self.far_dram = st, q_dram, k_dram, far_dram
        self.near, self.strip, self.causal = near, strip, causal
        self.scored, self.per_unit = st.sem("scored"), per_unit
        n = self.SLOTS
        self.q_stack = [st.sbuf(f"q_stack{i}", [STACK, GROUP, T], BF16) for i in range(n)]
        self.k_stack = [st.sbuf(f"k_stack{i}", [STACK, GROUP, T], BF16) for i in range(n)]
        self.loaded = [st.sem(f"stack_loaded{i}") for i in range(n)]
        self.max_row = [st.sem(f"max_row{i}") for i in range(n)]
        self.ready = [None] * n
        self.row_ready = [None] * n
        self.max_parts = st.sbuf("max_parts", [P, GROUP, NT, HALF])
        self.neg_max = st.sbuf("neg_max", [P, GROUP * NT])
        self.max_hi = st.sbuf("max_hi", [GROUP * NT, P], BF16)
        self.max_lo = st.sbuf("max_lo", [GROUP * NT, P], BF16)
        self.fixed = st.sem("fixed_rows")
        self.max_scored = st.sem("max_scored")
        self.maxed = st.sem("maxed")
        self.joined = st.sem("max_joined")
        self.turned = st.sem("max_turned")
        self.hi_kept = st.sem("max_hi_kept")
        self.lo_kept = st.sem("max_lo_kept")
        self.last_joined = self.last_turned = self.hi = self.lo = self.sent = None
        for i in range(n):
            self.fixed_ready = st.load(self.k_stack[i][STACK_QK:STACK, :, :],
                                       st.core.const["key_rows"][:, :, :], self.fixed)
        self.last_joined = st.dve(st.nc.vector.memset, self.max_parts[:, :, :, :], -3e38,
                                  sig=self.joined)

    def fill(self, u, b, g, stored):
        st, i = self.st, u % self.SLOTS
        hs = slice(g * GROUP * HD, (g + 1) * GROUP * HD)
        st.sp.wait(self.scored.at(self.per_unit * (u - self.SLOTS + 1)), *stored)
        for s in range(SPLITS):
            q = self.q_dram[b, s, hs, :].rearrange("(h d) t -> d h t", d=HD)
            for r in range(SPLITS):
                row = (s * SPLITS + r) * HD
                k = self.k_dram[b, r, hs, :].rearrange("(h d) t -> d h t", d=HD)
                st.load(self.q_stack[i][row:row + HD, :, :], q, self.loaded[i])
                st.load(self.k_stack[i][row:row + HD, :, :], k, self.loaded[i])
        far = self.far_dram[:, g * GROUP:(g + 1) * GROUP, :]
        self.ready[i] = st.load(self.q_stack[i][STACK_QK:ROW_MAX, :, :], far, self.loaded[i])

    def maxima(self, u, ring):
        st, nc, i = self.st, self.st.nc, u % self.SLOTS
        q, k = self.q_stack[i], self.k_stack[i]

        def tile(j, n, half):
            width = min(BANK, (n + 1) * P - half * BANK) if self.causal else BANK
            slot, bank, free = ring.take()
            st.pe.wait(*free, self.ready[i], self.fixed_ready)
            scored = st.pe(nc.tensor.matmul, bank[:, 0:width], q[0:ROW_MAX, j, n * P:(n + 1) * P],
                           k[0:ROW_MAX, j, half * BANK:half * BANK + width], start=True, stop=True,
                           sig=self.max_scored)
            out = self.max_parts[:, j, n, half:half + 1]
            wait = [scored, self.last_joined]
            bias = None
            if self.strip is not None and n - 1 <= half * (BANK // P) + BANK // P - 1 \
                    and n >= half * (BANK // P):
                bias, more = self.strip(u, j, n, half)
                wait += more
            elif self.causal and half == n // (BANK // P):
                bias = st.core.causal_strip[:, BANK - width:BANK]
                wait.append(st.core.const_ready)
            if bias is None:
                st.dve.wait(*wait)
                maxed = st.dve(nc.vector.tensor_reduce, out, bank[:, 0:width], AX.X, ALU.max, sig=self.maxed)
            else:
                st.dve.wait(*wait)
                maxed = st.dve(nc.vector.tensor_tensor_reduce, bank[:, 0:width], bank[:, 0:width],
                               bias, 1.0, -3e38, ALU.add, ALU.max, out,
                               sig=self.maxed)
            ring.done[slot] = [maxed]
            self.last_maxed = maxed

        def join():
            st.dve.wait(self.last_maxed, self.last_turned)
            joined = st.dve(nc.vector.tensor_reduce, self.neg_max[:, :],
                            self.max_parts[:, :, :, :].rearrange("p j n h -> p (j n) h"), AX.X,
                            ALU.max, negate=True,
                            sig=self.joined)
            self.last_joined = joined
            slot, bank, free = ring.take()
            st.pe.wait(*free, joined)
            turned = st.pe(nc.tensor.transpose, bank[0:GROUP * NT, 0:P], self.neg_max[:, :],
                           st.core.ident[:, :], sig=self.turned)
            self.last_turned = turned
            st.dve.wait(turned, self.sent)
            hi = st.dve(nc.vector.tensor_copy, self.max_hi[:, :], bank[0:GROUP * NT, 0:P], sig=self.hi_kept)
            st.dve.wait(hi)
            lo = st.dve(nc.vector.tensor_tensor, self.max_lo[:, :], bank[0:GROUP * NT, 0:P],
                        self.max_hi[:, :], ALU.subtract, sig=self.lo_kept)
            ring.done[slot] = [lo]
            for row, part in ((ROW_MAX, self.max_hi), (ROW_MAX + 1, self.max_lo)):
                st.sp.wait(lo)
                self.sent = st.load(
                    q[row:row + 1, :, :].rearrange("o j (n t) -> o (j n) t", t=P),
                    part[:, :], self.max_row[i])
            self.row_ready[i] = self.sent

        steps = []
        for j in range(GROUP):
            for n in range(NT):
                for half in range(HALF):
                    if not self.causal or half * BANK < (n + 1) * P:
                        steps.append((tile, (j, n, half)))
        f, a = steps[-1]
        steps[-1] = (lambda *args: (tile(*args), join()), a)
        return steps


def interleave(units, maxima, exps, lag):
    m_steps = [step for u in units for step in maxima(u)]
    per_m = len(m_steps) // len(units)
    e_steps = [(u, step) for u in units for step in exps(u)]
    per_e = len(e_steps) // len(units)
    at = 0
    for m, (f, args) in enumerate(m_steps):
        f(*args)
        while at < len(e_steps) and (at + per_e + lag) * per_m <= (m + 1) * per_e:
            f, args = e_steps[at][1]
            f(*args)
            at += 1
    for _, (f, args) in e_steps[at:]:
        f(*args)


def project_small(st, ring, w, bias, scale, out, x_chn, done, w_ready, extra=()):
    nc = st.nc
    slot, banks, free = ring.take()
    for half in range(HALF):
        st.pe.wait(*free, *w_ready)
        mm = st.pe(nc.tensor.matmul, banks[:, half, :], w, x_chn[:, half * BANK:(half + 1) * BANK],
                   start=True, stop=True,
                   sig=st.projected if half == HALF - 1 else None)
    st.dve.wait(mm, *extra)
    kept = st.dve(nc.vector.tensor_scalar, out.rearrange("p (a b) -> p a b", a=HALF), banks, bias,
                  scale, ALU.add, ALU.mult, sig=done)
    ring.done[slot] = [kept]
    return kept


def values_small(st, ring, w, bias, out, x_chn, done, w_ready, extra=()):
    nc = st.nc
    slot, banks, free = ring.take()
    for n in range(NT):
        st.pe.wait(*free, *w_ready)
        mm = st.pe(nc.tensor.matmul, banks[:, n // 4, (n % 4) * C:(n % 4 + 1) * C],
                   x_chn[:, n * P:(n + 1) * P], w, start=True, stop=True,
                   sig=st.projected if n == NT - 1 else None)
    st.dve.wait(mm, *extra)
    kept = st.dve(nc.vector.tensor_tensor, out, banks.rearrange("p a (n c) -> p (a n) c", c=C),
                  spread(bias, NT), ALU.add, sig=done)
    ring.done[slot] = [kept]
    return kept


class Weighted:

    W = 32

    def __init__(self, st, heads, score_ring, out_ring, small_ring, exps, v_tok, ctx):
        self.st, self.heads, self.v_tok, self.ctx = st, heads, v_tok, ctx
        self.score_ring, self.out_ring, self.small_ring = score_ring, out_ring, small_ring
        self.exps, self.n_tile, self.n_half = exps, 0, 0
        self.v_one = [st.sbuf(f"v_one{i}", [P, NT, GROUP, self.W]) for i in range(2)]
        self.out_chn = [st.sbuf(f"out_chn{i}", [P, BANK]) for i in range(2)]
        self.r_sum = st.sbuf("r_sum", [P, 4 * GROUP])
        self.v_filled = st.sem("v_filled")
        self.scored = heads.scored
        self.exped = st.sem("exped")
        self.weighted = st.sem("weighted")
        self.kept = st.sem("out_kept")
        self.turned = st.sem("out_turned")
        self.inverted = st.sem("sum_inverted")
        self.context = st.sem("context")
        self.per_unit = HALF * NT * 2
        nc = st.nc
        for i in range(2):
            z = st.pool(nc.gpsimd.memset, self.v_one[i][:, :, :, :], 0.0, sig=self.v_filled)
            st.pool.wait(z)
            z = st.pool(nc.gpsimd.memset, self.v_one[i][:, :, :, HD:HD + 1], 1.0,
                        sig=self.v_filled)
        self.zeroed = z

    def steps(self, u, v_at, c_at, g, v_ready):
        st, nc, heads = self.st, self.st.nc, self.heads
        i, vs = u % heads.SLOTS, u % 2
        q, k, v = heads.q_stack[i], heads.k_stack[i], self.v_one[vs]
        pending = []

        def fill_values():
            st.pool.wait(self.zeroed, self.weighted.at(self.per_unit * (u - 1)), v_ready())
            self.filled = st.pool(
                nc.gpsimd.tensor_copy, v[:, :, :, 0:HD],
                self.v_tok()[:, v_at:v_at + NT, g * GROUP * HD:(g + 1) * GROUP * HD]
                .rearrange("p n (j d) -> p n j d", d=HD), sig=self.v_filled)

        def scores(half, kb, pair):
            if half == 0 and kb == 0 and pair == 0:
                fill_values()
            n = self.n_tile
            self.n_tile += 1
            banks = self.score_ring.buffers[n % 2]
            lo = max(kb * P, half * BANK)
            hi = min(kb * P + NEAR, (half + 1) * BANK)
            near = heads.near is not None and lo < hi
            st.pe.wait(heads.row_ready[i], heads.ready[i])
            st.pe.wait(self.exped.at(n - 1), *(self.score_ring.done[n % 2] if n < 2 else ()))
            for a in range(2):
                j = 2 * pair + a
                st.pe(nc.tensor.matmul, banks[:, a, :], k[0:STACK, j, kb * P:(kb + 1) * P],
                      q[0:STACK, j, half * BANK:(half + 1) * BANK], start=True, stop=not near,
                      sig=None if near or a == 0 else self.scored)
                if near:
                    bias, loaded = heads.near(u, j, lo - kb * P, hi - kb * P)
                    st.pe.wait(loaded)
                    for s in range(SPLITS):
                        last = s == SPLITS - 1
                        st.pe(nc.tensor.matmul, banks[:, a, lo - half * BANK:hi - half * BANK],
                              st.core.flip_bf[:, :], bias[s], start=False, stop=last,
                              sig=self.scored if last and a == 1 else None)
            st.act.wait(self.scored.at(n + 1), self.weighted.at(n + 1 - len(self.exps)))
            st.act(nc.scalar.activation, self.exps[n % len(self.exps)], banks, ACT.Exp,
                   sig=self.exped)
            pending.append((kb, pair, n))
            if pair == 1 and kb > 0:
                weigh()
            if pair == 1 and kb == NT - 1:
                weigh()
                finish(half)

        def weigh():
            m = self.n_half
            out = self.out_ring.buffers[m % len(self.out_ring.buffers)]
            st.pe.wait(self.kept.at(m + 1 - len(self.out_ring.buffers)), self.filled)
            for _ in range(2):
                kb, pair, n = pending.pop(0)
                st.pe.wait(self.exped.at(n + 1))
                for a in range(2):
                    j = 2 * pair + a
                    st.pe(nc.tensor.matmul, out[self.W * j:self.W * (j + 1), :],
                          v[:, kb, j, :], self.exps[n % len(self.exps)][:, a, :], start=kb == 0,
                          stop=kb == NT - 1, sig=self.weighted if a == 1 else None)

        def finish(half):
            m = self.n_half
            self.n_half += 1
            out, chn = self.out_ring.buffers[m % len(self.out_ring.buffers)], self.out_chn[m % 2]
            st.dve.wait(self.weighted.at(NT * 2 * (m + 1)), self.turned.at(m - 1))
            st.dve(nc.vector.tensor_copy, chn[:, :], out, sig=self.kept)
            tslot, bank, emptied = self.small_ring.take()
            st.pe.wait(*emptied)
            st.pe.wait(self.kept.at(m + 1))
            for n in range(4):
                st.pe(nc.tensor.transpose, banks4(bank)[:, n, :], chn[:, n * P:(n + 1) * P],
                      st.core.ident[:, :], sig=self.turned if n == 3 else None)
            rows = bank.rearrange("p (m w) -> p m w", w=self.W)
            st.dve.wait(self.turned.at(m + 1), self.context.at(4 * m))
            st.dve(nc.vector.reciprocal, self.r_sum[:, :], rows[:, :, HD], sig=self.inverted)
            at = c_at + half * (BANK // P)
            dst = self.ctx()[:, at:at + 4, g * GROUP * HD:(g + 1) * GROUP * HD]
            st.dve.wait(self.inverted.at(m + 1))
            for n in range(4):
                st.dve(nc.vector.tensor_tensor, dst[:, n, :].rearrange("p (j d) -> p j d", d=HD),
                       rows[:, n * GROUP:(n + 1) * GROUP, 0:HD],
                       along(self.r_sum[:, n * GROUP:(n + 1) * GROUP], HD), ALU.mult,
                       sig=self.context)
            self.small_ring.done[tslot] = [self.context.at(4 * (m + 1))]

        return [(scores, (half, kb, pair)) for half in range(HALF) for kb in range(NT)
                for pair in range(2)]


class Rows:

    def __init__(self, st, ring, tag=""):
        self.st, self.ring = st, ring
        self.multiplied = st.sem(f"rows_multiplied{tag}")
        self.added = st.sem(f"rows_added{tag}")

    def __call__(self, chn, w, bias, residual, out, after, n_k=1):
        st, nc = self.st, self.st.nc
        slot, bank, free = self.ring.take()
        tiles = banks4(bank)
        for n in range(4):
            for k in range(n_k):
                st.pe.wait(*free, *after)
                mm = st.pe(nc.tensor.matmul, tiles[:, n, :], chn(k, n), w(k), start=k == 0,
                           stop=k == n_k - 1,
                           sig=self.multiplied if n == 3 and k == n_k - 1 else None)
        st.dve.wait(mm, *after)
        added = st.dve(nc.vector.tensor_tensor, out, tiles, residual, ALU.add,
                       sig=self.added)
        self.ring.done[slot] = [added]
        if bias is not None:
            st.dve.wait(added)
            added = st.dve(nc.vector.tensor_tensor, out, out, spread(bias, 4), ALU.add, sig=self.added)
        return added


N_BUCKETS = 32
MAX_DISTANCE = 64
BIAS_SCALE = 8.0
ROW = 3 * P


def position_bias(core):
    st = Stage(core, "bias")
    nc, const = core.nc, core.const
    ring = st.psum("p", 2)
    table = st.sbuf("table", [N_BUCKETS, H])
    hot = st.sbuf("hot", [N_BUCKETS, 2, ROW])
    level = st.sbuf("level", [STACK_FAR, 2])
    place = st.sbuf("place", [STACK_FAR, 2, NT])
    ends = st.sbuf("ends", [STACK_FAR, 2, H])
    part = st.sbuf("part", [STACK_FAR, 2, H], BF16)
    by_block = st.sbuf("by_block", [STACK_FAR, 2, H, NT])
    far_small = st.sbuf("far_small", [STACK_FAR, H, NT])
    far = st.sbuf("far", [STACK_FAR, H, T], BF16)
    near = st.sbuf("near", [H, 2, ROW])
    near_part = st.sbuf("near_part", [H, SPLITS, ROW], BF16)
    loaded, done, chain = st.sem("loaded"), st.sem("multiplied"), st.sem("chain")
    a_chain, stored = st.sem("a_chain"), core.bias_stored
    st.load(table[:, :], core.inp["L0_attn_rel_bias"][:, :], loaded)
    st.load(hot[:, :, :], const["bucket_hot"][:, :, :], loaded)
    st.load(level[:, :], const["far_level"][:, :], loaded)
    st.load(place[:, :, :], const["far_place"][:, :, :], loaded)
    rel = core.inp["L0_attn_rel_bias"]
    for e, row in enumerate((0, N_BUCKETS - 1)):
        t = st.load(ends[:, e, :], rel[row:row + 1, :].broadcast_to([STACK_FAR, H]), loaded)
    for e in range(2):
        st.pe.wait(t)
        mm = st.pe(nc.tensor.matmul, ring[0:H, e, 0:ROW], table[:, :], hot[:, e, :], start=True,
                   stop=True, sig=done)
    st.dve.wait(mm)
    v = st.dve(nc.vector.tensor_scalar, near[:, :, :], ring[0:H, :, 0:ROW], BIAS_SCALE, None,
               ALU.mult, sig=chain)
    st.sp.wait(v)
    st.load(core.near_rev[:, :], near[:, 1, :], stored)
    for s in range(SPLITS):
        st.dve.wait(v)
        v = st.dve(nc.vector.tensor_copy, near_part[:, s, :], near[:, 0, :], sig=chain)
        if s < SPLITS - 1:
            st.dve.wait(v)
            v = st.dve(nc.vector.tensor_tensor, near[:, 0, :], near[:, 0, :], near_part[:, s, :],
                       ALU.subtract, sig=chain)
    st.sp.wait(v)
    st.load(core.near_parts.rearrange("s h x -> h s x"), near_part[:, :, :], stored)
    st.dve.wait(t, v)
    v = st.dve(nc.vector.tensor_scalar, ends[:, :, :], ends[:, :, :], BIAS_SCALE, None, ALU.mult, sig=chain)
    for s in range(SPLITS - 1):
        st.dve.wait(v)
        v = st.dve(nc.vector.tensor_scalar, part[:, :, :], ends[:, :, :], level[:, s:s + 1], None,
                   ALU.mult, sig=chain)
        st.dve.wait(v)
        v = st.dve(nc.vector.tensor_tensor, ends[:, :, :], ends[:, :, :], part[:, :, :],
                   ALU.subtract, sig=chain)
    for e in range(2):
        st.dve.wait(v)
        v = st.dve(nc.vector.tensor_tensor, by_block[:, e, :, :], along(ends[:, e, :], NT),
                   spread(place[:, e, :], H), ALU.mult, sig=chain)
    st.dve.wait(v)
    v = st.dve(nc.vector.tensor_tensor, far_small[:, :, :], by_block[:, 0, :, :],
               by_block[:, 1, :, :], ALU.add, sig=chain)
    for n in range(2):
        hs = slice(n * H // 2, (n + 1) * H // 2)
        dst = far[:, hs, :].rearrange("p h (n t) -> p (h n) t", t=P)
        src = along(far_small[:, hs, :].rearrange("p h n -> p (h n)"), P)
        if n:
            st.dve.wait(v)
            f = st.dve(nc.vector.tensor_copy, dst, src, sig=chain)
        else:
            st.act.wait(v)
            f = st.act(nc.scalar.copy, dst, src, sig=a_chain)
        st.sp.wait(f)
        t = st.load(core.far_bias[:, hs, :], far[:, hs, :], stored)
    core.bias_ready = t
    st.sp.wait(t)
    st.run()


def broadcast_rows(st, name, src, n, count, lane=None):
    out = st.sbuf(name, [P, n])
    t = st.load(out[:, :], src.rearrange("(o n) -> o n", o=1).broadcast_to([P, n]), count)
    return out, t


def column(st, name, src, count):
    out = st.sbuf(name, [P, 1])
    t = st.load(out[:, :], src.rearrange("(p o) -> p o", o=1), count)
    return out, t


def near_window(handle, row):
    ap = handle[row]
    return bass.AP(tensor=ap.tensor, offset=ap.offset, ap=[[1, P], [ROW, GROUP], [1, NEAR]])


def layer0(core):
    st = Stage(core, "l0")
    nc, inp, const = core.nc, core.inp, core.const
    nb = core.n_batch
    score_banks, small_banks, out_banks = st.psum("score", 4), st.psum("small", 2), st.psum("out", 2)
    score_ring = Ring([score_banks[:, 0:2, :], score_banks[:, 2:4, :]])
    small_ring = Ring([small_banks[:, 0, :], small_banks[:, 1, :]])
    out_ring = Ring([out_banks[:, 0, :], out_banks[:, 1, :]])
    st.projected = st.sem("projected")
    w_loaded = st.sem("w_loaded")
    w = {}
    for n in "qkvo":
        w[n] = st.sbuf(f"w{n}", [P, C])
        st.load(w[n][:, :], inp[f"L0_attn_W{n}"][:, :], w_loaded)
    bq, _ = column(st, "bq", inp["L0_attn_bq"], w_loaded)
    bk, _ = column(st, "bk", inp["L0_attn_bk"], w_loaded)
    bv, _ = broadcast_rows(st, "bv", inp["L0_attn_bv"], C, w_loaded)
    bo, w_ready = broadcast_rows(st, "bo", inp["L0_attn_bo"], C, w_loaded)
    x, xc = core.x_tok, core.x_chn
    x_loaded = [st.sem(f"x_loaded{b}") for b in range(nb)]
    turn = Turn(st, small_ring)
    x_ready = []
    for b in range(nb):
        t = st.load(x[:, b * NT:(b + 1) * NT, :],
                    inp["L0_attn_hidden_states"][b].rearrange("(n p) c -> p n c", p=P), x_loaded[b])
        for n in range(b * NT, (b + 1) * NT, 4):
            t2 = turn(x[:, n:n + 4, :], xc[:, n * P:n * P + BANK], [t])
        x_ready.append(t2)
    heads = SmallHeads(st, HALF * NT * 2, core.q_parts, core.k_parts, core.far_bias,
                       near=lambda u, j, lo, hi: near_of(u, j, lo, hi),
                       strip=lambda u, j, n, half: strip_of(u, j, n, half))
    v_tok, ctx_tok = core.big[:, 0:nb * T], core.big[:, nb * T:2 * nb * T]
    v_tok = v_tok.rearrange("p (n c) -> p n c", c=C)
    ctx_tok = ctx_tok.rearrange("p (n c) -> p n c", c=C)
    q_done, k_done, v_done = st.sem("q_done"), st.sem("k_done"), st.sem("v_done")
    split_q, split_k = Parts(st, "q"), Parts(st, "k")
    value = {n: st.sbuf(f"value_{n}", [P, T]) for n in "qk"}
    scale = 1.0 / np.sqrt(HD)
    stored, v_ready = [], []
    for b in range(nb):
        cols = xc[:, b * T:(b + 1) * T]
        wait = [w_ready, x_ready[b]]
        q = project_small(st, score_ring, w["q"][:, :], bq[:, 0:1], float(scale), value["q"][:, :],
                          cols, q_done, wait, [split_q.last_less])
        s1 = split_q(value["q"][:, :], core.q_parts[b], [q])
        k = project_small(st, score_ring, w["k"][:, :], bk[:, 0:1], 1.0, value["k"][:, :], cols,
                          k_done, wait, [split_k.last_less])
        s2 = split_k(value["k"][:, :], core.k_parts[b], [k])
        stored.append([s1, s2])
        v_ready.append(values_small(st, score_ring, w["v"][:, :], bv[:, :],
                                    v_tok[:, b * NT:(b + 1) * NT, :], cols, v_done, wait))
    strip = core.attn_w[:, 0:GROUP * T].rearrange("p (j x) -> p j x", x=T)
    strip_at = 3 * P
    near = [st.sbuf(f"near{i}", [P, SPLITS, GROUP, NEAR], BF16) for i in range(2)]
    strip_zero, strip_loaded = st.sem("strip_zero"), st.sem("strip_loaded")
    strip_flipped, strip_kept = st.sem("strip_flipped"), st.sem("strip_kept")
    near_loaded = [st.sem(f"near_loaded{i}") for i in range(2)]
    zero = st.pool(nc.gpsimd.memset, strip, 0.0, sig=strip_zero)
    units = [(g, b) for g in range(H // GROUP) for b in range(nb)]
    near_ready = {}

    def load_strip(g):
        raw = value["q"]
        st.sp.wait(stored[-1][0], split_q.last_less, strip_flipped.at(HALF * g))
        raw_ready = st.load(raw[:, :].rearrange("p (j x) -> p j x", x=NEAR),
                            near_window(core.near_rev, slice(g * GROUP, (g + 1) * GROUP)),
                            strip_loaded)
        for half in range(HALF):
            slot, bank, emptied = small_ring.take()
            st.pe.wait(*emptied, raw_ready)
            st.pe(nc.tensor.matmul, bank, core.flip[:, :], raw[:, half * BANK:(half + 1) * BANK],
                  start=True, stop=True, sig=strip_flipped)
            flips = HALF * g + half + 1
            st.act.wait(strip_flipped.at(flips), zero, heads.last_maxed if g else None)
            st.act(nc.scalar.copy, strip[:, 2 * half:2 * half + 2, strip_at:strip_at + NEAR],
                   bank.rearrange("p (j x) -> p j x", x=NEAR), sig=strip_kept)
            small_ring.done[slot] = [strip_kept.at(flips)]

    def load_near(g):
        for s in range(SPLITS):
            st.sp.wait(heads.scored.at(heads.per_unit * nb * (g - 1)))
            near_ready[g] = st.load(near[g % 2][:, s, :, :],
                                    near_window(core.near_parts[s],
                                                slice(g * GROUP, (g + 1) * GROUP)),
                                    near_loaded[g % 2])

    def near_of(u, j, lo, hi):
        g = units[u][0]
        return [near[g % 2][:, s, j, lo:hi] for s in range(SPLITS)], near_ready[g]

    def strip_of(u, j, n, half):
        g = units[u][0]
        at = BANK - n * P + half * BANK
        return strip[:, j, at:at + BANK], [strip_kept.at(HALF * (g + 1))]

    exps = [st.sbuf(f"exps{i}", [P, 2, BANK]) for i in range(4)]
    weighted = Weighted(st, heads, score_ring, out_ring, small_ring, [e[:, :, :] for e in exps],
                        lambda: v_tok, lambda: ctx_tok)

    def maxima(u):
        g, b = units[u]
        steps = heads.maxima(u, small_ring)

        def first(f, args):
            if b == 0:
                load_strip(g)
            if u == 0:
                heads.fill(0, b, g, stored[b])
            f(*args)

        def ahead(f, args):
            if b == 0:
                load_near(g)
            if u + 1 < len(units):
                g2, b2 = units[u + 1]
                heads.fill(u + 1, b2, g2, stored[b2])
            f(*args)
        steps[0] = (first, steps[0])
        steps[24] = (ahead, steps[24])
        return steps

    interleave(range(len(units)), maxima,
               lambda u: weighted.steps(u, units[u][1] * NT, units[u][1] * NT, units[u][0],
                                        lambda: v_ready[units[u][1]]), lag=6)

    ctx_chn = Ring(weighted.out_chn)
    turn_ctx = Turn(st, small_ring, "_ctx")
    rows, norm = Rows(st, small_ring), Norm(st)
    done = weighted.context.at(4 * HALF * len(units))
    for b in range(nb):
        for n in range(b * NT, (b + 1) * NT, 4):
            cslot, chn, free = ctx_chn.take()
            kept = turn_ctx(ctx_tok[:, n:n + 4, :], chn[:, :], [done] + free)
            y = rows(lambda k, m: chn[:, m * P:(m + 1) * P], lambda k: w["o"][:, :], bo[:, :],
                     x[:, n:n + 4, :], x[:, n:n + 4, :], [kept, w_ready])
            ctx_chn.done[cslot] = [y]
        tiles = slice(b * NT, (b + 1) * NT)
        out = norm(x[:, tiles, :], x[:, tiles, :], [y])
        for n in range(b * NT, (b + 1) * NT, 4):
            kept = turn(x[:, n:n + 4, :], xc[:, n * P:n * P + BANK], [out])
    st.run()


def ternary_ffn(core):
    st = Stage(core, "tern")
    nc, inp = core.nc, core.inp
    x, xc, nb = core.x_tok, core.x_chn, core.n_batch
    banks = st.psum("p", 4)
    ring = Ring([banks[:, i, :] for i in range(4)])
    loaded, chain, summed = st.sem("loaded"), st.sem("chain"), st.sem("summed")
    w = st.sbuf("w", [P, C])
    up, down, total, delta = (st.sbuf(n, s) for n, s in (("up", [P, C]), ("down", [P, C]),
                                                         ("total", [P, 1]), ("delta", [P, 2])))
    st.load(w[:, :], inp["L0_ffn_weight_t"][:, :], loaded)
    alpha = st.sbuf("alpha", [P, 1])
    st.load(alpha[:, :], inp["L0_ffn_alpha"].rearrange("(o n) -> o n", o=1).broadcast_to([P, 1]),
            loaded)
    bias, t = broadcast_rows(st, "bias", inp["L0_ffn_bias"], C, loaded)
    st.dve.wait(t)
    v = st.dve(nc.vector.tensor_reduce, total[:, :], w[:, :], AX.X, ALU.add,
               apply_absolute_value=True, sig=chain)
    slot, bank, free = ring.take()
    st.pe.wait(v, core.const_ready)
    mm = st.pe(nc.tensor.matmul, bank[:, 0:1], core.ones[:, :], total[:, :], start=True, stop=True, sig=summed)
    st.dve.wait(mm)
    v = st.dve(nc.vector.tensor_scalar, delta[:, 0:1], bank[:, 0:1], 1.0 / (C * C), 0.7, ALU.mult,
               ALU.mult, sig=chain)
    ring.done[slot] = [v]
    st.dve.wait(v)
    v = st.dve(nc.vector.tensor_scalar, delta[:, 1:2], delta[:, 0:1], -1.0, None, ALU.mult, sig=chain)
    st.dve.wait(v)
    v = st.dve(nc.vector.tensor_scalar, up[:, :], w[:, :], delta[:, 0:1], None, ALU.is_gt, sig=chain)
    st.dve.wait(v)
    v = st.dve(nc.vector.tensor_scalar, down[:, :], w[:, :], delta[:, 1:2], None, ALU.is_lt, sig=chain)
    st.dve.wait(v)
    v = st.dve(nc.vector.tensor_tensor, up[:, :], up[:, :], down[:, :], ALU.subtract,
               sig=chain)
    st.dve.wait(v)
    w_ready = st.dve(nc.vector.tensor_scalar, up[:, :], up[:, :], alpha[:, 0:1], None, ALU.mult, sig=chain)
    rows, norm, turn = Rows(st, ring), Norm(st), Turn(st, ring)
    for b in range(nb):
        for n in range(b * NT, (b + 1) * NT, 4):
            y = rows(lambda k, m: xc[:, (n + m) * P:(n + m + 1) * P], lambda k: up[:, :],
                     bias[:, :], x[:, n:n + 4, :], x[:, n:n + 4, :], [w_ready])
        tiles = slice(b * NT, (b + 1) * NT)
        out = norm(x[:, tiles, :], x[:, tiles, :], [y])
        for n in range(b * NT, (b + 1) * NT, 4):
            turn(x[:, n:n + 4, :], xc[:, n * P:n * P + BANK], [out])
    st.run()


TAPS = 4
LOG1P_TERMS = 9


def linear_attention(core):
    st = Stage(core, "lin")
    nc, inp, const, nb = core.nc, core.inp, core.const, core.n_batch
    x, xc = core.x_tok, core.x_chn
    work_banks, out_banks = st.psum("work", 6), st.psum("out", 2)
    pairs = Ring([work_banks[:, 2 * i:2 * i + 2, :] for i in range(3)])
    out_free = []
    loaded = st.sem("loaded")
    w_qkv = st.sbuf("w_qkv", [P, 3 * C])
    w_z, w_out = st.sbuf("w_z", [P, C]), st.sbuf("w_out", [P, C])
    w_gate = st.sbuf("w_gate", [P, 2 * H])
    taps = st.sbuf("taps", [P, 3, TAPS])
    st.load(w_qkv[:, :], inp["L1_attn_W_qkv_t"][:, :], loaded)
    st.load(w_z[:, :], inp["L1_attn_W_z_t"][:, :], loaded)
    st.load(w_out[:, :], inp["L1_attn_W_out_t"][:, :], loaded)
    st.load(w_gate[:, 0:H], inp["L1_attn_W_b_t"][:, :], loaded)
    st.load(w_gate[:, H:2 * H], inp["L1_attn_W_a_t"][:, :], loaded)
    st.load(taps[:, :, :], inp["L1_attn_conv_w"].rearrange("(g p) o k -> p g (o k)", p=P), loaded)
    same_head = st.sbuf("same_head", [P, C])
    pick_v, place_v = st.sbuf("pick_v", [P, HD, C]), st.sbuf("place_v", [P, HD, C])
    gate_rows = st.sbuf("gate_rows", [2 * H, 2, C])
    st.load(same_head[:, :], const["same_head"][:, :], loaded)
    st.load(pick_v[:, :, :], const["pick_v"][:, :, :], loaded)
    st.load(place_v[:, :, :], const["place_v"][:, :, :], loaded)
    st.load(gate_rows[:, :, :], const["gate_rows"][:, :, :], loaded)
    dt_bias, _ = broadcast_rows(st, "dt_bias", inp["L1_attn_dt_bias"], H, loaded)
    a_log, ready = broadcast_rows(st, "a_log", inp["L1_attn_A_log"], H, loaded)
    ready = [ready, core.const_ready]
    small = st.sbuf("small", [P, 1])
    small_ready = st.pool(nc.gpsimd.memset, small[:, :], 1e-6, sig=st.sem("small_ready"))

    n_tiles = nb * NT
    gates = st.sbuf("gates", [P, n_tiles, 2 * H])
    z, e, s, s2, poly = (st.sbuf(n, [P, n_tiles, H]) for n in ("gz", "ge", "gs", "gs2", "gpoly"))
    rate = st.sbuf("rate", [P, H])
    g_mm, dv, av = st.sem("g_mm"), st.sem("g_dve"), st.sem("g_act")
    per_bank = BANK // (2 * H)
    slot, bank, free = pairs.take()
    flat = bank.rearrange("p a (n h) -> p (a n) h", h=2 * H)
    for n in range(n_tiles):
        st.pe.wait(*ready)
        mm = st.pe(nc.tensor.matmul, flat[:, n, :], xc[:, n * P:(n + 1) * P], w_gate[:, :],
                   start=True, stop=True, sig=g_mm)
    flat = flat[:, 0:n_tiles, :]
    st.dve.wait(mm, *ready)
    v = st.dve(nc.vector.tensor_tensor, z[:, :, :], flat[:, :, H:2 * H], spread(dt_bias[:, :], n_tiles),
               ALU.add, sig=dv)
    st.dve.wait(v)
    v = st.dve(nc.vector.scalar_tensor_tensor, s[:, :, :], z[:, :, :], -1.0, z[:, :, :], ALU.mult,
               ALU.max, sig=dv)
    st.act.wait(v)
    beta = st.act(nc.scalar.activation, gates[:, :, 0:H], flat[:, :, 0:H], ACT.Sigmoid, sig=av)
    pairs.done[slot] = [v, beta]
    st.act.wait(v)
    a = st.act(nc.scalar.activation, e[:, :, :], s[:, :, :], ACT.Exp, scale=-1.0, sig=av)
    r = st.act(nc.scalar.activation, rate[:, :], a_log[:, :], ACT.Exp, sig=av)
    st.dve.wait(a)
    v = st.dve(nc.vector.tensor_scalar, s[:, :, :], e[:, :, :], 2.0, None, ALU.add,
               sig=dv)
    st.dve.wait(v)
    v = st.dve(nc.vector.reciprocal, s[:, :, :], s[:, :, :], sig=dv)
    st.dve.wait(v)
    v = st.dve(nc.vector.tensor_tensor, s[:, :, :], s[:, :, :], e[:, :, :], ALU.mult,
               sig=dv)
    st.dve.wait(v)
    v = st.dve(nc.vector.tensor_tensor, s2[:, :, :], s[:, :, :], s[:, :, :], ALU.mult,
               sig=dv)
    top = LOG1P_TERMS - 1
    st.dve.wait(v)
    v = st.dve(nc.vector.tensor_scalar, poly[:, :, :], s2[:, :, :], 2.0 / (2 * top + 1), None,
               ALU.mult, sig=dv)
    for n in range(top - 1, 0, -1):
        st.dve.wait(v)
        v = st.dve(nc.vector.scalar_tensor_tensor, poly[:, :, :], poly[:, :, :],
                   2.0 / (2 * n + 1), s2[:, :, :], ALU.add, ALU.mult, sig=dv)
    st.dve.wait(v)
    v = st.dve(nc.vector.scalar_tensor_tensor, poly[:, :, :], poly[:, :, :], 2.0, s[:, :, :],
               ALU.add, ALU.mult, sig=dv)
    st.dve.wait(v)
    v = st.dve(nc.vector.scalar_tensor_tensor, poly[:, :, :], z[:, :, :], 0.0, poly[:, :, :],
               ALU.max, ALU.add, sig=dv)
    st.dve.wait(v, r)
    v = st.dve(nc.vector.tensor_tensor, poly[:, :, :], poly[:, :, :], spread(rate[:, :], n_tiles),
               ALU.mult, sig=dv)
    st.act.wait(v)
    decay = st.act(nc.scalar.activation, gates[:, :, H:2 * H], poly[:, :, :], ACT.Exp, scale=-1.0, sig=av)
    gates_row = st.sbuf("gates_row", [2 * H, nb * T])
    g_turn = st.sem("g_turned")
    for n in range(0, n_tiles, 8):
        slot, bank, free = pairs.take()
        for m in range(8):
            st.pe.wait(*free, decay, beta)
            t = st.pe(nc.tensor.transpose, bank[0:2 * H, m // 4, (m % 4) * P:(m % 4 + 1) * P],
                      gates[:, n + m, :], core.ident[:, :], sig=g_turn)
        st.act.wait(t)
        gates_ready = st.act(nc.scalar.copy,
                             gates_row[:, n * P:(n + 8) * P].rearrange("p (a b) -> p a b", a=2),
                             bank[0:2 * H, :, :], sig=av)
        pairs.done[slot] = [gates_ready]

    PAD = TAPS - 1
    mixed = [st.sbuf(f"mixed{g}", [P, PAD + T]) for g in range(3)]
    conv = [st.sbuf(f"conv{g}", [P, T]) for g in range(3)]
    silu_z, beta_v, decay_b = (st.sbuf(n, [P, T]) for n in ("silu_z", "beta_v", "decay_b"))
    square, norm_r = st.sbuf("square", [P, T]), st.sbuf("norm_r", [P, T])
    drive = Ring([st.sbuf(f"drive{i}", [P, T]) for i in range(2)])
    state = Ring([st.sbuf(f"state{i}", [P, T]) for i in range(2)])
    read_out = Ring([st.sbuf(f"read_out{i}", [P, T]) for i in range(2)])
    o = st.sbuf("o", [P, T])
    mm_s, act_s, dve_s, pool_s = (st.sem(n) for n in ("mm", "act", "dve", "pool"))
    row_ring = Ring([work_banks[:, i, :] for i in range(2)])
    for g in range(3):
        pad = st.pool(nc.gpsimd.memset, mixed[g][:, 0:PAD], 0.0, sig=pool_s)

    def two(ap):
        return ap.rearrange("p (a b) -> p a b", a=HALF)

    def product(w, rhs, after, **kw):
        slot, bank, free = pairs.take()
        for half in range(HALF):
            st.pe.wait(*free, *after)
            mm = st.pe(nc.tensor.matmul, bank[:, half, :], w, rhs[:, half * BANK:(half + 1) * BANK],
                       start=True, stop=True, sig=mm_s)
        return slot, bank, mm

    def head_norm(src, scale, eps_scale, out_scale, after, out):
        st.dve.wait(*after)
        sq = st.dve(nc.vector.tensor_tensor, square[:, :], src, src, ALU.mult,
                    sig=dve_s)
        slot, bank, mm = product(same_head[:, :], square, [sq])
        st.act.wait(mm, small_ready, sq)
        root = st.act(nc.scalar.activation, two(norm_r[:, :]), bank, ACT.Sqrt, bias=small[:, 0:1],
                      scale=scale, sig=act_s)
        pairs.done[slot] = [root]
        st.dve.wait(root)
        inv = st.dve(nc.vector.reciprocal, norm_r[:, :], norm_r[:, :], sig=dve_s)
        st.dve.wait(inv)
        return st.dve(nc.vector.scalar_tensor_tensor, out, src, out_scale, norm_r[:, :], ALU.mult,
                      ALU.mult, sig=dve_s)

    rows, norm = Rows(st, pairs_as_single(pairs)), Norm(st)
    turn = Turn(st, rows.ring)
    gated = st.sbuf("gated", [P, T])
    done = pad
    for b in range(nb):
        cols = xc[:, b * T:(b + 1) * T]
        conv_done = []
        for g in range(3):
            slot, bank, mm = product(w_qkv[:, g * C:(g + 1) * C], cols, ready)
            st.act.wait(mm, done, pad)
            kept = st.act(nc.scalar.copy, two(mixed[g][:, PAD:PAD + T]), bank, sig=act_s)
            pairs.done[slot] = [kept]
            st.dve.wait(kept, done)
            v = st.dve(nc.vector.tensor_scalar, conv[g][:, :], mixed[g][:, PAD:PAD + T],
                       taps[:, g, PAD:PAD + 1], None, ALU.mult, sig=dve_s)
            for k in range(PAD):
                st.dve.wait(v)
                v = st.dve(nc.vector.scalar_tensor_tensor, conv[g][:, :], mixed[g][:, k:k + T],
                           taps[:, g, k:k + 1], conv[g][:, :], ALU.mult, ALU.add,
                           sig=dve_s)
            conv_done.append(v)
        slot, bank, mm = product(w_z[:, :], cols, ready)
        silued = []
        for g in range(3):
            st.act.wait(conv_done[g])
            silued.append(st.act(nc.scalar.activation, conv[g][:, :], conv[g][:, :], ACT.Silu, sig=act_s))
        st.act.wait(mm, done)
        z_done = st.act(nc.scalar.activation, two(silu_z[:, :]), bank, ACT.Silu,
                        sig=act_s)
        pairs.done[slot] = [z_done]
        q = head_norm(conv[0][:, :], 1.0, None, HD ** -0.5, [silued[0]], conv[0][:, :])
        kk = head_norm(conv[1][:, :], 1.0, None, 1.0, [silued[1]], conv[1][:, :])
        row = gates_row[:, b * T:(b + 1) * T]
        slot, bank, mm = product(gate_rows[:, 0, :], row, [gates_ready])
        st.dve.wait(mm, silued[2])
        bv = st.dve(nc.vector.tensor_tensor, two(beta_v[:, :]), bank, two(conv[2][:, :]), ALU.mult, sig=dve_s)
        pairs.done[slot] = [bv]
        slot, bank, mm = product(gate_rows[:, 1, :], row, [gates_ready])
        st.act.wait(mm, done)
        dec = st.act(nc.scalar.copy, two(decay_b[:, :]), bank, sig=act_s)
        pairs.done[slot] = [dec]
        waiting = []

        def put(vi, ro, read):
            for half in range(HALF):
                st.pe.wait(*out_free, read)
                mm = st.pe(nc.tensor.matmul, out_banks[:, half, :], place_v[:, vi, :],
                           ro[:, half * BANK:(half + 1) * BANK], start=vi == 0, stop=vi == HD - 1, sig=mm_s)
            return mm

        for vi in range(HD):
            slot, bank, mm = product(pick_v[:, vi, :], beta_v, [bv])
            ds, dr, dfree = drive.take()
            st.dve.wait(mm, kk, *dfree)
            v = st.dve(nc.vector.tensor_tensor, two(dr[:, :]), bank, two(conv[1][:, :]), ALU.mult, sig=dve_s)
            pairs.done[slot] = [v]
            ss, sc, sfree = state.take()
            st.dve.wait(v, dec, *sfree)
            v = st.dve(nc.vector.tensor_tensor_scan, sc[:, :], decay_b[:, :], dr[:, :], 0.0,
                       ALU.mult, ALU.add, sig=dve_s)
            drive.done[ds] = [v]
            rs, ro, rfree = read_out.take()
            st.pool.wait(v, q, *rfree)
            r = st.pool(nc.gpsimd.tensor_tensor, ro[:, :], sc[:, :], conv[0][:, :], ALU.mult, sig=pool_s)
            state.done[ss] = [r]
            waiting.append((vi, ro, r, rs))
            if len(waiting) > 1:
                a = waiting.pop(0)
                read_out.done[a[3]] = [put(*a[:3])]
        a = waiting.pop(0)
        mm = put(*a[:3])
        read_out.done[a[3]] = [mm]
        st.act.wait(mm)
        kept = st.act(nc.scalar.copy, two(o[:, :]), out_banks[:, :, :], sig=act_s)
        out_free = [kept]
        v = head_norm(o[:, :], 1.0 / HD, None, 1.0, [kept], o[:, :])
        st.dve.wait(v)
        gd = st.dve(nc.vector.tensor_tensor, gated[:, :], o[:, :], silu_z[:, :], ALU.mult, sig=dve_s)
        done = gd
        for n in range(b * NT, (b + 1) * NT, 4):
            m0 = n - b * NT
            y = rows(lambda k, m: gated[:, (m0 + m) * P:(m0 + m + 1) * P], lambda k: w_out[:, :],
                     None, x[:, n:n + 4, :], x[:, n:n + 4, :], [gd])
        tiles = slice(b * NT, (b + 1) * NT)
        out = norm(x[:, tiles, :], x[:, tiles, :], [y])
        for n in range(b * NT, (b + 1) * NT, 4):
            turn(x[:, n:n + 4, :], xc[:, n * P:n * P + BANK], [out])
    st.run()


class pairs_as_single:

    def __init__(self, pairs):
        self.pairs, self.done = pairs, pairs.done

    def take(self):
        slot, bank, free = self.pairs.take()
        return slot, bank[:, 0, :], free


class TopTwo:

    def __init__(self, st, tiles, n):
        self.st, self.tiles, self.n = st, tiles, n
        self.a, self.b, self.first, self.second = (st.sbuf(f"top_{i}", [P, tiles, n])
                                                   for i in ("a", "b", "first", "second"))
        self.m1, self.m2, self.key = (st.sbuf(f"top_{i}", [P, tiles]) for i in ("m1", "m2", "key"))
        self.ramp = st.sbuf("top_ramp", [P, n])
        self.loaded, self.dv = st.sem("top_loaded"), st.sem("top_dve")
        self.ramp_ready = st.load(self.ramp[:, :], st.core.const[f"ramp{n}"][:, :], self.loaded)

    def pick(self, scores, peak, hot, after):
        st, nc, n = self.st, self.st.nc, self.n
        st.dve.wait(*after)
        v = st.dve(nc.vector.tensor_reduce, peak[:, :], scores, AX.X, ALU.max,
                   sig=self.dv)
        st.dve.wait(v)
        v = st.dve(nc.vector.tensor_tensor, self.a[:, :, :], scores, along(peak[:, :], n),
                   ALU.is_equal, sig=self.dv)
        st.dve.wait(v, self.ramp_ready)
        v = st.dve(nc.vector.tensor_tensor, self.a[:, :, :], self.a[:, :, :],
                   spread(self.ramp[:, :], self.tiles), ALU.mult,
                   sig=self.dv)
        st.dve.wait(v)
        v = st.dve(nc.vector.tensor_reduce, self.key[:, :], self.a[:, :, :], AX.X, ALU.max, sig=self.dv)
        st.dve.wait(v)
        return st.dve(nc.vector.tensor_tensor, hot[:, :, :], self.a[:, :, :],
                      along(self.key[:, :], n), ALU.is_equal, sig=self.dv)

    def __call__(self, scores, gates, after):
        st, nc, n = self.st, self.st.nc, self.n
        v = self.pick(scores, self.m1, self.first, after)
        st.dve.wait(v)
        v = st.dve(nc.vector.scalar_tensor_tensor, self.b[:, :, :], self.first[:, :, :], -4.0,
                   scores, ALU.mult, ALU.add, sig=self.dv)
        v = self.pick(self.b[:, :, :], self.m2, self.second, [v])
        st.dve.wait(v)
        v = st.dve(nc.vector.tensor_tensor, self.key[:, :], self.m1[:, :], self.m2[:, :], ALU.add, sig=self.dv)
        st.dve.wait(v)
        v = st.dve(nc.vector.reciprocal, self.key[:, :], self.key[:, :], sig=self.dv)
        for m, hot in ((self.m1, self.first), (self.m2, self.second)):
            st.dve.wait(v)
            v = st.dve(nc.vector.tensor_tensor, m[:, :], m[:, :], self.key[:, :], ALU.mult, sig=self.dv)
            st.dve.wait(v)
            v = st.dve(nc.vector.tensor_tensor, hot[:, :, :], hot[:, :, :], along(m[:, :], n),
                       ALU.mult, sig=self.dv)
        st.dve.wait(v)
        return st.dve(nc.vector.tensor_tensor, gates, self.first[:, :, :], self.second[:, :, :],
                      ALU.add, sig=self.dv)


def router(st, ring, w, bias, chn, n_tiles, n, out, done, after):
    nc = st.nc
    slot, bank, free = ring.take()
    flat = bank.rearrange("p (t e) -> p t e", e=n)
    for t in range(n_tiles):
        st.pe.wait(*after, *free)
        mm = st.pe(nc.tensor.matmul, flat[:, t, :], chn[:, t * P:(t + 1) * P], w, start=True,
                   stop=True, sig=st.routed)
    st.dve.wait(mm, *after)
    kept = st.dve(nc.vector.tensor_tensor, out, flat[:, 0:n_tiles, :], spread(bias, n_tiles),
                  ALU.add, sig=done)
    ring.done[slot] = [kept]
    return kept


def gate_rows_of(st, ring, gates, rows, n_tiles, n, after):
    nc = st.nc
    turned, kept = st.sem("gates_turned"), st.sem("gates_kept")
    for t in range(0, n_tiles, 4):
        slot, bank, free = ring.take()
        for m in range(4):
            st.pe.wait(*free, *after)
            mm = st.pe(nc.tensor.transpose, bank[0:n, m * P:(m + 1) * P], gates[:, t + m, :],
                       st.core.ident[:, :], sig=turned)
        st.act.wait(mm)
        last = st.act(nc.scalar.copy, rows[:, t * P:(t + 4) * P], bank[0:n, :],
                      sig=kept)
        ring.done[slot] = [last]
    return last


E1, I1 = 16, 64


def expert_ffn(core):
    st = Stage(core, "moe1")
    nc, inp, const, nb = core.nc, core.inp, core.const, core.n_batch
    x, xc = core.x_tok, core.x_chn
    n_tiles = nb * NT
    banks = st.psum("p", 8)
    ring = Ring([banks[:, i, :] for i in range(6)])
    out_ring = Ring([banks[:, 6 + i, :] for i in range(2)])
    st.routed = st.sem("routed")
    loaded, big_loaded = st.sem("loaded"), st.sem("big_loaded")
    w_router = st.sbuf("w_router", [P, E1])
    pair_rows = st.sbuf("pair_rows", [E1, E1 // 2, P])
    st.load(w_router[:, :], inp["L1_ffn_gate_w"][:, :], loaded)
    st.load(pair_rows[:, :, :], const["pair_rows"][:, :, :], loaded)
    router_bias, small_ready = broadcast_rows(st, "router_bias", inp["L1_ffn_gate_b"], E1, loaded)
    pairs_n = E1 // 2
    wg, wu = st.sbuf("wg", [P, E1, I1]), st.sbuf("wu", [P, E1, I1])
    wd = st.sbuf("wd", [P, pairs_n, C])
    sg, su, sd = st.sbuf("sg", [P, I1]), st.sbuf("su", [P, I1]), st.sbuf("sd", [I1, C])
    st.load(sg[:, :], inp["L1_ffn_shared_wg"][:, :], big_loaded)
    st.load(su[:, :], inp["L1_ffn_shared_wu"][:, :], big_loaded)
    st.load(sd[:, :], inp["L1_ffn_shared_wd"][:, :], big_loaded)
    st.load(wg[:, :, :], inp["L1_ffn_experts_wg"].rearrange("e d i -> d e i"), big_loaded)
    st.load(wu[:, :, :], inp["L1_ffn_experts_wu"].rearrange("e d i -> d e i"), big_loaded)
    w_ready = st.load(wd[:, :, :], inp["L1_ffn_experts_wd"].rearrange("(m e) i d -> (e i) m d", e=2),
                      big_loaded)
    logits, gates = st.sbuf("logits", [P, n_tiles, E1]), st.sbuf("gates", [P, n_tiles, E1])
    gate_row = st.sbuf("gate_row", [E1, nb * T])
    r_done, sig_done = st.sem("logits_done"), st.sem("sigmoid_done")
    v = router(st, ring, w_router[:, :], router_bias[:, :], xc, n_tiles, E1, logits[:, :, :],
               r_done, [small_ready])
    st.act.wait(v)
    v = st.act(nc.scalar.activation, logits[:, :, :], logits[:, :, :], ACT.Sigmoid,
               sig=sig_done)
    top = TopTwo(st, n_tiles, E1)
    v = top(logits[:, :, :], gates[:, :, :], [v])
    row_ready = gate_rows_of(st, ring, gates, gate_row, n_tiles, E1, [v])
    act_g = Ring([st.sbuf(f"act_g{i}", [P, BANK]) for i in range(3)])
    hidden = Ring([st.sbuf(f"hidden{i}", [P, BANK]) for i in range(3)])
    up_mm, silued, lifted, scaled, down_mm = (st.sem(n) for n in
                                              ("up_mm", "silued", "lifted", "scaled", "down_mm"))
    added = st.sem("added")
    norm, turn = Norm(st), Turn(st, ring)
    for b in range(nb):
        for n in range(b * NT, (b + 1) * NT, 4):
            cols = xc[:, n * P:n * P + BANK]
            oslot, out, ofree = out_ring.take()
            late = []

            def down(m, k, h, hslot, ready):
                rows = I1 if m == 0 else P
                for i in range(4):
                    st.pe.wait(*ofree, ready, w_ready)
                    mm = st.pe(nc.tensor.matmul, banks4(out)[:, i, :], h[0:rows, i * P:(i + 1) * P],
                               k, start=m == 0 and i == 0, stop=m == pairs_n, skip_group_check=True, sig=down_mm)
                hidden.done[hslot] = [mm]
                return mm

            for m in range(pairs_n + 1):
                if m == 0:
                    g_w, u_w, k, r = sg[:, :], su[:, :], sd[:, :], I1
                else:
                    pair = slice(2 * (m - 1), 2 * m)
                    g_w = wg[:, pair, :].rearrange("p e i -> p (e i)")
                    u_w = wu[:, pair, :].rearrange("p e i -> p (e i)")
                    k, r = wd[:, m - 1, :], P
                gs, gb, gfree = ring.take()
                st.pe.wait(*gfree, w_ready)
                mm_g = st.pe(nc.tensor.matmul, gb[0:r, :], g_w, cols, start=True, stop=True, sig=up_mm)
                us, ub, ufree = ring.take()
                st.pe.wait(*ufree)
                mm_u = st.pe(nc.tensor.matmul, ub[0:r, :], u_w, cols, start=True, stop=True, sig=up_mm)
                a_s, ag, afree = act_g.take()
                st.act.wait(mm_g, *afree)
                a = st.act(nc.scalar.activation, ag[0:r, :], gb[0:r, :], ACT.Silu, sig=silued)
                ring.done[gs] = [a]
                hs, h, hfree = hidden.take()
                st.dve.wait(a, mm_u, *hfree)
                v = st.dve(nc.vector.tensor_tensor, h[0:r, :], ub[0:r, :], ag[0:r, :], ALU.mult, sig=lifted)
                ring.done[us] = [v]
                act_g.done[a_s] = [v]
                if m:
                    bs, bb, bfree = ring.take()
                    st.pe.wait(*bfree, row_ready)
                    mm = st.pe(nc.tensor.matmul, bb, pair_rows[:, m - 1, :],
                               gate_row[:, n * P:n * P + BANK], start=True, stop=True, sig=up_mm)
                    st.dve.wait(v, mm)
                    v = st.dve(nc.vector.tensor_tensor, h[:, :], bb, h[:, :], ALU.mult, sig=scaled)
                    ring.done[bs] = [v]
                late.append((m, k, h, hs, v))
                if len(late) > 1:
                    down(*late.pop(0))
            mm = down(*late.pop(0))
            st.dve.wait(mm)
            y = st.dve(nc.vector.scalar_tensor_tensor, x[:, n:n + 4, :], x[:, n:n + 4, :], 2.0,
                       banks4(out), ALU.mult, ALU.add, sig=added)
            out_ring.done[oslot] = [y]
        tiles = slice(b * NT, (b + 1) * NT)
        done = norm(x[:, tiles, :], x[:, tiles, :], [y])
        for n in range(b * NT, (b + 1) * NT, 4):
            turn(x[:, n:n + 4, :], xc[:, n * P:n * P + BANK], [done])
    st.run()


def causal_attention(core):
    st = Stage(core, "caus")
    nc, inp, const, nb = core.nc, core.inp, core.const, core.n_batch
    x, xc = core.x_tok, core.x_chn
    score_banks, small_banks, out_banks = st.psum("score", 4), st.psum("small", 2), st.psum("out", 2)
    score_ring = Ring([score_banks[:, 0:2, :], score_banks[:, 2:4, :]])
    small_ring = Ring([small_banks[:, 0, :], small_banks[:, 1, :]])
    out_ring = Ring([out_banks[:, 0, :], out_banks[:, 1, :]])
    st.projected = st.sem("projected")
    loaded = st.sem("loaded")
    w = st.sbuf("w", [P, 2 * C])
    bias = st.sbuf("bias", [P, 2])
    head_w = st.sbuf("head_w", [P, H, C])
    st.load(w[:, :], inp["L2_attn_W_attn"][:, :], loaded)
    st.load(bias[:, :], inp["L2_attn_b_attn_c"][:, :], loaded)
    w_ready = st.load(head_w[:, :, :], inp["L2_attn_head_weights"].rearrange("(o h) c -> o h c", o=1)
                      .broadcast_to([P, H, C]), loaded)
    heads = SmallHeads(st, 2 * (BANK // P) * 3, core.q_parts, core.k_parts, const["zero_rows"],
                       causal=True)
    q_done, k_done = st.sem("q_done"), st.sem("k_done")
    split_q, split_k = Parts(st, "q"), Parts(st, "k")
    value = {n: st.sbuf(f"value_{n}", [P, T]) for n in "qk"}
    stored = []
    for b in range(nb):
        cols = xc[:, b * T:(b + 1) * T]
        q = project_small(st, score_ring, w[:, 0:C], bias[:, 0:1], HD ** -0.5, value["q"][:, :],
                          cols, q_done, [w_ready], [split_q.last_less])
        s1 = split_q(value["q"][:, :], core.q_parts[b], [q])
        k = project_small(st, score_ring, w[:, C:2 * C], bias[:, 1:2], 1.0, value["k"][:, :],
                          cols, k_done, [w_ready], [split_k.last_less])
        s2 = split_k(value["k"][:, :], core.k_parts[b], [k])
        stored.append([s1, s2])

    x_one = [st.sbuf(f"x_one{i}", [P, NT, C + 1]) for i in range(2)]
    y = [core.attn_w[:, i * T:(i + 1) * T].rearrange("p (n c) -> p n c", c=C) for i in range(2)]
    e = core.big[:, 0:2 * NT * BANK].rearrange("p (a k q) -> p a k q", a=2, k=NT)
    x_made, y_zero, exped, weighted = (st.sem(n) for n in (
        "x_made", "y_zero", "exped", "weighted"))
    inverted, scaled, summed = st.sem("inverted"), st.sem("scaled"), st.sem("summed")
    scored = heads.scored
    r_sum = st.sbuf("r_sum", [P, 2])
    part = [st.sbuf(f"part{i}", [P, 2, C]) for i in range(3)]
    units = [(b, g) for b in range(nb) for g in range(H // GROUP)]
    QB = BANK // P
    norm, turn = Norm(st), Turn(st, small_ring)
    x_added = st.sem("x_added")
    n = {"tile": 0, "pair": 0, "out": 0}
    outs_of_pair = 2 * (QB // 2)
    outs_of_batch = H // 2 * HALF * outs_of_pair

    def steps(u):
        b, g = units[u]
        i = u % heads.SLOTS
        q, k = heads.q_stack[i], heads.k_stack[i]

        def start_batch():
            st.pool.wait(weighted.at(outs_of_batch * (b - 1)))
            st.pool(nc.gpsimd.memset, x_one[b % 2][:, :, C:C + 1], 1.0, sig=x_made)
            st.pool.wait(x_made.at(2 * b + 1))
            st.pool(nc.gpsimd.tensor_copy, x_one[b % 2][:, :, 0:C], x[:, b * NT:(b + 1) * NT, :],
                    sig=x_made)
            st.pool.wait(x_added.at(b - 1))
            st.pool(nc.gpsimd.memset, y[b % 2], 0.0, sig=y_zero)

        def scores(half, pair, kb):
            if g == 0 and half == 0 and pair == 0 and kb == 0:
                start_batch()
            t = n["tile"]
            n["tile"] += 1
            banks = score_ring.buffers[t % 2]
            diagonal = kb >= half * QB
            lo = max(kb * P - half * BANK, 0)
            st.pe.wait(heads.row_ready[i], heads.ready[i])
            st.pe.wait(exped.at(t - 1), *(score_ring.done[t % 2] if t < 2 else ()))
            for a in range(2):
                j = 2 * pair + a
                st.pe(nc.tensor.matmul, banks[:, a, lo:BANK], k[0:STACK, j, kb * P:(kb + 1) * P],
                      q[0:STACK, j, half * BANK + lo:(half + 1) * BANK], start=True,
                      stop=not diagonal, sig=scored if a == 1 and not diagonal else None)
                if diagonal:
                    st.pe(nc.tensor.matmul, banks[:, a, lo:lo + P], st.core.ident_bf[:, :],
                          st.core.causal_mask[:, :], start=False, stop=True,
                          sig=scored if a == 1 else None)
            st.act.wait(scored.at(t + 1), weighted.at(outs_of_pair * n["pair"]))
            st.act(nc.scalar.activation, e[:, :, kb, lo:BANK], banks[:, :, lo:BANK], ACT.Exp,
                   sig=exped)
            if kb == QB * (half + 1) - 1:
                st.pe.wait(exped.at(t + 1), x_made.at(2 * (b + 1)))
                for a in range(2):
                    for two in range(QB // 2):
                        weigh(half, 2 * pair + a, a, two)
                n["pair"] += 1

        def weigh(half, j, a, two):
            o = n["out"]
            n["out"] += 1
            out, p = out_ring.buffers[o % 2], part[o % 3]
            st.pe.wait(scaled.at(2 * (o - 1)))
            for m in range(2):
                nq = 2 * two + m
                kbs = half * QB + nq + 1
                for kb in range(kbs):
                    st.pe(nc.tensor.matmul, out[:, m * (C + 1):(m + 1) * (C + 1)],
                          e[:, a, kb, nq * P:(nq + 1) * P], x_one[b % 2][:, kb, :],
                          start=kb == 0, stop=kb == kbs - 1,
                          sig=weighted if m == 1 and kb == kbs - 1 else None)
            both = out[:, 0:2 * (C + 1)].rearrange("p (m c) -> p m c", c=C + 1)
            st.dve.wait(weighted.at(o + 1), scaled.at(2 * o))
            st.dve(nc.vector.reciprocal, r_sum[:, :], both[:, :, C], sig=inverted)
            st.dve.wait(inverted.at(o + 1), w_ready, summed.at(o - 2))
            for m in range(2):
                st.dve(nc.vector.scalar_tensor_tensor, p[:, m, :], both[:, m, 0:C],
                       r_sum[:, m:m + 1], head_w[:, g * GROUP + j, :], ALU.mult, ALU.mult,
                       sig=scaled)
            at = half * QB + 2 * two
            st.pool.wait(scaled.at(2 * (o + 1)), y_zero.at(b + 1), summed.at(o))
            st.pool(nc.gpsimd.tensor_tensor, y[b % 2][:, at:at + 2, :], y[b % 2][:, at:at + 2, :],
                    p[:, :, :], ALU.add, sig=summed)

        def finish():
            tiles = slice(b * NT, (b + 1) * NT)
            st.dve.wait(summed.at(outs_of_batch * (b + 1)))
            st.dve(nc.vector.tensor_tensor, x[:, tiles, :], x[:, tiles, :], y[b % 2], ALU.add,
                   sig=x_added)
            out = norm(x[:, tiles, :], x[:, tiles, :], [x_added.at(b + 1)])
            for m in range(b * NT, (b + 1) * NT, 4):
                turn(x[:, m:m + 4, :], xc[:, m * P:m * P + BANK], [out])

        out = [(scores, (half, pair, kb)) for half in range(HALF) for pair in range(2)
               for kb in range(QB * (half + 1))]
        if g == H // GROUP - 1:
            f, a = out[-1]
            out[-1] = (lambda *args: (f(*args), finish()), a)
        return out

    def maxima(u):
        b, g = units[u]
        out = heads.maxima(u, small_ring)

        def first(f, args):
            if u == 0:
                heads.fill(0, b, g, stored[b])
            f(*args)

        def ahead(f, args):
            if u + 1 < len(units):
                b2, g2 = units[u + 1]
                heads.fill(u + 1, b2, g2, stored[b2])
            f(*args)
        out[0] = (first, out[0])
        out[24] = (ahead, out[24])
        return out

    interleave(range(len(units)), maxima, steps, lag=4)
    st.run()


E2, FF = 8, 512


def rotary_attention(core):
    st = Stage(core, "rot")
    nc, inp, const, nb = core.nc, core.inp, core.const, core.n_batch
    x, xc, x1 = core.x_tok, core.x_chn, core.x_mid
    score_banks, small_banks, out_banks = st.psum("score", 4), st.psum("small", 2), st.psum("out", 2)
    score_ring = Ring([score_banks[:, 0:2, :], score_banks[:, 2:4, :]])
    small_ring = Ring([small_banks[:, 0, :], small_banks[:, 1, :]])
    out_ring = Ring([out_banks[:, 0, :], out_banks[:, 1, :]])
    st.projected = st.sem("projected")
    w_loaded = st.sem("w_loaded")
    w = {}
    for n in "qkvo":
        w[n] = st.sbuf(f"w{n}", [P, C])
        st.load(w[n][:, :], inp[f"L2_ffn_W{n}"][:, :], w_loaded)
    bq, _ = column(st, "bq", inp["L2_ffn_bq"], w_loaded)
    bk, _ = column(st, "bk", inp["L2_ffn_bk"], w_loaded)
    bv, _ = broadcast_rows(st, "bv", inp["L2_ffn_bv"], C, w_loaded)
    bo, _ = broadcast_rows(st, "bo", inp["L2_ffn_bo"], C, w_loaded)
    g1, _ = broadcast_rows(st, "g1", inp["L2_ffn_g1"], C, w_loaded)
    be1, _ = broadcast_rows(st, "be1", inp["L2_ffn_be1"], C, w_loaded)
    rotate = st.sbuf("rotate", [P, C])
    angle = core.big[:, 2 * T:4 * T].rearrange("p (a t) -> p a t", a=2)
    st.load(rotate[:, :], const["rotate"][:, :], w_loaded)
    w_ready = st.load(angle, const["angle"][:, :, :], w_loaded)
    heads = SmallHeads(st, HALF * NT * 2, core.q_parts, core.k_parts, const["zero_rows"])
    done = {n: st.sem(f"{n}_done") for n in "qkv"}
    split = {n: Parts(st, n) for n in "qk"}
    value = {n: st.sbuf(f"value_{n}", [P, T]) for n in "qk"}
    turned = Ring([core.big[:, i * T:(i + 1) * T] for i in range(2)])
    v_tok = core.big[:, 4 * T:4 * T + nb * T].rearrange("p (n c) -> p n c", c=C)
    rot_mm, rot_v = st.sem("rot_mm"), st.sem("rot_v")
    bias = {"q": bq, "k": bk}
    scale = {"q": HD ** -0.5, "k": 1.0}
    dram = {"q": core.q_parts, "k": core.k_parts}
    stored, v_ready = [], []

    def two(ap):
        return ap.rearrange("p (a b) -> p a b", a=HALF)

    for b in range(nb):
        cols = xc[:, b * T:(b + 1) * T]
        both = []
        for n in "qk":
            val = value[n]
            ready = project_small(st, score_ring, w[n][:, :], bias[n][:, 0:1], scale[n], val[:, :],
                                  cols, done[n], [w_ready], [split[n].last_less])
            slot, bank, free = score_ring.take()
            for half in range(HALF):
                st.pe.wait(*free, ready)
                mm = st.pe(nc.tensor.matmul, bank[:, half, :], rotate[:, :],
                           val[:, half * BANK:(half + 1) * BANK], start=True, stop=True, sig=rot_mm)
            ts, t, tfree = turned.take()
            st.dve.wait(mm, *tfree)
            r = st.dve(nc.vector.tensor_tensor, two(t), bank, two(angle[:, 1, :]), ALU.mult, sig=rot_v)
            score_ring.done[slot] = [r]
            st.dve.wait(r)
            v = st.dve(nc.vector.tensor_tensor, val[:, :], val[:, :], angle[:, 0, :], ALU.mult, sig=rot_v)
            st.dve.wait(v)
            v = st.dve(nc.vector.tensor_tensor, val[:, :], val[:, :], t, ALU.add,
                       sig=rot_v)
            turned.done[ts] = [v]
            both.append(split[n](val[:, :], dram[n][b], [v]))
        stored.append(both)
        v_ready.append(values_small(st, score_ring, w["v"][:, :], bv[:, :],
                                    v_tok[:, b * NT:(b + 1) * NT, :], cols, done["v"], [w_ready]))
    units = [(b, g) for b in range(nb) for g in range(H // GROUP)]
    exps = [core.attn_w[:, i * T:(i + 1) * T].rearrange("p (a q) -> p a q", a=2) for i in range(4)]
    ctx = [st.sbuf(f"ctx{i}", [P, NT, C]) for i in range(2)]
    at = {"b": 0}
    weighted = Weighted(st, heads, score_ring, out_ring, small_ring, exps,
                        lambda: v_tok, lambda: ctx[at["b"] % 2])
    ctx_chn = Ring(weighted.out_chn)
    turn, turn_ctx = Turn(st, small_ring), Turn(st, small_ring, "_ctx")
    rows, norm = Rows(st, small_ring), Norm(st)
    affine = st.sem("affine")

    def finish(b):
        c = ctx[b % 2]
        done_b = weighted.context.at(4 * HALF * (H // GROUP) * (b + 1))
        for n in range(0, NT, 4):
            cslot, chn, free = ctx_chn.take()
            kept = turn_ctx(c[:, n:n + 4, :], chn[:, :], [done_b] + free)
            m0 = b * NT + n
            y = rows(lambda k, m: chn[:, m * P:(m + 1) * P], lambda k: w["o"][:, :], bo[:, :],
                     x[:, m0:m0 + 4, :], x1[:, m0:m0 + 4, :], [kept, w_ready])
            ctx_chn.done[cslot] = [y]
        tiles = slice(b * NT, (b + 1) * NT)
        out = norm(x1[:, tiles, :], x1[:, tiles, :], [y])
        st.dve.wait(out)
        v = st.dve(nc.vector.tensor_tensor, x1[:, tiles, :], x1[:, tiles, :], spread(g1[:, :], NT),
                   ALU.mult, sig=affine)
        st.dve.wait(v)
        v = st.dve(nc.vector.tensor_tensor, x1[:, tiles, :], x1[:, tiles, :], spread(be1[:, :], NT),
                   ALU.add, sig=affine)
        for n in range(b * NT, (b + 1) * NT, 4):
            turn(x1[:, n:n + 4, :], xc[:, n * P:n * P + BANK], [v])

    def maxima(u):
        b, g = units[u]
        out = heads.maxima(u, small_ring)

        def first(f, args):
            if u == 0:
                heads.fill(0, b, g, stored[b])
            f(*args)

        def ahead(f, args):
            if u + 1 < len(units):
                b2, g2 = units[u + 1]
                heads.fill(u + 1, b2, g2, stored[b2])
            f(*args)
        out[0] = (first, out[0])
        out[24] = (ahead, out[24])
        return out

    def exp_steps(u):
        b, g = units[u]
        out = weighted.steps(u, b * NT, 0, g, lambda: v_ready[b])

        def mark(f, args):
            at["b"] = b
            f(*args)
        out[0] = (mark, out[0])
        if g == H // GROUP - 1:
            f, a = out[-1]
            out[-1] = (lambda *args: (f(*args), finish(b)), a)
        return out

    interleave(range(len(units)), maxima, exp_steps, lag=6)
    st.run()


class Experts:

    def __init__(self, st, w1, w2, b1, b2, ready, func, hidden):
        self.st, self.w1, self.w2, self.b1, self.b2 = st, w1, w2, b1, b2
        self.ready, self.func = ready, func
        banks = st.psum("experts", 5)
        self.up_ring = Ring([banks[:, i, :] for i in range(3)])
        self.down_ring = Ring([banks[:, 3 + i, :] for i in range(2)])
        self.hidden = Ring(hidden)
        self.up, self.acted, self.down, self.gated = (st.sem(n) for n in (
            "up", "acted", "down", "gated"))

    def __call__(self, cols, gates, gate_rows, gates_ready, rows_ready, acc, base, base_ready):
        st, nc = self.st, self.st.nc
        slot, bank, free = self.down_ring.take()
        for i in range(4):
            st.pe.wait(*free, rows_ready, self.ready)
            mm = st.pe(nc.tensor.matmul, banks4(bank)[:, i, :], gate_rows(i), self.b2, start=True,
                       stop=True, sig=self.down)
        st.dve.wait(mm, *base_ready)
        v = st.dve(nc.vector.tensor_tensor, acc, banks4(bank), base, ALU.add, sig=self.gated)
        self.down_ring.done[slot] = [v]
        late = []

        def down():
            e, hs = late.pop(0)
            slot, bank, free = self.down_ring.take()
            for i in range(4):
                for c in range(FF // P):
                    hslot, h, a = hs[c]
                    st.pe.wait(*free, a)
                    mm = st.pe(nc.tensor.matmul, banks4(bank)[:, i, :], h[:, i * P:(i + 1) * P],
                               self.w2[:, e, c, :], start=c == 0, stop=c == FF // P - 1, sig=self.down)
            for hslot, _, _ in hs:
                self.hidden.done[hslot] = [mm]
            for i in range(4):
                st.dve.wait(mm, gates_ready, self.last_acc)
                v = st.dve(nc.vector.scalar_tensor_tensor, acc[:, i, :], banks4(bank)[:, i, :],
                           gates(e, i), acc[:, i, :], ALU.mult, ALU.add, sig=self.gated)
            self.last_acc = v
            self.down_ring.done[slot] = [v]

        self.last_acc = v
        for e in range(E2):
            hs = []
            for c in range(FF // P):
                uslot, ub, ufree = self.up_ring.take()
                st.pe.wait(*ufree, self.ready)
                mm = st.pe(nc.tensor.matmul, ub, self.w1[:, e, c * P:(c + 1) * P], cols, start=True,
                           stop=True, sig=self.up)
                hslot, h, hfree = self.hidden.take()
                st.act.wait(mm, self.ready, *hfree)
                a = st.act(nc.scalar.activation, h, ub, self.func, bias=self.b1[:, e, c:c + 1], sig=self.acted)
                self.up_ring.done[uslot] = [a]
                hs.append((hslot, h, a))
            late.append((e, hs))
            if len(late) > 1:
                down()
        down()
        return self.last_acc


def load_experts(st, core, name, small):
    inp = core.inp
    loaded = st.sem("experts_loaded")
    w1 = core.big[:, 0:E2 * FF].rearrange("p (e f) -> p e f", e=E2)
    w2 = core.big[:, E2 * FF:2 * E2 * FF].rearrange("p (e c d) -> p e c d", e=E2, d=C)
    b1, b2 = st.sbuf("b1", [P, E2, FF // P]), st.sbuf("b2", [E2, C])
    for e in range(E2):
        st.load(w1[:, e, :], inp[f"{name}_W1"][e], loaded)
        st.load(w2[:, e, :, :], inp[f"{name}_W2"][e].rearrange("(c p) d -> p c d", p=P), loaded)
    st.load(b1[:, :, :], inp[f"{name}_b1_c"][:, :, :], loaded)
    ready = st.load(b2[:, :], inp[f"{name}_b2"][:, :], loaded)
    return w1, w2, b1, b2, ready


def block_experts(core):
    st = Stage(core, "moe2")
    nc, inp, const, nb = core.nc, core.inp, core.const, core.n_batch
    x, xc, x1 = core.x_tok, core.x_chn, core.x_mid
    n_tiles = nb * NT
    small_banks = st.psum("small", 3)
    ring = Ring([small_banks[:, i, :] for i in range(3)])
    st.routed = st.sem("routed")
    loaded = st.sem("loaded")
    w_router = st.sbuf("w_router", [P, E2])
    st.load(w_router[:, :], inp["L2_ffn_Wg"][:, :], loaded)
    router_bias, _ = broadcast_rows(st, "router_bias", inp["L2_ffn_bg"], E2, loaded)
    g2, _ = broadcast_rows(st, "g2", inp["L2_ffn_g2"], C, loaded)
    be2, small_ready = broadcast_rows(st, "be2", inp["L2_ffn_be2"], C, loaded)
    w1, w2, b1, b2, w_ready = load_experts(st, core, "L2_ffn", None)
    logits, gates = st.sbuf("logits", [P, n_tiles, E2]), st.sbuf("gates", [P, n_tiles, E2])
    total = st.sbuf("total", [P, n_tiles])
    gate_row = st.sbuf("gate_row", [E2, nb * T])
    r_done, sm, ex = st.sem("logits_done"), st.sem("softmax"), st.sem("exp_done")
    v = router(st, ring, w_router[:, :], router_bias[:, :], xc, n_tiles, E2, logits[:, :, :],
               r_done, [small_ready])
    st.dve.wait(v)
    v = st.dve(nc.vector.tensor_reduce, total[:, :], logits[:, :, :], AX.X, ALU.max,
               sig=sm)
    st.dve.wait(v)
    v = st.dve(nc.vector.tensor_tensor, logits[:, :, :], logits[:, :, :], along(total[:, :], E2),
               ALU.subtract, sig=sm)
    st.act.wait(v)
    v = st.act(nc.scalar.activation, logits[:, :, :], logits[:, :, :], ACT.Exp, sig=ex)
    st.dve.wait(v)
    v = st.dve(nc.vector.tensor_reduce, total[:, :], logits[:, :, :], AX.X, ALU.add,
               sig=sm)
    st.dve.wait(v)
    v = st.dve(nc.vector.reciprocal, total[:, :], total[:, :], sig=sm)
    st.dve.wait(v)
    v = st.dve(nc.vector.tensor_tensor, logits[:, :, :], logits[:, :, :], along(total[:, :], E2),
               ALU.mult, sig=sm)
    top = TopTwo(st, n_tiles, E2)
    gates_ready = top(logits[:, :, :], gates[:, :, :], [v])
    rows_ready = gate_rows_of(st, ring, gates, gate_row, n_tiles, E2, [gates_ready])
    hidden = [st.sbuf(f"hidden{i}", [P, BANK]) for i in range(8)]
    experts = Experts(st, w1, w2, b1, b2[:, :], w_ready, ACT.Gelu, [h[:, :] for h in hidden])
    norm, turn = Norm(st), Turn(st, ring)
    affine = st.sem("affine")
    for b in range(nb):
        for n in range(b * NT, (b + 1) * NT, 4):
            v = experts(xc[:, n * P:n * P + BANK], lambda e, i: gates[:, n + i, e:e + 1],
                        lambda i: gate_row[:, (n + i) * P:(n + i + 1) * P], gates_ready, rows_ready,
                        x1[:, n:n + 4, :], x1[:, n:n + 4, :], [])
        tiles = slice(b * NT, (b + 1) * NT)
        v = norm(x1[:, tiles, :], x1[:, tiles, :], [v])
        st.dve.wait(v, small_ready)
        v = st.dve(nc.vector.tensor_tensor, x1[:, tiles, :], x1[:, tiles, :], spread(g2[:, :], NT),
                   ALU.mult, sig=affine)
        st.dve.wait(v)
        v = st.dve(nc.vector.tensor_tensor, x1[:, tiles, :], x1[:, tiles, :], spread(be2[:, :], NT),
                   ALU.add, sig=affine)
        st.dve.wait(v)
        v = st.dve(nc.vector.tensor_tensor, x[:, tiles, :], x[:, tiles, :], x1[:, tiles, :],
                   ALU.add, sig=affine)
        v = norm(x[:, tiles, :], x[:, tiles, :], [v])
        for n in range(b * NT, (b + 1) * NT, 4):
            turn(x[:, n:n + 4, :], xc[:, n * P:n * P + BANK], [v])
    st.run()


WIDE = 64
PAIRS = H // 2


def wide_attention(core):
    st = Stage(core, "wide")
    nc, inp, const, nb = core.nc, core.inp, core.const, core.n_batch
    x, xc = core.x_tok, core.x_chn
    banks = st.psum("p", 8)
    score_ring = Ring([banks[:, 0:2, :], banks[:, 2:4, :]])
    turn_ring = Ring([banks[:, 4, :], banks[:, 5, :]])
    out_ring = Ring([banks[:, 6, :]])
    small_ring = Ring([banks[:, 7, :]])
    loaded = st.sem("loaded")
    wide_w = {n: core.big[:, i * 8 * C:(i + 1) * 8 * C] for i, n in enumerate("qkvo")}
    for n in "qkv":
        st.load(wide_w[n], inp[f"L3_attn_W{n}_t"][:, :], loaded)
    w_o = wide_w["o"].rearrange("p (m c) -> p m c", c=C)
    st.load(w_o, inp["L3_attn_Wo_t"].rearrange("(m p) c -> p m c", p=P), loaded)
    bq, bk = st.sbuf("bq", [P, PAIRS]), st.sbuf("bk", [P, PAIRS])
    st.load(bq[:, :], inp["L3_attn_bq_c"][:, :], loaded)
    st.load(bk[:, :], inp["L3_attn_bk_c"][:, :], loaded)
    scale = st.sbuf("scale", [P, PAIRS])
    two_heads = inp["L3_attn_adaptive_scale_c"]
    for a in range(2):
        st.load(scale[a * WIDE:(a + 1) * WIDE, :], two_heads[a:a + 1, :].broadcast_to([WIDE, PAIRS]), loaded)
    head_rows = st.sbuf("head_rows", [2, P])
    st.load(head_rows[:, :], const["head_rows"][:, :], loaded)
    bv, _ = broadcast_rows(st, "bv", inp["L3_attn_bv"], H * WIDE, loaded)
    bo, _ = broadcast_rows(st, "bo", inp["L3_attn_bo"], C, loaded)
    gamma, _ = broadcast_rows(st, "gamma", inp["L3_attn_gamma"], C, loaded)
    beta, ready = broadcast_rows(st, "beta", inp["L3_attn_beta"], C, loaded)
    st.dve.wait(ready)
    scaled = st.dve(nc.vector.tensor_scalar, scale[:, :], scale[:, :], WIDE ** -0.5, None, ALU.mult, sig=st.sem("scaled"))
    q_pad = [[st.sbuf(f"q_pad{i}{a}", [P, T]) for a in range(2)] for i in range(2)]
    k_chn = [st.sbuf(f"k_chn{i}", [P, T]) for i in range(2)]
    v_tok = [st.sbuf(f"v_tok{i}", [P, NT, C]) for i in range(2)]
    zeroed = st.sem("zeroed")
    for i in range(2):
        for a in range(2):
            other = slice((1 - a) * WIDE, (2 - a) * WIDE)
            zero = st.pool(nc.gpsimd.memset, q_pad[i][a][other, :], 0.0, sig=zeroed)
    weights = Ring([st.sbuf(f"weights{i}", [P, T]) for i in range(3)])
    turned_w = Ring([core.attn_w[:, :].rearrange("p (k q) -> p k q", k=NT),
                      core.big[:, 4 * T:8 * T].rearrange("p (k q) -> p k q", k=NT),
                      st.sbuf("turned_w2", [P, NT, BANK])[:, :, :]])
    att = st.sbuf("att", [P, PAIRS, T])
    neg_max = Ring([st.sbuf(f"neg_max{i}", [P, 1]) for i in range(4)])
    sums = [st.sbuf(f"sums{i}", [P, NT // HALF, 2]) for i in range(2)]
    inv = [st.sbuf(f"inv{i}", [P, NT // HALF, 2]) for i in range(2)]
    inv_row = st.sbuf("inv_row", [2, BANK])
    inv_all = st.sbuf("inv_all", [P, BANK])
    projected, q_kept, k_kept, v_kept = (st.sem(n) for n in ("projected", "q_kept", "k_kept",
                                                             "v_kept"))
    scored, maxed, exped, turned, t_dve, t_act = (st.sem(n) for n in (
        "scored", "maxed", "exped", "turned", "turned_dve", "turned_act"))
    weighted, inverted, row_turned, row_kept, all_mm, all_kept, normed = (st.sem(n) for n in (
        "weighted", "inverted", "row_turned", "row_kept", "all_mm", "all_kept", "normed"))
    units = [(b, m) for b in range(nb) for m in range(PAIRS)]
    used = [[None], [None]]
    att_free = []
    kept_of = {}

    def project(u):
        b, m = units[u]
        i = u % 2
        cols = xc[:, b * T:(b + 1) * T]
        pair = slice(m * P, (m + 1) * P)
        slot, bank, free = score_ring.take()
        for half in range(HALF):
            st.pe.wait(*free, ready)
            mm = st.pe(nc.tensor.matmul, bank[:, half, :], wide_w["q"][:, pair],
                       cols[:, half * BANK:(half + 1) * BANK], start=True, stop=True, sig=projected)
        for a in range(2):
            own = slice(a * WIDE, (a + 1) * WIDE)
            st.dve.wait(mm, scaled, *used[i])
            q = st.dve(nc.vector.tensor_scalar,
                       q_pad[i][a][own, :].rearrange("p (h t) -> p h t", h=HALF), bank[own, :, :],
                       bq[own, m:m + 1], scale[own, m:m + 1], ALU.add, ALU.mult, sig=q_kept)
        score_ring.done[slot] = [q]
        slot, bank, free = score_ring.take()
        for half in range(HALF):
            st.pe.wait(*free)
            mm = st.pe(nc.tensor.matmul, bank[:, half, :], wide_w["k"][:, pair],
                       cols[:, half * BANK:(half + 1) * BANK], start=True, stop=True,
                       sig=projected)
        st.act.wait(mm, ready, *used[i])
        k = st.act(nc.scalar.activation, k_chn[i][:, :].rearrange("p (h t) -> p h t", h=HALF), bank,
                   ACT.Identity, bias=bk[:, m:m + 1], sig=k_kept)
        score_ring.done[slot] = [k]
        slot, bank, free = score_ring.take()
        for n in range(NT):
            st.pe.wait(*free)
            mm = st.pe(nc.tensor.matmul, bank[:, n // 4, (n % 4) * P:(n % 4 + 1) * P],
                       cols[:, n * P:(n + 1) * P], wide_w["v"][:, pair], start=True, stop=True, sig=projected)
        st.dve.wait(mm, *used[i])
        v = st.dve(nc.vector.tensor_tensor, v_tok[i][:, :, :],
                   bank.rearrange("p a (n c) -> p (a n) c", c=C), spread(bv[:, pair], NT), ALU.add, sig=v_kept)
        score_ring.done[slot] = [v]
        kept_of[u] = (q, k, v)

    count = {"copy": 0}

    def score(u, half, a, n):
        i = u % 2
        q, k, v = kept_of[u]
        qn = half * (NT // HALF) + n
        slot, bank, free = score_ring.take()
        for part in range(HALF):
            st.pe.wait(*free, q, k, zero)
            mm = st.pe(nc.tensor.matmul, bank[:, part, :], q_pad[i][a][:, qn * P:(qn + 1) * P],
                       k_chn[i][:, part * BANK:(part + 1) * BANK], start=True, stop=True, sig=scored)
        ms, m1, mfree = neg_max.take()
        st.dve.wait(mm, *mfree)
        mx = st.dve(nc.vector.tensor_reduce, m1[:, :], bank, AX.XY, ALU.max, negate=True, sig=maxed)
        ws, w, wfree = weights.take()
        st.act.wait(mx, *wfree, *sums_free[half % 2])
        e = st.act(nc.scalar.activation, w[:, :].rearrange("p (h t) -> p h t", h=HALF), bank,
                   ACT.Exp, bias=m1[:, 0:1], accum_out=sums[half % 2][:, n, a:a + 1], sig=exped)
        score_ring.done[slot] = [e]
        neg_max.done[ms] = [e]
        return ws, w, e

    sums_free = [[], []]

    def turn_weights(state, a, n, w, ws, e):
        tw, wait = state[a]
        for part in range(2):
            slot, bank, free = turn_ring.take()
            for k in range(4):
                kb = part * 4 + k
                st.pe.wait(*free, e)
                mm = st.pe(nc.tensor.transpose, banks4(bank)[:, k, :], w[:, kb * P:(kb + 1) * P],
                           core.ident[:, :], sig=turned)
            dst = tw[:, part * 4:part * 4 + 4, n * P:(n + 1) * P]
            count["copy"] += 1
            if count["copy"] % 2:
                st.dve.wait(mm, *wait)
                c = st.dve(nc.vector.tensor_copy, dst, banks4(bank), sig=t_dve)
                state["dve"] = c
            else:
                st.act.wait(mm, *wait)
                c = st.act(nc.scalar.copy, dst, banks4(bank), sig=t_act)
                state["act"] = c
            turn_ring.done[slot] = [c]
        weights.done[ws] = [mm]

    def weigh(u, half, state):
        b, m = units[u]
        i = u % 2
        s = half % 2
        oslot, out, ofree = out_ring.take()
        for kb in range(NT):
            for a in range(2):
                own = slice(a * WIDE, (a + 1) * WIDE)
                st.pe.wait(*ofree, state['dve'], state['act'], kept_of[u][2])
                mm = st.pe(nc.tensor.matmul, out[own, :], v_tok[i][:, kb, own],
                           state[a][0][:, kb, :], start=kb == 0, stop=kb == NT - 1, sig=weighted)
        for a in range(2):
            turned_w.done[state["slots"][a]] = [mm]
        used[i] = [mm]
        st.dve.wait(state['e'], *inv_free[s])
        r = st.dve(nc.vector.reciprocal, inv[s][:, :, :], sums[s][:, :, :], sig=inverted)
        sums_free[s] = [r]
        slot, bank, free = small_ring.take()
        for n in range(NT // HALF):
            st.pe.wait(*free, r)
            t = st.pe(nc.tensor.transpose, bank[0:2, n * P:(n + 1) * P], inv[s][:, n, :],
                      core.ident[:, :], sig=row_turned)
        inv_free[s] = [t]
        st.act.wait(t, *row_free)
        row = st.act(nc.scalar.copy, inv_row[:, :], bank[0:2, :], sig=row_kept)
        st.pe.wait(row, ready)
        mm2 = st.pe(nc.tensor.matmul, bank, head_rows[:, :], inv_row[:, :], start=True, stop=True, sig=all_mm)
        row_free[:] = [mm2]
        st.act.wait(mm2, *all_free)
        full = st.act(nc.scalar.copy, inv_all[:, :], bank, sig=all_kept)
        small_ring.done[slot] = [full]
        st.dve.wait(full, mm, *att_free)
        done = st.dve(nc.vector.tensor_tensor, att[:, m, half * BANK:(half + 1) * BANK], out,
                      inv_all[:, :], ALU.mult, sig=normed)
        all_free[:] = [done]
        out_ring.done[oslot] = [done]
        return done

    inv_free, row_free, all_free = [[], []], [], []
    rows, norm, turn = Rows(st, small_ring), Norm(st), Turn(st, turn_ring, "_x")
    affine, resid = st.sem("affine"), st.sem("resid")
    mid = st.sbuf("mid", [P, NT, C])

    def finish(b, done):
        tiles = slice(b * NT, (b + 1) * NT)
        for n in range(0, NT, 4):
            y = rows(lambda k, m: att[:, k, (n + m) * P:(n + m + 1) * P], lambda k: w_o[:, k, :],
                     bo[:, :], x[:, b * NT + n:b * NT + n + 4, :], mid[:, n:n + 4, :], [done],
                     n_k=PAIRS)
        att_free[:] = [y]
        v = norm(mid[:, :, :], mid[:, :, :], [y])
        st.dve.wait(v)
        v = st.dve(nc.vector.tensor_tensor, mid[:, :, :], mid[:, :, :], spread(gamma[:, :], NT),
                   ALU.mult, sig=affine)
        st.dve.wait(v)
        v = st.dve(nc.vector.tensor_tensor, mid[:, :, :], mid[:, :, :], spread(beta[:, :], NT),
                   ALU.add, sig=affine)
        st.dve.wait(v)
        v = st.dve(nc.vector.tensor_tensor, x[:, tiles, :], x[:, tiles, :], mid[:, :, :], ALU.add, sig=affine)
        v = norm(x[:, tiles, :], x[:, tiles, :], [v])
        for n in range(b * NT, (b + 1) * NT, 4):
            turn(x[:, n:n + 4, :], xc[:, n * P:n * P + BANK], [v])

    late, blocks = [], []

    def flush(keep):
        while len(late) > keep:
            state, a, n, w, ws, e, last, u, half = late.pop(0)
            turn_weights(state, a, n, w, ws, e)
            if last:
                state["e"] = e
                blocks.append((u, half, state))

    def flush_blocks():
        while blocks:
            u, half, state = blocks.pop(0)
            done = weigh(u, half, state)
            if half == HALF - 1 and units[u][1] == PAIRS - 1:
                finish(units[u][0], done)

    for u in range(len(units)):
        if u == 0:
            project(0)
        for half in range(HALF):
            state = {"slots": []}
            for a in range(2):
                slot, tw, wait = turned_w.take()
                state["slots"].append(slot)
                state[a] = (tw, wait)
                for n in range(NT // HALF):
                    ws, w, e = score(u, half, a, n)
                    late.append((state, a, n, w, ws, e, a == 1 and n == NT // HALF - 1, u, half))
                    flush(1)
                    flush_blocks()
            if half == 0 and u + 1 < len(units):
                project(u + 1)
    flush(0)
    flush_blocks()
    st.run()


ENTMAX_ITER = 25
GATE_FLOOR = 1e-9


def entmax(st, logits, gates, n_tiles, after):
    nc, n = st.nc, E2
    s = st.sem("entmax")
    xs, diff, power, p = (st.sbuf(f"ent_{i}", [P, n_tiles, n]) for i in ("x", "diff", "power", "p"))
    low, width, mid, f_low, f, keep = (st.sbuf(f"ent_{i}", [P, n_tiles]) for i in (
        "low", "width", "mid", "f_low", "f", "keep"))
    high = st.sbuf("ent_high", [P, n_tiles])

    def dve(method, *args, **kw):
        nonlocal v
        st.dve.wait(v)
        v = st.dve(method, *args, sig=s, **kw)

    def mass(tau, out):
        dve(nc.vector.tensor_tensor, diff[:, :, :], xs[:, :, :], along(tau[:, :], n), ALU.subtract)
        dve(nc.vector.scalar_tensor_tensor, power[:, :, :], diff[:, :, :], 0.0, diff[:, :, :],
            ALU.max, ALU.mult)
        dve(nc.vector.tensor_reduce, out[:, :], power[:, :, :], AX.X, ALU.add)

    v = after
    dve(nc.vector.tensor_scalar, xs[:, :, :], logits, 0.5, None, ALU.mult)
    dve(nc.vector.tensor_reduce, high[:, :], xs[:, :, :], AX.X, ALU.max)
    dve(nc.vector.tensor_scalar, low[:, :], high[:, :], 1.0, None, ALU.subtract)
    dve(nc.vector.tensor_scalar, high[:, :], high[:, :], (1.0 / n) ** 0.5, None, ALU.subtract)
    dve(nc.vector.tensor_tensor, width[:, :], high[:, :], low[:, :], ALU.subtract)
    mass(low, f_low)
    dve(nc.vector.tensor_scalar, f_low[:, :], f_low[:, :], 1.0, None, ALU.subtract)
    for _ in range(ENTMAX_ITER):
        dve(nc.vector.tensor_scalar, width[:, :], width[:, :], 0.5, None, ALU.mult)
        dve(nc.vector.tensor_tensor, mid[:, :], low[:, :], width[:, :], ALU.add)
        mass(mid, f)
        dve(nc.vector.scalar_tensor_tensor, f[:, :], f[:, :], 1.0, f_low[:, :], ALU.subtract,
            ALU.mult)
        dve(nc.vector.tensor_scalar, keep[:, :], f[:, :], 0.0, None, ALU.is_ge)
        dve(nc.vector.copy_predicated, low[:, :], keep[:, :].bitcast(mybir.dt.uint32), mid[:, :])
    mass(mid, f)
    dve(nc.vector.reciprocal, f[:, :], f[:, :])
    dve(nc.vector.tensor_tensor, p[:, :, :], power[:, :, :], along(f[:, :], n), ALU.mult)
    dve(nc.vector.scalar_tensor_tensor, gates, p[:, :, :], GATE_FLOOR, p[:, :, :], ALU.is_gt,
        ALU.mult)
    return v


def entmax_experts(core):
    st = Stage(core, "moe3")
    nc, inp, nb = core.nc, core.inp, core.n_batch
    x, xc, acc = core.x_tok, core.x_chn, core.x_mid
    n_tiles = nb * NT
    small_banks = st.psum("small", 3)
    ring = Ring([small_banks[:, i, :] for i in range(3)])
    st.routed = st.sem("routed")
    loaded = st.sem("loaded")
    w_router = st.sbuf("w_router", [P, E2])
    st.load(w_router[:, :], inp["L3_ffn_Wr"][:, :], loaded)
    router_bias, small_ready = broadcast_rows(st, "router_bias", inp["L3_ffn_br"], E2, loaded)
    w1, w2, b1, b2, w_ready = load_experts(st, core, "L3_ffn", None)
    logits, gates = st.sbuf("logits", [P, n_tiles, E2]), st.sbuf("gates", [P, n_tiles, E2])
    gate_row = st.sbuf("gate_row", [E2, nb * T])
    v = router(st, ring, w_router[:, :], router_bias[:, :], xc, n_tiles, E2, logits[:, :, :],
               st.sem("logits_done"), [small_ready])
    gates_ready = entmax(st, logits[:, :, :], gates[:, :, :], n_tiles, v)
    rows_ready = gate_rows_of(st, ring, gates, gate_row, n_tiles, E2, [gates_ready])
    hidden = [st.sbuf(f"hidden{i}", [P, BANK]) for i in range(8)]
    experts = Experts(st, w1, w2, b1, b2[:, :], w_ready, ACT.Relu, [h[:, :] for h in hidden])
    norm = Norm(st)
    stored = st.sem("stored")
    for b in range(nb):
        for n in range(b * NT, (b + 1) * NT, 4):
            v = experts(xc[:, n * P:n * P + BANK], lambda e, i: gates[:, n + i, e:e + 1],
                        lambda i: gate_row[:, (n + i) * P:(n + i + 1) * P], gates_ready, rows_ready,
                        acc[:, n:n + 4, :], x[:, n:n + 4, :], [])
        tiles = slice(b * NT, (b + 1) * NT)
        v = norm(acc[:, tiles, :], x[:, tiles, :], [v])
    st.run()


def constants():
    bf16 = np.dtype("bfloat16")
    f = np.float32
    c = {"ident": np.eye(P, dtype=f), "ones": np.ones((P, P), f),
         "flip": np.ascontiguousarray(np.eye(P, dtype=f)[::-1])}
    tok_block = np.arange(T) // P
    rows = np.zeros((STACK - STACK_QK, GROUP, T), f)
    for s in range(SPLITS):
        for j in range(NT):
            rows[s * NT + j] = tok_block == j
    rows[STACK_FAR:] = 1.0
    c["key_rows"] = rows.astype(bf16)
    c["zero_rows"] = np.zeros((STACK_FAR, H, T), bf16)
    d = np.arange(ROW) - (P - 1)
    rp = np.maximum(d, 0)
    exact = N_BUCKETS // 2
    big = exact + (np.log(np.maximum(rp, 1).astype(f) / f(exact)) / f(np.log(MAX_DISTANCE / exact))
                   * f(N_BUCKETS - exact)).astype(np.int32)
    bucket = np.where(rp < exact, rp, np.minimum(big, N_BUCKETS - 1))
    hot = np.zeros((N_BUCKETS, 2, ROW), f)
    hot[bucket, 0, np.arange(ROW)] = 1.0
    back = np.arange(ROW)
    at = 2 * P - 1 - back + (P - 1)
    ok = at >= 0
    hot[bucket[np.maximum(at, 0)][ok], 1, back[ok]] = 1.0
    c["bucket_hot"] = hot
    part = np.arange(STACK_FAR) // NT
    key = np.arange(STACK_FAR) % NT
    c["far_level"] = np.stack([part > 0, part > 1], 1).astype(f)
    place = np.zeros((STACK_FAR, 2, NT), f)
    for n in range(NT):
        place[:, 0, n] = n < key
        place[:, 1, n] = n >= key + 2
    c["far_place"] = place
    i = np.arange(P)
    head, chan = i // HD, i % HD
    same = head[:, None] == head[None, :]
    c["same_head"] = same.astype(f)
    v = np.arange(HD)[None, :, None]
    c["pick_v"] = (same[:, None, :] & (chan[:, None, None] == v)).astype(f)
    c["place_v"] = (same[:, None, :] & (chan[None, None, :] == v)).astype(f)
    gate = np.zeros((2 * H, 2, C), f)
    for n in range(2):
        gate[n * H + head, n, i] = 1.0
    c["gate_rows"] = gate
    pair = np.zeros((E1, E1 // 2, P), f)
    for e in range(E1):
        pair[e, e // 2, (e % 2) * I1:(e % 2 + 1) * I1] = 1.0
    c["pair_rows"] = pair
    rotate = np.zeros((P, C), f)
    half = HD // 2
    low = i[chan < half]
    rotate[low + half, low] = -1.0
    rotate[low, low + half] = 1.0
    c["rotate"] = rotate
    freq = f(1.0) / f(10000.0) ** (np.arange(0, HD, 2, dtype=f) / f(HD))
    turn = np.arange(T, dtype=f)[:, None] * freq[None, :].astype(f)
    turn = np.concatenate([turn, turn], axis=-1)[:, chan].T
    c["angle"] = np.stack([np.cos(turn), np.sin(turn)], 1).astype(f)
    c["head_rows"] = (np.arange(2)[:, None] == i[None, :] // WIDE).astype(f)
    for n in (8, E1):
        c[f"ramp{n}"] = np.tile(np.arange(n, 0, -1, dtype=f), (P, 1))
    strip = np.zeros((P, BANK), f)
    strip[:, BANK - P:] = np.where(i[None, :] > i[:, None], f(-1e30), f(0))
    c["causal_strip"] = strip
    c["causal_mask"] = np.where(i[:, None] > i[None, :], f(-1e30), f(0)).astype(bf16)
    return c


def build(nc, inp, const, out, n_batch, upto=99):
    core = Core()
    core.nc, core.inp, core.const, core.n_batch = nc, inp, const, n_batch
    with ExitStack() as ctx:
        def sbuf(name, shape, dtype=F32):
            return ctx.enter_context(nc.sbuf_tensor(name, shape, dtype))

        def dram(name, shape, dtype=F32):
            return nc.dram_tensor(name, shape, dtype, kind="Internal").ap()

        names = iter(range(256))
        core.counts = []
        core.new_count = lambda: Count(ctx.enter_context(nc.semaphore(f"count{next(names)}")))
        core.x_tok = sbuf("x_tok", [P, n_batch * NT, C])
        core.x_chn = sbuf("x_chn", [P, n_batch * T])
        core.x_mid = None
        core.big = sbuf("big", [P, 2 * 4 * T])
        core.attn_w = sbuf("attn_w", [P, 4 * T])
        core.ident, core.ident_bf = sbuf("ident", [P, P]), sbuf("ident_bf", [P, P], BF16)
        core.flip, core.flip_bf = sbuf("flip", [P, P]), sbuf("flip_bf", [P, P], BF16)
        core.ones, core.eps = sbuf("ones", [P, P]), sbuf("eps", [P, 1])
        core.causal_strip = sbuf("causal_strip", [P, BANK])
        core.causal_mask = sbuf("causal_mask", [P, P], BF16)
        core.q_parts = dram("q_parts", (n_batch, SPLITS, C, T), BF16)
        core.k_parts = dram("k_parts", (n_batch, SPLITS, C, T), BF16)
        core.far_bias = dram("far_bias", (STACK_FAR, H, T), BF16)
        core.near_rev = dram("near_rev", (H, ROW))
        core.near_parts = dram("near_parts", (SPLITS, H, ROW), BF16)
        core.bias_stored = Count(ctx.enter_context(nc.semaphore("bias_stored")))

        st = Stage(core, "start")
        loaded, made = Count(ctx.enter_context(nc.semaphore("const_loaded"))), st.sem("made")
        for name, dst in (("ident", core.ident), ("ones", core.ones), ("flip", core.flip),
                          ("causal_strip", core.causal_strip), ("causal_mask", core.causal_mask)):
            t = st.load(dst[:, :], const[name][:, :], loaded)
        core.const_ready = core.ident_ready = t
        core.eps_ready = None
        st.pool(nc.gpsimd.memset, core.eps[:, :], LN_EPS, sig=made)
        st.act.wait(t)
        st.act(nc.scalar.copy, core.ident_bf[:, :], core.ident[:, :], sig=made)
        st.act.wait(t)
        st.act(nc.scalar.copy, core.flip_bf[:, :], core.flip[:, :], sig=made)
        st.run()

        stages = [position_bias, layer0, ternary_ffn, linear_attention, expert_ffn,
                  causal_attention, rotary_attention, block_experts, wide_attention,
                  entmax_experts]
        for n, stage in enumerate(stages):
            if n < upto:
                with ExitStack() as inner:
                    if stage is rotary_attention:
                        mid_ctx = ctx.enter_context(ExitStack())
                        core.x_mid = mid_ctx.enter_context(
                            nc.sbuf_tensor("x_mid", [P, n_batch * NT, C], F32))
                    if stage is entmax_experts:
                        core.x_mid = inner.enter_context(
                            nc.sbuf_tensor("x_sum", [P, n_batch * NT, C], F32))
                    stage(core)
                    if stage is block_experts:
                        mid_ctx.close()
        st = Stage(core, "end")
        stored = st.sem("stored")
        for b in range(n_batch):
            t = st.load(out[b].rearrange("(n p) c -> p n c", p=P),
                        core.x_tok[:, b * NT:(b + 1) * NT, :], stored)
        st.sp.wait(t)
        st.run()


def layout(inputs):
    out = {}
    for name, a in inputs.items():
        if name == "L0_ffn_weight":
            out["L0_ffn_weight_t"] = a.T
        elif name in ("L1_attn_W_qkv", "L1_attn_W_z", "L1_attn_W_b", "L1_attn_W_a",
                      "L1_attn_W_out", "L3_attn_Wq", "L3_attn_Wk", "L3_attn_Wv", "L3_attn_Wo"):
            out[name + "_t"] = a.T
        elif name in ("L2_attn_b_attn", "L3_attn_bq", "L3_attn_bk"):
            out[name + "_c"] = a.reshape(-1, P).T
        elif name == "L3_attn_adaptive_scale":
            out[name + "_c"] = a.reshape(-1, 2).T
        elif name in ("L2_ffn_b1", "L3_ffn_b1"):
            out[name + "_c"] = a.reshape(E2, -1, P).transpose(2, 0, 1)
        else:
            out[name] = a
    return out


def kernel(**inputs):
    from concourse import bacc
    from concourse.bass_utils import run_bass_kernel_spmd

    nc = bacc.Bacc("TRN2", target_bir_lowering=False, num_devices=1)
    n_batch = inputs["L0_attn_hidden_states"].shape[0]
    arrays, inp, const = {}, {}, {}
    for tensors, source, prefix in ((inp, layout(inputs), "in_"), (const, constants(), "const_")):
        for name, a in source.items():
            a = np.ascontiguousarray(a)
            arrays[prefix + name] = a
            tensors[name] = nc.dram_tensor(prefix + name, a.shape, mybir.dt.from_np(a.dtype),
                                           kind="ExternalInput").ap()
    out = nc.dram_tensor("out", (n_batch, T, C), F32, kind="ExternalOutput").ap()
    build(nc, inp, const, out, n_batch)
    r = run_bass_kernel_spmd(nc, [arrays], core_ids=[0])
    return r.results[0]["out"]
```

```python
from contextlib import ExitStack

import numpy as np
import concourse.bass as bass
from concourse import mybir

P = 128
T = 1024
C = 128
H = 16
NT = T // P
BANK = 512
HALF = T // BANK
LN_EPS = 1e-5

F32 = mybir.dt.float32
BF16 = mybir.dt.bfloat16
ALU = mybir.AluOpType
ACT = mybir.ActivationFunctionType
AX = mybir.AxisListType

SPLITS = 3
HD = C // H
STACK_QK = SPLITS * SPLITS * HD
STACK_FAR = SPLITS * NT
ROW_MAX = STACK_QK + STACK_FAR
STACK = ROW_MAX + 2
GROUP = 4
NEAR = 2 * P


class Count:

    def __init__(self, handle):
        self.handle, self.value, self.start = handle, 0, 0

    def at(self, n):
        return (self, self.start + n) if n > 0 else None


class Lane:

    def __init__(self):
        self.items, self.passed = [], {}

    def wait(self, *marks):
        for mark in marks:
            if mark is not None and self.passed.get(mark[0], 0) < mark[1]:
                self.passed[mark[0]] = mark[1]
                self.items.append((mark[0].handle, mark[1]))

    def __call__(self, method, *args, sig=None, step=1, **kw):
        self.items.append((method, args, kw, sig and sig.handle, step))
        if sig is None:
            return None
        sig.value += step
        return sig, sig.value

    def issue(self, engine):
        for item in self.items:
            if len(item) == 2:
                engine.wait_ge(*item)
                continue
            method, args, kw, sig, step = item
            instruction = method(*args, **kw)
            if sig is not None:
                instruction.then_inc(sig, step)


class Ring:

    def __init__(self, buffers):
        self.buffers, self.done, self.at = buffers, [[] for _ in buffers], -1

    def take(self):
        self.at = (self.at + 1) % len(self.buffers)
        return self.at, self.buffers[self.at], self.done[self.at]


class Core:
    pass


class Stage:

    def __init__(self, core, name):
        self.core, self.name, self.nc, self.ctx = core, name, core.nc, ExitStack()
        self.pe, self.act, self.dve, self.pool, self.sp = (Lane() for _ in range(5))
        self.counts = []

    def sbuf(self, name, shape, dtype=F32):
        return self.ctx.enter_context(self.nc.sbuf_tensor(f"{self.name}_{name}", shape, dtype))

    def psum(self, name, n):
        return self.ctx.enter_context(self.nc.psum_tensor(f"{self.name}_{name}", [P, n, BANK], F32))

    def sem(self, name):
        count = self.core.counts.pop() if self.core.counts else self.core.new_count()
        count.start = count.value
        self.counts.append(count)
        return count

    def load(self, out, in_, count):
        return self.sp(self.nc.sync.dma_start, out, in_, sig=count, step=16)

    def run(self):
        nc = self.nc
        with nc.Block() as block:
            @block.tensor
            def _(e):
                self.pe.issue(e)

            @block.scalar
            def _(e):
                self.act.issue(e)

            @block.vector
            def _(e):
                self.dve.issue(e)

            @block.gpsimd
            def _(e):
                self.pool.issue(e)

            @block.sync
            def _(e):
                self.sp.issue(e)
        self.core.counts += reversed(self.counts)
        self.ctx.close()


def banks4(bank):
    return bank.rearrange("p (n c) -> p n c", c=C)


def spread(ap, n):
    return ap[:, None, :].broadcast_to([ap.shape[0], n, ap.shape[1]])


def along(ap, n):
    return ap[:, :, None].broadcast_to([ap.shape[0], ap.shape[1], n])


class Norm:

    def __init__(self, st, tag=""):
        self.st = st
        self.stats = st.sbuf(f"stats{tag}", [P, NT, 6])
        self.mv = st.sbuf(f"mv{tag}", [P, NT, 2])
        self.std = st.sbuf(f"std{tag}", [P, NT])
        self.rstd = st.sbuf(f"rstd{tag}", [P, NT])
        self.n_stats = st.sem(f"n_stats{tag}")
        self.n_mv = st.sem(f"n_mv{tag}")
        self.n_std = st.sem(f"n_std{tag}")
        self.n_rstd = st.sem(f"n_rstd{tag}")
        self.n_out = st.sem(f"n_out{tag}")
        self.last = None

    def __call__(self, src, dst, after):
        st, nc, n = self.st, self.st.nc, src.shape[1]
        for i in range(n):
            st.dve.wait(*after, self.last)
            seen = st.dve(nc.vector.bn_stats, self.stats[:, i, :], src[:, i, :], sig=self.n_stats)
        for i in range(n):
            st.dve.wait((seen[0], seen[1] - n + 1 + i))
            mv = st.dve(nc.vector.bn_aggr, self.mv[:, i, :], self.stats[:, i, :], sig=self.n_mv)
        st.act.wait(mv, st.core.eps_ready)
        std = st.act(nc.scalar.activation, self.std[:, 0:n], self.mv[:, 0:n, 1], ACT.Sqrt,
                     bias=st.core.eps[:, 0:1], sig=self.n_std)
        st.dve.wait(std)
        rstd = st.dve(nc.vector.reciprocal, self.rstd[:, 0:n], self.std[:, 0:n],
                      sig=self.n_rstd)
        for i in range(n):
            st.dve.wait(rstd)
            out = st.dve(nc.vector.tensor_scalar, dst[:, i, :], src[:, i, :], self.mv[:, i, 0:1],
                         self.rstd[:, i:i + 1], ALU.subtract, ALU.mult,
                         sig=self.n_out)
        self.last = out
        return out


class Turn:

    def __init__(self, st, banks, tag=""):
        self.st, self.banks = st, banks
        self.turned = st.sem(f"turned{tag}")
        self.kept = st.sem(f"kept{tag}")

    def __call__(self, src, dst, after, copy_on="act"):
        st, nc = self.st, self.st.nc
        slot, bank, free = self.banks.take()
        for i in range(4):
            st.pe.wait(*after, *free, st.core.ident_ready)
            t = st.pe(nc.tensor.transpose, banks4(bank)[:, i, :], src[:, i, :], st.core.ident[:, :], sig=self.turned if i == 3 else None)
        if copy_on == "act":
            st.act.wait(t)
            kept = st.act(nc.scalar.copy, dst, bank, sig=self.kept)
        else:
            st.dve.wait(t)
            kept = st.dve(nc.vector.tensor_copy, dst, bank, sig=self.kept)
        self.banks.done[slot] = [kept]
        return kept


class Parts:

    def __init__(self, st, tag):
        self.st = st
        self.rest = st.sbuf(f"rest_{tag}", [P, T])
        self.parts = st.sbuf(f"parts_{tag}", [P, SPLITS, T], BF16)
        self.cast = st.sem(f"cast_{tag}")
        self.less = st.sem(f"less_{tag}")
        self.stored = st.sem(f"stored_{tag}")
        self.last = self.last_less = None

    def __call__(self, value, dram, after):
        st, nc = self.st, self.st.nc
        src, ready = value, after
        for s in range(SPLITS):
            st.act.wait(*ready, self.last)
            cast = st.act(nc.scalar.copy, self.parts[:, s, :], src,
                          sig=self.cast)
            if s < SPLITS - 1:
                st.dve.wait(cast)
                less = st.dve(nc.vector.tensor_tensor, self.rest[:, :], src, self.parts[:, s, :],
                              ALU.subtract, sig=self.less)
                src, ready = self.rest[:, :], [less]
                if s == 0:
                    self.last_less = less
        st.sp.wait(cast)
        self.last = st.load(dram.rearrange("s c t -> c s t"), self.parts[:, :, :], self.stored)
        return self.last


class SmallHeads:

    SLOTS = 3

    def __init__(self, st, per_unit, q_dram, k_dram, far_dram, near=None, strip=None, causal=False):
        self.st, self.q_dram, self.k_dram, self.far_dram = st, q_dram, k_dram, far_dram
        self.near, self.strip, self.causal = near, strip, causal
        self.scored, self.per_unit = st.sem("scored"), per_unit
        n = self.SLOTS
        self.q_stack = [st.sbuf(f"q_stack{i}", [STACK, GROUP, T], BF16) for i in range(n)]
        self.k_stack = [st.sbuf(f"k_stack{i}", [STACK, GROUP, T], BF16) for i in range(n)]
        self.loaded = [st.sem(f"stack_loaded{i}") for i in range(n)]
        self.max_row = [st.sem(f"max_row{i}") for i in range(n)]
        self.ready = [None] * n
        self.row_ready = [None] * n
        self.max_parts = st.sbuf("max_parts", [P, GROUP, NT, HALF])
        self.neg_max = st.sbuf("neg_max", [P, GROUP * NT])
        self.max_hi = st.sbuf("max_hi", [GROUP * NT, P], BF16)
        self.max_lo = st.sbuf("max_lo", [GROUP * NT, P], BF16)
        self.fixed = st.sem("fixed_rows")
        self.max_scored = st.sem("max_scored")
        self.maxed = st.sem("maxed")
        self.joined = st.sem("max_joined")
        self.turned = st.sem("max_turned")
        self.hi_kept = st.sem("max_hi_kept")
        self.lo_kept = st.sem("max_lo_kept")
        self.last_joined = self.last_turned = self.hi = self.lo = self.sent = None
        for i in range(n):
            self.fixed_ready = st.load(self.k_stack[i][STACK_QK:STACK, :, :],
                                       st.core.const["key_rows"][:, :, :], self.fixed)
        self.last_joined = st.dve(st.nc.vector.memset, self.max_parts[:, :, :, :], -3e38,
                                  sig=self.joined)

    def fill(self, u, b, g, stored):
        st, i = self.st, u % self.SLOTS
        hs = slice(g * GROUP * HD, (g + 1) * GROUP * HD)
        st.sp.wait(self.scored.at(self.per_unit * (u - self.SLOTS + 1)), *stored)
        for s in range(SPLITS):
            q = self.q_dram[b, s, hs, :].rearrange("(h d) t -> d h t", d=HD)
            for r in range(SPLITS):
                row = (s * SPLITS + r) * HD
                k = self.k_dram[b, r, hs, :].rearrange("(h d) t -> d h t", d=HD)
                st.load(self.q_stack[i][row:row + HD, :, :], q, self.loaded[i])
                st.load(self.k_stack[i][row:row + HD, :, :], k, self.loaded[i])
        far = self.far_dram[:, g * GROUP:(g + 1) * GROUP, :]
        self.ready[i] = st.load(self.q_stack[i][STACK_QK:ROW_MAX, :, :], far, self.loaded[i])

    def maxima(self, u, ring):
        st, nc, i = self.st, self.st.nc, u % self.SLOTS
        q, k = self.q_stack[i], self.k_stack[i]

        def tile(j, n, half):
            width = min(BANK, (n + 1) * P - half * BANK) if self.causal else BANK
            slot, bank, free = ring.take()
            st.pe.wait(*free, self.ready[i], self.fixed_ready)
            scored = st.pe(nc.tensor.matmul, bank[:, 0:width], q[0:ROW_MAX, j, n * P:(n + 1) * P],
                           k[0:ROW_MAX, j, half * BANK:half * BANK + width], start=True, stop=True,
                           sig=self.max_scored)
            out = self.max_parts[:, j, n, half:half + 1]
            wait = [scored, self.last_joined]
            bias = None
            if self.strip is not None and n - 1 <= half * (BANK // P) + BANK // P - 1 \
                    and n >= half * (BANK // P):
                bias, more = self.strip(u, j, n, half)
                wait += more
            elif self.causal and half == n // (BANK // P):
                bias = st.core.causal_strip[:, BANK - width:BANK]
                wait.append(st.core.const_ready)
            if bias is None:
                st.dve.wait(*wait)
                maxed = st.dve(nc.vector.tensor_reduce, out, bank[:, 0:width], AX.X, ALU.max, sig=self.maxed)
            else:
                st.dve.wait(*wait)
                maxed = st.dve(nc.vector.tensor_tensor_reduce, bank[:, 0:width], bank[:, 0:width],
                               bias, 1.0, -3e38, ALU.add, ALU.max, out,
                               sig=self.maxed)
            ring.done[slot] = [maxed]
            self.last_maxed = maxed

        def join():
            st.dve.wait(self.last_maxed, self.last_turned)
            joined = st.dve(nc.vector.tensor_reduce, self.neg_max[:, :],
                            self.max_parts[:, :, :, :].rearrange("p j n h -> p (j n) h"), AX.X,
                            ALU.max, negate=True,
                            sig=self.joined)
            self.last_joined = joined
            slot, bank, free = ring.take()
            st.pe.wait(*free, joined)
            turned = st.pe(nc.tensor.transpose, bank[0:GROUP * NT, 0:P], self.neg_max[:, :],
                           st.core.ident[:, :], sig=self.turned)
            self.last_turned = turned
            st.dve.wait(turned, self.sent)
            hi = st.dve(nc.vector.tensor_copy, self.max_hi[:, :], bank[0:GROUP * NT, 0:P], sig=self.hi_kept)
            st.dve.wait(hi)
            lo = st.dve(nc.vector.tensor_tensor, self.max_lo[:, :], bank[0:GROUP * NT, 0:P],
                        self.max_hi[:, :], ALU.subtract, sig=self.lo_kept)
            ring.done[slot] = [lo]
            for row, part in ((ROW_MAX, self.max_hi), (ROW_MAX + 1, self.max_lo)):
                st.sp.wait(lo)
                self.sent = st.load(
                    q[row:row + 1, :, :].rearrange("o j (n t) -> o (j n) t", t=P),
                    part[:, :], self.max_row[i])
            self.row_ready[i] = self.sent

        steps = []
        for j in range(GROUP):
            for n in range(NT):
                for half in range(HALF):
                    if not self.causal or half * BANK < (n + 1) * P:
                        steps.append((tile, (j, n, half)))
        f, a = steps[-1]
        steps[-1] = (lambda *args: (tile(*args), join()), a)
        return steps


def interleave(units, maxima, exps, lag):
    m_steps = [step for u in units for step in maxima(u)]
    per_m = len(m_steps) // len(units)
    e_steps = [(u, step) for u in units for step in exps(u)]
    per_e = len(e_steps) // len(units)
    at = 0
    for m, (f, args) in enumerate(m_steps):
        f(*args)
        while at < len(e_steps) and (at + per_e + lag) * per_m <= (m + 1) * per_e:
            f, args = e_steps[at][1]
            f(*args)
            at += 1
    for _, (f, args) in e_steps[at:]:
        f(*args)


def project_small(st, ring, w, bias, scale, out, x_chn, done, w_ready, extra=()):
    nc = st.nc
    slot, banks, free = ring.take()
    for half in range(HALF):
        st.pe.wait(*free, *w_ready)
        mm = st.pe(nc.tensor.matmul, banks[:, half, :], w, x_chn[:, half * BANK:(half + 1) * BANK],
                   start=True, stop=True,
                   sig=st.projected if half == HALF - 1 else None)
    st.dve.wait(mm, *extra)
    kept = st.dve(nc.vector.tensor_scalar, out.rearrange("p (a b) -> p a b", a=HALF), banks, bias,
                  scale, ALU.add, ALU.mult, sig=done)
    ring.done[slot] = [kept]
    return kept


def values_small(st, ring, w, bias, out, x_chn, done, w_ready, extra=()):
    nc = st.nc
    slot, banks, free = ring.take()
    for n in range(NT):
        st.pe.wait(*free, *w_ready)
        mm = st.pe(nc.tensor.matmul, banks[:, n // 4, (n % 4) * C:(n % 4 + 1) * C],
                   x_chn[:, n * P:(n + 1) * P], w, start=True, stop=True,
                   sig=st.projected if n == NT - 1 else None)
    st.dve.wait(mm, *extra)
    kept = st.dve(nc.vector.tensor_tensor, out, banks.rearrange("p a (n c) -> p (a n) c", c=C),
                  spread(bias, NT), ALU.add, sig=done)
    ring.done[slot] = [kept]
    return kept


class Weighted:

    W = 32

    def __init__(self, st, heads, score_ring, out_ring, small_ring, exps, v_tok, ctx):
        self.st, self.heads, self.v_tok, self.ctx = st, heads, v_tok, ctx
        self.score_ring, self.out_ring, self.small_ring = score_ring, out_ring, small_ring
        self.exps, self.n_tile, self.n_half = exps, 0, 0
        self.v_one = [st.sbuf(f"v_one{i}", [P, NT, GROUP, self.W]) for i in range(2)]
        self.out_chn = [st.sbuf(f"out_chn{i}", [P, BANK]) for i in range(2)]
        self.r_sum = st.sbuf("r_sum", [P, 4 * GROUP])
        self.v_filled = st.sem("v_filled")
        self.scored = heads.scored
        self.exped = st.sem("exped")
        self.weighted = st.sem("weighted")
        self.kept = st.sem("out_kept")
        self.turned = st.sem("out_turned")
        self.inverted = st.sem("sum_inverted")
        self.context = st.sem("context")
        self.per_unit = HALF * NT * 2
        nc = st.nc
        for i in range(2):
            z = st.pool(nc.gpsimd.memset, self.v_one[i][:, :, :, :], 0.0, sig=self.v_filled)
            st.pool.wait(z)
            z = st.pool(nc.gpsimd.memset, self.v_one[i][:, :, :, HD:HD + 1], 1.0,
                        sig=self.v_filled)
        self.zeroed = z

    def steps(self, u, v_at, c_at, g, v_ready):
        st, nc, heads = self.st, self.st.nc, self.heads
        i, vs = u % heads.SLOTS, u % 2
        q, k, v = heads.q_stack[i], heads.k_stack[i], self.v_one[vs]
        pending = []

        def fill_values():
            st.pool.wait(self.zeroed, self.weighted.at(self.per_unit * (u - 1)), v_ready())
            self.filled = st.pool(
                nc.gpsimd.tensor_copy, v[:, :, :, 0:HD],
                self.v_tok()[:, v_at:v_at + NT, g * GROUP * HD:(g + 1) * GROUP * HD]
                .rearrange("p n (j d) -> p n j d", d=HD), sig=self.v_filled)

        def scores(half, kb, pair):
            if half == 0 and kb == 0 and pair == 0:
                fill_values()
            n = self.n_tile
            self.n_tile += 1
            banks = self.score_ring.buffers[n % 2]
            lo = max(kb * P, half * BANK)
            hi = min(kb * P + NEAR, (half + 1) * BANK)
            near = heads.near is not None and lo < hi
            st.pe.wait(heads.row_ready[i], heads.ready[i])
            st.pe.wait(self.exped.at(n - 1), *(self.score_ring.done[n % 2] if n < 2 else ()))
            for a in range(2):
                j = 2 * pair + a
                st.pe(nc.tensor.matmul, banks[:, a, :], k[0:STACK, j, kb * P:(kb + 1) * P],
                      q[0:STACK, j, half * BANK:(half + 1) * BANK], start=True, stop=not near,
                      sig=None if near or a == 0 else self.scored)
                if near:
                    bias, loaded = heads.near(u, j, lo - kb * P, hi - kb * P)
                    st.pe.wait(loaded)
                    for s in range(SPLITS):
                        last = s == SPLITS - 1
                        st.pe(nc.tensor.matmul, banks[:, a, lo - half * BANK:hi - half * BANK],
                              st.core.flip_bf[:, :], bias[s], start=False, stop=last,
                              sig=self.scored if last and a == 1 else None)
            st.act.wait(self.scored.at(n + 1), self.weighted.at(n + 1 - len(self.exps)))
            st.act(nc.scalar.activation, self.exps[n % len(self.exps)], banks, ACT.Exp,
                   sig=self.exped)
            pending.append((kb, pair, n))
            if pair == 1 and kb > 0:
                weigh()
            if pair == 1 and kb == NT - 1:
                weigh()
                finish(half)

        def weigh():
            m = self.n_half
            out = self.out_ring.buffers[m % len(self.out_ring.buffers)]
            st.pe.wait(self.kept.at(m + 1 - len(self.out_ring.buffers)), self.filled)
            for _ in range(2):
                kb, pair, n = pending.pop(0)
                st.pe.wait(self.exped.at(n + 1))
                for a in range(2):
                    j = 2 * pair + a
                    st.pe(nc.tensor.matmul, out[self.W * j:self.W * (j + 1), :],
                          v[:, kb, j, :], self.exps[n % len(self.exps)][:, a, :], start=kb == 0,
                          stop=kb == NT - 1, sig=self.weighted if a == 1 else None)

        def finish(half):
            m = self.n_half
            self.n_half += 1
            out, chn = self.out_ring.buffers[m % len(self.out_ring.buffers)], self.out_chn[m % 2]
            st.dve.wait(self.weighted.at(NT * 2 * (m + 1)), self.turned.at(m - 1))
            st.dve(nc.vector.tensor_copy, chn[:, :], out, sig=self.kept)
            tslot, bank, emptied = self.small_ring.take()
            st.pe.wait(*emptied)
            st.pe.wait(self.kept.at(m + 1))
            for n in range(4):
                st.pe(nc.tensor.transpose, banks4(bank)[:, n, :], chn[:, n * P:(n + 1) * P],
                      st.core.ident[:, :], sig=self.turned if n == 3 else None)
            rows = bank.rearrange("p (m w) -> p m w", w=self.W)
            st.dve.wait(self.turned.at(m + 1), self.context.at(4 * m))
            st.dve(nc.vector.reciprocal, self.r_sum[:, :], rows[:, :, HD], sig=self.inverted)
            at = c_at + half * (BANK // P)
            dst = self.ctx()[:, at:at + 4, g * GROUP * HD:(g + 1) * GROUP * HD]
            st.dve.wait(self.inverted.at(m + 1))
            for n in range(4):
                st.dve(nc.vector.tensor_tensor, dst[:, n, :].rearrange("p (j d) -> p j d", d=HD),
                       rows[:, n * GROUP:(n + 1) * GROUP, 0:HD],
                       along(self.r_sum[:, n * GROUP:(n + 1) * GROUP], HD), ALU.mult,
                       sig=self.context)
            self.small_ring.done[tslot] = [self.context.at(4 * (m + 1))]

        return [(scores, (half, kb, pair)) for half in range(HALF) for kb in range(NT)
                for pair in range(2)]


class Rows:

    def __init__(self, st, ring, tag=""):
        self.st, self.ring = st, ring
        self.multiplied = st.sem(f"rows_multiplied{tag}")
        self.added = st.sem(f"rows_added{tag}")

    def __call__(self, chn, w, bias, residual, out, after, n_k=1):
        st, nc = self.st, self.st.nc
        slot, bank, free = self.ring.take()
        tiles = banks4(bank)
        for n in range(4):
            for k in range(n_k):
                st.pe.wait(*free, *after)
                mm = st.pe(nc.tensor.matmul, tiles[:, n, :], chn(k, n), w(k), start=k == 0,
                           stop=k == n_k - 1,
                           sig=self.multiplied if n == 3 and k == n_k - 1 else None)
        st.dve.wait(mm, *after)
        added = st.dve(nc.vector.tensor_tensor, out, tiles, residual, ALU.add,
                       sig=self.added)
        self.ring.done[slot] = [added]
        if bias is not None:
            st.dve.wait(added)
            added = st.dve(nc.vector.tensor_tensor, out, out, spread(bias, 4), ALU.add, sig=self.added)
        return added


N_BUCKETS = 32
MAX_DISTANCE = 64
BIAS_SCALE = 8.0
ROW = 3 * P


def position_bias(core):
    st = Stage(core, "bias")
    nc, const = core.nc, core.const
    ring = st.psum("p", 2)
    table = st.sbuf("table", [N_BUCKETS, H])
    hot = st.sbuf("hot", [N_BUCKETS, 2, ROW])
    level = st.sbuf("level", [STACK_FAR, 2])
    place = st.sbuf("place", [STACK_FAR, 2, NT])
    ends = st.sbuf("ends", [STACK_FAR, 2, H])
    part = st.sbuf("part", [STACK_FAR, 2, H], BF16)
    by_block = st.sbuf("by_block", [STACK_FAR, 2, H, NT])
    far_small = st.sbuf("far_small", [STACK_FAR, H, NT])
    far = st.sbuf("far", [STACK_FAR, H, T], BF16)
    near = st.sbuf("near", [H, 2, ROW])
    near_part = st.sbuf("near_part", [H, SPLITS, ROW], BF16)
    loaded, done, chain = st.sem("loaded"), st.sem("multiplied"), st.sem("chain")
    a_chain, stored = st.sem("a_chain"), core.bias_stored
    st.load(table[:, :], core.inp["L0_attn_rel_bias"][:, :], loaded)
    st.load(hot[:, :, :], const["bucket_hot"][:, :, :], loaded)
    st.load(level[:, :], const["far_level"][:, :], loaded)
    st.load(place[:, :, :], const["far_place"][:, :, :], loaded)
    rel = core.inp["L0_attn_rel_bias"]
    for e, row in enumerate((0, N_BUCKETS - 1)):
        t = st.load(ends[:, e, :], rel[row:row + 1, :].broadcast_to([STACK_FAR, H]), loaded)
    for e in range(2):
        st.pe.wait(t)
        mm = st.pe(nc.tensor.matmul, ring[0:H, e, 0:ROW], table[:, :], hot[:, e, :], start=True,
                   stop=True, sig=done)
    st.dve.wait(mm)
    v = st.dve(nc.vector.tensor_scalar, near[:, :, :], ring[0:H, :, 0:ROW], BIAS_SCALE, None,
               ALU.mult, sig=chain)
    st.sp.wait(v)
    st.load(core.near_rev[:, :], near[:, 1, :], stored)
    for s in range(SPLITS):
        st.dve.wait(v)
        v = st.dve(nc.vector.tensor_copy, near_part[:, s, :], near[:, 0, :], sig=chain)
        if s < SPLITS - 1:
            st.dve.wait(v)
            v = st.dve(nc.vector.tensor_tensor, near[:, 0, :], near[:, 0, :], near_part[:, s, :],
                       ALU.subtract, sig=chain)
    st.sp.wait(v)
    st.load(core.near_parts.rearrange("s h x -> h s x"), near_part[:, :, :], stored)
    st.dve.wait(t, v)
    v = st.dve(nc.vector.tensor_scalar, ends[:, :, :], ends[:, :, :], BIAS_SCALE, None, ALU.mult, sig=chain)
    for s in range(SPLITS - 1):
        st.dve.wait(v)
        v = st.dve(nc.vector.tensor_scalar, part[:, :, :], ends[:, :, :], level[:, s:s + 1], None,
                   ALU.mult, sig=chain)
        st.dve.wait(v)
        v = st.dve(nc.vector.tensor_tensor, ends[:, :, :], ends[:, :, :], part[:, :, :],
                   ALU.subtract, sig=chain)
    for e in range(2):
        st.dve.wait(v)
        v = st.dve(nc.vector.tensor_tensor, by_block[:, e, :, :], along(ends[:, e, :], NT),
                   spread(place[:, e, :], H), ALU.mult, sig=chain)
    st.dve.wait(v)
    v = st.dve(nc.vector.tensor_tensor, far_small[:, :, :], by_block[:, 0, :, :],
               by_block[:, 1, :, :], ALU.add, sig=chain)
    for n in range(2):
        hs = slice(n * H // 2, (n + 1) * H // 2)
        dst = far[:, hs, :].rearrange("p h (n t) -> p (h n) t", t=P)
        src = along(far_small[:, hs, :].rearrange("p h n -> p (h n)"), P)
        if n:
            st.dve.wait(v)
            f = st.dve(nc.vector.tensor_copy, dst, src, sig=chain)
        else:
            st.act.wait(v)
            f = st.act(nc.scalar.copy, dst, src, sig=a_chain)
        st.sp.wait(f)
        t = st.load(core.far_bias[:, hs, :], far[:, hs, :], stored)
    core.bias_ready = t
    st.sp.wait(t)
    st.run()


def broadcast_rows(st, name, src, n, count, lane=None):
    out = st.sbuf(name, [P, n])
    t = st.load(out[:, :], src.rearrange("(o n) -> o n", o=1).broadcast_to([P, n]), count)
    return out, t


def column(st, name, src, count):
    out = st.sbuf(name, [P, 1])
    t = st.load(out[:, :], src.rearrange("(p o) -> p o", o=1), count)
    return out, t


def near_window(handle, row):
    ap = handle[row]
    return bass.AP(tensor=ap.tensor, offset=ap.offset, ap=[[1, P], [ROW, GROUP], [1, NEAR]])


def layer0(core):
    st = Stage(core, "l0")
    nc, inp, const = core.nc, core.inp, core.const
    nb = core.n_batch
    score_banks, small_banks, out_banks = st.psum("score", 4), st.psum("small", 3), st.psum("out", 1)
    score_ring = Ring([score_banks[:, 0:2, :], score_banks[:, 2:4, :]])
    small_ring = Ring([small_banks[:, i, :] for i in range(3)])
    out_ring = Ring([out_banks[:, 0, :]])
    st.projected = st.sem("projected")
    w_loaded = st.sem("w_loaded")
    w = {}
    for n in "qkvo":
        w[n] = st.sbuf(f"w{n}", [P, C])
        st.load(w[n][:, :], inp[f"L0_attn_W{n}"][:, :], w_loaded)
    bq, _ = column(st, "bq", inp["L0_attn_bq"], w_loaded)
    bk, _ = column(st, "bk", inp["L0_attn_bk"], w_loaded)
    bv, _ = broadcast_rows(st, "bv", inp["L0_attn_bv"], C, w_loaded)
    bo, w_ready = broadcast_rows(st, "bo", inp["L0_attn_bo"], C, w_loaded)
    x, xc = core.x_tok, core.x_chn
    x_loaded = [st.sem(f"x_loaded{b}") for b in range(nb)]
    turn = Turn(st, small_ring)
    x_ready = []
    for b in range(nb):
        t = st.load(x[:, b * NT:(b + 1) * NT, :],
                    inp["L0_attn_hidden_states"][b].rearrange("(n p) c -> p n c", p=P), x_loaded[b])
        for n in range(b * NT, (b + 1) * NT, 4):
            t2 = turn(x[:, n:n + 4, :], xc[:, n * P:n * P + BANK], [t])
        x_ready.append(t2)
    heads = SmallHeads(st, HALF * NT * 2, core.q_parts, core.k_parts, core.far_bias,
                       near=lambda u, j, lo, hi: near_of(u, j, lo, hi),
                       strip=lambda u, j, n, half: strip_of(u, j, n, half))
    v_tok, ctx_tok = core.big[:, 0:nb * T], core.big[:, nb * T:2 * nb * T]
    v_tok = v_tok.rearrange("p (n c) -> p n c", c=C)
    ctx_tok = ctx_tok.rearrange("p (n c) -> p n c", c=C)
    q_done, k_done, v_done = st.sem("q_done"), st.sem("k_done"), st.sem("v_done")
    split_q, split_k = Parts(st, "q"), Parts(st, "k")
    value = {n: st.sbuf(f"value_{n}", [P, T]) for n in "qk"}
    scale = 1.0 / np.sqrt(HD)
    stored, v_ready = [], []
    for b in range(nb):
        cols = xc[:, b * T:(b + 1) * T]
        wait = [w_ready, x_ready[b]]
        q = project_small(st, score_ring, w["q"][:, :], bq[:, 0:1], float(scale), value["q"][:, :],
                          cols, q_done, wait, [split_q.last_less])
        s1 = split_q(value["q"][:, :], core.q_parts[b], [q])
        k = project_small(st, score_ring, w["k"][:, :], bk[:, 0:1], 1.0, value["k"][:, :], cols,
                          k_done, wait, [split_k.last_less])
        s2 = split_k(value["k"][:, :], core.k_parts[b], [k])
        stored.append([s1, s2])
        v_ready.append(values_small(st, score_ring, w["v"][:, :], bv[:, :],
                                    v_tok[:, b * NT:(b + 1) * NT, :], cols, v_done, wait))
    strip = core.attn_w[:, 0:GROUP * T].rearrange("p (j x) -> p j x", x=T)
    strip_at = 3 * P
    near = [st.sbuf(f"near{i}", [P, SPLITS, GROUP, NEAR], BF16) for i in range(2)]
    strip_zero, strip_loaded = st.sem("strip_zero"), st.sem("strip_loaded")
    strip_flipped, strip_kept = st.sem("strip_flipped"), st.sem("strip_kept")
    near_loaded = [st.sem(f"near_loaded{i}") for i in range(2)]
    zero = st.pool(nc.gpsimd.memset, strip, 0.0, sig=strip_zero)
    units = [(g, b) for g in range(H // GROUP) for b in range(nb)]
    near_ready = {}

    def load_strip(g):
        raw = value["q"]
        st.sp.wait(stored[-1][0], split_q.last_less, strip_flipped.at(HALF * g))
        raw_ready = st.load(raw[:, :].rearrange("p (j x) -> p j x", x=NEAR),
                            near_window(core.near_rev, slice(g * GROUP, (g + 1) * GROUP)),
                            strip_loaded)
        for half in range(HALF):
            slot, bank, emptied = small_ring.take()
            st.pe.wait(*emptied, raw_ready)
            st.pe(nc.tensor.matmul, bank, core.flip[:, :], raw[:, half * BANK:(half + 1) * BANK],
                  start=True, stop=True, sig=strip_flipped)
            flips = HALF * g + half + 1
            st.act.wait(strip_flipped.at(flips), zero, heads.last_maxed if g else None)
            st.act(nc.scalar.copy, strip[:, 2 * half:2 * half + 2, strip_at:strip_at + NEAR],
                   bank.rearrange("p (j x) -> p j x", x=NEAR), sig=strip_kept)
            small_ring.done[slot] = [strip_kept.at(flips)]

    def load_near(g):
        for s in range(SPLITS):
            st.sp.wait(heads.scored.at(heads.per_unit * nb * (g - 1)))
            near_ready[g] = st.load(near[g % 2][:, s, :, :],
                                    near_window(core.near_parts[s],
                                                slice(g * GROUP, (g + 1) * GROUP)),
                                    near_loaded[g % 2])

    def near_of(u, j, lo, hi):
        g = units[u][0]
        return [near[g % 2][:, s, j, lo:hi] for s in range(SPLITS)], near_ready[g]

    def strip_of(u, j, n, half):
        g = units[u][0]
        at = BANK - n * P + half * BANK
        return strip[:, j, at:at + BANK], [strip_kept.at(HALF * (g + 1))]

    exps = [st.sbuf(f"exps{i}", [P, 2, BANK]) for i in range(4)]
    weighted = Weighted(st, heads, score_ring, out_ring, small_ring, [e[:, :, :] for e in exps],
                        lambda: v_tok, lambda: ctx_tok)

    def maxima(u):
        g, b = units[u]
        steps = heads.maxima(u, small_ring)

        def first(f, args):
            if b == 0:
                load_strip(g)
            if u == 0:
                heads.fill(0, b, g, stored[b])
            f(*args)

        def ahead(f, args):
            if b == 0:
                load_near(g)
            if u + 1 < len(units):
                g2, b2 = units[u + 1]
                heads.fill(u + 1, b2, g2, stored[b2])
            f(*args)
        steps[0] = (first, steps[0])
        steps[24] = (ahead, steps[24])
        return steps

    interleave(range(len(units)), maxima,
               lambda u: weighted.steps(u, units[u][1] * NT, units[u][1] * NT, units[u][0],
                                        lambda: v_ready[units[u][1]]), lag=6)

    ctx_chn = Ring(weighted.out_chn)
    turn_ctx = Turn(st, small_ring, "_ctx")
    rows, norm = Rows(st, small_ring), Norm(st)
    done = weighted.context.at(4 * HALF * len(units))
    for b in range(nb):
        for n in range(b * NT, (b + 1) * NT, 4):
            cslot, chn, free = ctx_chn.take()
            kept = turn_ctx(ctx_tok[:, n:n + 4, :], chn[:, :], [done] + free)
            y = rows(lambda k, m: chn[:, m * P:(m + 1) * P], lambda k: w["o"][:, :], bo[:, :],
                     x[:, n:n + 4, :], x[:, n:n + 4, :], [kept, w_ready])
            ctx_chn.done[cslot] = [y]
        tiles = slice(b * NT, (b + 1) * NT)
        out = norm(x[:, tiles, :], x[:, tiles, :], [y])
        for n in range(b * NT, (b + 1) * NT, 4):
            kept = turn(x[:, n:n + 4, :], xc[:, n * P:n * P + BANK], [out])
    st.run()


def ternary_ffn(core):
    st = Stage(core, "tern")
    nc, inp = core.nc, core.inp
    x, xc, nb = core.x_tok, core.x_chn, core.n_batch
    banks = st.psum("p", 4)
    ring = Ring([banks[:, i, :] for i in range(4)])
    loaded, chain, summed = st.sem("loaded"), st.sem("chain"), st.sem("summed")
    w = st.sbuf("w", [P, C])
    up, down, total, delta = (st.sbuf(n, s) for n, s in (("up", [P, C]), ("down", [P, C]),
                                                         ("total", [P, 1]), ("delta", [P, 2])))
    st.load(w[:, :], inp["L0_ffn_weight_t"][:, :], loaded)
    alpha = st.sbuf("alpha", [P, 1])
    st.load(alpha[:, :], inp["L0_ffn_alpha"].rearrange("(o n) -> o n", o=1).broadcast_to([P, 1]),
            loaded)
    bias, t = broadcast_rows(st, "bias", inp["L0_ffn_bias"], C, loaded)
    st.dve.wait(t)
    v = st.dve(nc.vector.tensor_reduce, total[:, :], w[:, :], AX.X, ALU.add,
               apply_absolute_value=True, sig=chain)
    slot, bank, free = ring.take()
    st.pe.wait(v, core.const_ready)
    mm = st.pe(nc.tensor.matmul, bank[:, 0:1], core.ones[:, :], total[:, :], start=True, stop=True, sig=summed)
    st.dve.wait(mm)
    v = st.dve(nc.vector.tensor_scalar, delta[:, 0:1], bank[:, 0:1], 1.0 / (C * C), 0.7, ALU.mult,
               ALU.mult, sig=chain)
    ring.done[slot] = [v]
    st.dve.wait(v)
    v = st.dve(nc.vector.tensor_scalar, delta[:, 1:2], delta[:, 0:1], -1.0, None, ALU.mult, sig=chain)
    st.dve.wait(v)
    v = st.dve(nc.vector.tensor_scalar, up[:, :], w[:, :], delta[:, 0:1], None, ALU.is_gt, sig=chain)
    st.dve.wait(v)
    v = st.dve(nc.vector.tensor_scalar, down[:, :], w[:, :], delta[:, 1:2], None, ALU.is_lt, sig=chain)
    st.dve.wait(v)
    v = st.dve(nc.vector.tensor_tensor, up[:, :], up[:, :], down[:, :], ALU.subtract,
               sig=chain)
    st.dve.wait(v)
    w_ready = st.dve(nc.vector.tensor_scalar, up[:, :], up[:, :], alpha[:, 0:1], None, ALU.mult, sig=chain)
    rows, norm, turn = Rows(st, ring), Norm(st), Turn(st, ring)
    for b in range(nb):
        for n in range(b * NT, (b + 1) * NT, 4):
            y = rows(lambda k, m: xc[:, (n + m) * P:(n + m + 1) * P], lambda k: up[:, :],
                     bias[:, :], x[:, n:n + 4, :], x[:, n:n + 4, :], [w_ready])
        tiles = slice(b * NT, (b + 1) * NT)
        out = norm(x[:, tiles, :], x[:, tiles, :], [y])
        for n in range(b * NT, (b + 1) * NT, 4):
            turn(x[:, n:n + 4, :], xc[:, n * P:n * P + BANK], [out])
    st.run()


TAPS = 4
LOG1P_TERMS = 9


def linear_attention(core):
    st = Stage(core, "lin")
    nc, inp, const, nb = core.nc, core.inp, core.const, core.n_batch
    x, xc = core.x_tok, core.x_chn
    work_banks, out_banks = st.psum("work", 6), st.psum("out", 2)
    pairs = Ring([work_banks[:, 2 * i:2 * i + 2, :] for i in range(3)])
    out_free = []
    loaded = st.sem("loaded")
    w_qkv = st.sbuf("w_qkv", [P, 3 * C])
    w_z, w_out = st.sbuf("w_z", [P, C]), st.sbuf("w_out", [P, C])
    w_gate = st.sbuf("w_gate", [P, 2 * H])
    taps = st.sbuf("taps", [P, 3, TAPS])
    st.load(w_qkv[:, :], inp["L1_attn_W_qkv_t"][:, :], loaded)
    st.load(w_z[:, :], inp["L1_attn_W_z_t"][:, :], loaded)
    st.load(w_out[:, :], inp["L1_attn_W_out_t"][:, :], loaded)
    st.load(w_gate[:, 0:H], inp["L1_attn_W_b_t"][:, :], loaded)
    st.load(w_gate[:, H:2 * H], inp["L1_attn_W_a_t"][:, :], loaded)
    st.load(taps[:, :, :], inp["L1_attn_conv_w"].rearrange("(g p) o k -> p g (o k)", p=P), loaded)
    same_head = st.sbuf("same_head", [P, C])
    pick_v, place_v = st.sbuf("pick_v", [P, HD, C]), st.sbuf("place_v", [P, HD, C])
    gate_rows = st.sbuf("gate_rows", [2 * H, 2, C])
    st.load(same_head[:, :], const["same_head"][:, :], loaded)
    st.load(pick_v[:, :, :], const["pick_v"][:, :, :], loaded)
    st.load(place_v[:, :, :], const["place_v"][:, :, :], loaded)
    st.load(gate_rows[:, :, :], const["gate_rows"][:, :, :], loaded)
    dt_bias, _ = broadcast_rows(st, "dt_bias", inp["L1_attn_dt_bias"], H, loaded)
    a_log, ready = broadcast_rows(st, "a_log", inp["L1_attn_A_log"], H, loaded)
    ready = [ready, core.const_ready]
    small = st.sbuf("small", [P, 1])
    small_ready = st.pool(nc.gpsimd.memset, small[:, :], 1e-6, sig=st.sem("small_ready"))

    n_tiles = nb * NT
    gates = st.sbuf("gates", [P, n_tiles, 2 * H])
    z, e, s, s2, poly = (st.sbuf(n, [P, n_tiles, H]) for n in ("gz", "ge", "gs", "gs2", "gpoly"))
    rate = st.sbuf("rate", [P, H])
    g_mm, dv, av = st.sem("g_mm"), st.sem("g_dve"), st.sem("g_act")
    per_bank = BANK // (2 * H)
    slot, bank, free = pairs.take()
    flat = bank.rearrange("p a (n h) -> p (a n) h", h=2 * H)
    for n in range(n_tiles):
        st.pe.wait(*ready)
        mm = st.pe(nc.tensor.matmul, flat[:, n, :], xc[:, n * P:(n + 1) * P], w_gate[:, :],
                   start=True, stop=True, sig=g_mm)
    flat = flat[:, 0:n_tiles, :]
    st.dve.wait(mm, *ready)
    v = st.dve(nc.vector.tensor_tensor, z[:, :, :], flat[:, :, H:2 * H], spread(dt_bias[:, :], n_tiles),
               ALU.add, sig=dv)
    st.dve.wait(v)
    v = st.dve(nc.vector.scalar_tensor_tensor, s[:, :, :], z[:, :, :], -1.0, z[:, :, :], ALU.mult,
               ALU.max, sig=dv)
    st.act.wait(v)
    beta = st.act(nc.scalar.activation, gates[:, :, 0:H], flat[:, :, 0:H], ACT.Sigmoid, sig=av)
    pairs.done[slot] = [v, beta]
    st.act.wait(v)
    a = st.act(nc.scalar.activation, e[:, :, :], s[:, :, :], ACT.Exp, scale=-1.0, sig=av)
    r = st.act(nc.scalar.activation, rate[:, :], a_log[:, :], ACT.Exp, sig=av)
    st.dve.wait(a)
    v = st.dve(nc.vector.tensor_scalar, s[:, :, :], e[:, :, :], 2.0, None, ALU.add,
               sig=dv)
    st.dve.wait(v)
    v = st.dve(nc.vector.reciprocal, s[:, :, :], s[:, :, :], sig=dv)
    st.dve.wait(v)
    v = st.dve(nc.vector.tensor_tensor, s[:, :, :], s[:, :, :], e[:, :, :], ALU.mult,
               sig=dv)
    st.dve.wait(v)
    v = st.dve(nc.vector.tensor_tensor, s2[:, :, :], s[:, :, :], s[:, :, :], ALU.mult,
               sig=dv)
    top = LOG1P_TERMS - 1
    st.dve.wait(v)
    v = st.dve(nc.vector.tensor_scalar, poly[:, :, :], s2[:, :, :], 2.0 / (2 * top + 1), None,
               ALU.mult, sig=dv)
    for n in range(top - 1, 0, -1):
        st.dve.wait(v)
        v = st.dve(nc.vector.scalar_tensor_tensor, poly[:, :, :], poly[:, :, :],
                   2.0 / (2 * n + 1), s2[:, :, :], ALU.add, ALU.mult, sig=dv)
    st.dve.wait(v)
    v = st.dve(nc.vector.scalar_tensor_tensor, poly[:, :, :], poly[:, :, :], 2.0, s[:, :, :],
               ALU.add, ALU.mult, sig=dv)
    st.dve.wait(v)
    v = st.dve(nc.vector.scalar_tensor_tensor, poly[:, :, :], z[:, :, :], 0.0, poly[:, :, :],
               ALU.max, ALU.add, sig=dv)
    st.dve.wait(v, r)
    v = st.dve(nc.vector.tensor_tensor, poly[:, :, :], poly[:, :, :], spread(rate[:, :], n_tiles),
               ALU.mult, sig=dv)
    st.act.wait(v)
    decay = st.act(nc.scalar.activation, gates[:, :, H:2 * H], poly[:, :, :], ACT.Exp, scale=-1.0, sig=av)
    gates_row = st.sbuf("gates_row", [2 * H, nb * T])
    g_turn = st.sem("g_turned")
    for n in range(0, n_tiles, 8):
        slot, bank, free = pairs.take()
        for m in range(8):
            st.pe.wait(*free, decay, beta)
            t = st.pe(nc.tensor.transpose, bank[0:2 * H, m // 4, (m % 4) * P:(m % 4 + 1) * P],
                      gates[:, n + m, :], core.ident[:, :], sig=g_turn)
        st.act.wait(t)
        gates_ready = st.act(nc.scalar.copy,
                             gates_row[:, n * P:(n + 8) * P].rearrange("p (a b) -> p a b", a=2),
                             bank[0:2 * H, :, :], sig=av)
        pairs.done[slot] = [gates_ready]

    PAD = TAPS - 1
    mixed = [st.sbuf(f"mixed{g}", [P, PAD + T]) for g in range(3)]
    conv = [st.sbuf(f"conv{g}", [P, T]) for g in range(3)]
    silu_z, beta_v, decay_b = (st.sbuf(n, [P, T]) for n in ("silu_z", "beta_v", "decay_b"))
    square, norm_r = st.sbuf("square", [P, T]), st.sbuf("norm_r", [P, T])
    drive = Ring([st.sbuf(f"drive{i}", [P, T]) for i in range(2)])
    state = Ring([st.sbuf(f"state{i}", [P, T]) for i in range(2)])
    read_out = Ring([st.sbuf(f"read_out{i}", [P, T]) for i in range(2)])
    o = st.sbuf("o", [P, T])
    mm_s, act_s, dve_s, pool_s = (st.sem(n) for n in ("mm", "act", "dve", "pool"))
    row_ring = Ring([work_banks[:, i, :] for i in range(2)])
    for g in range(3):
        pad = st.pool(nc.gpsimd.memset, mixed[g][:, 0:PAD], 0.0, sig=pool_s)

    def two(ap):
        return ap.rearrange("p (a b) -> p a b", a=HALF)

    def product(w, rhs, after, **kw):
        slot, bank, free = pairs.take()
        for half in range(HALF):
            st.pe.wait(*free, *after)
            mm = st.pe(nc.tensor.matmul, bank[:, half, :], w, rhs[:, half * BANK:(half + 1) * BANK],
                       start=True, stop=True, sig=mm_s)
        return slot, bank, mm

    def head_norm(src, scale, eps_scale, out_scale, after, out):
        st.dve.wait(*after)
        sq = st.dve(nc.vector.tensor_tensor, square[:, :], src, src, ALU.mult,
                    sig=dve_s)
        slot, bank, mm = product(same_head[:, :], square, [sq])
        st.act.wait(mm, small_ready, sq)
        root = st.act(nc.scalar.activation, two(norm_r[:, :]), bank, ACT.Sqrt, bias=small[:, 0:1],
                      scale=scale, sig=act_s)
        pairs.done[slot] = [root]
        st.dve.wait(root)
        inv = st.dve(nc.vector.reciprocal, norm_r[:, :], norm_r[:, :], sig=dve_s)
        st.dve.wait(inv)
        return st.dve(nc.vector.scalar_tensor_tensor, out, src, out_scale, norm_r[:, :], ALU.mult,
                      ALU.mult, sig=dve_s)

    rows, norm = Rows(st, FirstBank(pairs)), Norm(st)
    turn = Turn(st, rows.ring)
    gated = st.sbuf("gated", [P, T])
    done = pad
    for b in range(nb):
        cols = xc[:, b * T:(b + 1) * T]
        conv_done = []
        for g in range(3):
            slot, bank, mm = product(w_qkv[:, g * C:(g + 1) * C], cols, ready)
            st.act.wait(mm, done, pad)
            kept = st.act(nc.scalar.copy, two(mixed[g][:, PAD:PAD + T]), bank, sig=act_s)
            pairs.done[slot] = [kept]
            st.dve.wait(kept, done)
            v = st.dve(nc.vector.tensor_scalar, conv[g][:, :], mixed[g][:, PAD:PAD + T],
                       taps[:, g, PAD:PAD + 1], None, ALU.mult, sig=dve_s)
            for k in range(PAD):
                st.dve.wait(v)
                v = st.dve(nc.vector.scalar_tensor_tensor, conv[g][:, :], mixed[g][:, k:k + T],
                           taps[:, g, k:k + 1], conv[g][:, :], ALU.mult, ALU.add,
                           sig=dve_s)
            conv_done.append(v)
        slot, bank, mm = product(w_z[:, :], cols, ready)
        silued = []
        for g in range(3):
            st.act.wait(conv_done[g])
            silued.append(st.act(nc.scalar.activation, conv[g][:, :], conv[g][:, :], ACT.Silu, sig=act_s))
        st.act.wait(mm, done)
        z_done = st.act(nc.scalar.activation, two(silu_z[:, :]), bank, ACT.Silu,
                        sig=act_s)
        pairs.done[slot] = [z_done]
        q = head_norm(conv[0][:, :], 1.0, None, HD ** -0.5, [silued[0]], conv[0][:, :])
        kk = head_norm(conv[1][:, :], 1.0, None, 1.0, [silued[1]], conv[1][:, :])
        row = gates_row[:, b * T:(b + 1) * T]
        slot, bank, mm = product(gate_rows[:, 0, :], row, [gates_ready])
        st.dve.wait(mm, silued[2])
        bv = st.dve(nc.vector.tensor_tensor, two(beta_v[:, :]), bank, two(conv[2][:, :]), ALU.mult, sig=dve_s)
        pairs.done[slot] = [bv]
        slot, bank, mm = product(gate_rows[:, 1, :], row, [gates_ready])
        st.act.wait(mm, done)
        dec = st.act(nc.scalar.copy, two(decay_b[:, :]), bank, sig=act_s)
        pairs.done[slot] = [dec]
        waiting = []

        def put(vi, ro, read):
            for half in range(HALF):
                st.pe.wait(*out_free, read)
                mm = st.pe(nc.tensor.matmul, out_banks[:, half, :], place_v[:, vi, :],
                           ro[:, half * BANK:(half + 1) * BANK], start=vi == 0, stop=vi == HD - 1, sig=mm_s)
            return mm

        for vi in range(HD):
            slot, bank, mm = product(pick_v[:, vi, :], beta_v, [bv])
            ds, dr, dfree = drive.take()
            st.dve.wait(mm, kk, *dfree)
            v = st.dve(nc.vector.tensor_tensor, two(dr[:, :]), bank, two(conv[1][:, :]), ALU.mult, sig=dve_s)
            pairs.done[slot] = [v]
            ss, sc, sfree = state.take()
            st.dve.wait(v, dec, *sfree)
            v = st.dve(nc.vector.tensor_tensor_scan, sc[:, :], decay_b[:, :], dr[:, :], 0.0,
                       ALU.mult, ALU.add, sig=dve_s)
            drive.done[ds] = [v]
            rs, ro, rfree = read_out.take()
            st.pool.wait(v, q, *rfree)
            r = st.pool(nc.gpsimd.tensor_tensor, ro[:, :], sc[:, :], conv[0][:, :], ALU.mult, sig=pool_s)
            state.done[ss] = [r]
            waiting.append((vi, ro, r, rs))
            if len(waiting) > 1:
                a = waiting.pop(0)
                read_out.done[a[3]] = [put(*a[:3])]
        a = waiting.pop(0)
        mm = put(*a[:3])
        read_out.done[a[3]] = [mm]
        st.act.wait(mm)
        kept = st.act(nc.scalar.copy, two(o[:, :]), out_banks[:, :, :], sig=act_s)
        out_free = [kept]
        v = head_norm(o[:, :], 1.0 / HD, None, 1.0, [kept], o[:, :])
        st.dve.wait(v)
        gd = st.dve(nc.vector.tensor_tensor, gated[:, :], o[:, :], silu_z[:, :], ALU.mult, sig=dve_s)
        done = gd
        for n in range(b * NT, (b + 1) * NT, 4):
            m0 = n - b * NT
            y = rows(lambda k, m: gated[:, (m0 + m) * P:(m0 + m + 1) * P], lambda k: w_out[:, :],
                     None, x[:, n:n + 4, :], x[:, n:n + 4, :], [gd])
        tiles = slice(b * NT, (b + 1) * NT)
        out = norm(x[:, tiles, :], x[:, tiles, :], [y])
        for n in range(b * NT, (b + 1) * NT, 4):
            turn(x[:, n:n + 4, :], xc[:, n * P:n * P + BANK], [out])
    st.run()


class FirstBank:

    def __init__(self, pairs):
        self.pairs, self.done = pairs, pairs.done

    def take(self):
        slot, bank, free = self.pairs.take()
        return slot, bank[:, 0, :], free


class TopTwo:

    def __init__(self, st, tiles, n):
        self.st, self.tiles, self.n = st, tiles, n
        self.a, self.b, self.first, self.second = (st.sbuf(f"top_{i}", [P, tiles, n])
                                                   for i in ("a", "b", "first", "second"))
        self.m1, self.m2, self.key = (st.sbuf(f"top_{i}", [P, tiles]) for i in ("m1", "m2", "key"))
        self.ramp = st.sbuf("top_ramp", [P, n])
        self.loaded, self.dv = st.sem("top_loaded"), st.sem("top_dve")
        self.ramp_ready = st.load(self.ramp[:, :], st.core.const[f"ramp{n}"][:, :], self.loaded)

    def pick(self, scores, peak, hot, after):
        st, nc, n = self.st, self.st.nc, self.n
        st.dve.wait(*after)
        v = st.dve(nc.vector.tensor_reduce, peak[:, :], scores, AX.X, ALU.max,
                   sig=self.dv)
        st.dve.wait(v)
        v = st.dve(nc.vector.tensor_tensor, self.a[:, :, :], scores, along(peak[:, :], n),
                   ALU.is_equal, sig=self.dv)
        st.dve.wait(v, self.ramp_ready)
        v = st.dve(nc.vector.tensor_tensor, self.a[:, :, :], self.a[:, :, :],
                   spread(self.ramp[:, :], self.tiles), ALU.mult,
                   sig=self.dv)
        st.dve.wait(v)
        v = st.dve(nc.vector.tensor_reduce, self.key[:, :], self.a[:, :, :], AX.X, ALU.max, sig=self.dv)
        st.dve.wait(v)
        return st.dve(nc.vector.tensor_tensor, hot[:, :, :], self.a[:, :, :],
                      along(self.key[:, :], n), ALU.is_equal, sig=self.dv)

    def __call__(self, scores, gates, after):
        st, nc, n = self.st, self.st.nc, self.n
        v = self.pick(scores, self.m1, self.first, after)
        st.dve.wait(v)
        v = st.dve(nc.vector.scalar_tensor_tensor, self.b[:, :, :], self.first[:, :, :], -4.0,
                   scores, ALU.mult, ALU.add, sig=self.dv)
        v = self.pick(self.b[:, :, :], self.m2, self.second, [v])
        st.dve.wait(v)
        v = st.dve(nc.vector.tensor_tensor, self.key[:, :], self.m1[:, :], self.m2[:, :], ALU.add, sig=self.dv)
        st.dve.wait(v)
        v = st.dve(nc.vector.reciprocal, self.key[:, :], self.key[:, :], sig=self.dv)
        for m, hot in ((self.m1, self.first), (self.m2, self.second)):
            st.dve.wait(v)
            v = st.dve(nc.vector.tensor_tensor, m[:, :], m[:, :], self.key[:, :], ALU.mult, sig=self.dv)
            st.dve.wait(v)
            v = st.dve(nc.vector.tensor_tensor, hot[:, :, :], hot[:, :, :], along(m[:, :], n),
                       ALU.mult, sig=self.dv)
        st.dve.wait(v)
        return st.dve(nc.vector.tensor_tensor, gates, self.first[:, :, :], self.second[:, :, :],
                      ALU.add, sig=self.dv)


def router(st, ring, w, bias, chn, n_tiles, n, out, done, after):
    nc = st.nc
    slot, bank, free = ring.take()
    flat = bank.rearrange("p (t e) -> p t e", e=n)
    for t in range(n_tiles):
        st.pe.wait(*after, *free)
        mm = st.pe(nc.tensor.matmul, flat[:, t, :], chn[:, t * P:(t + 1) * P], w, start=True,
                   stop=True, sig=st.routed)
    st.dve.wait(mm, *after)
    kept = st.dve(nc.vector.tensor_tensor, out, flat[:, 0:n_tiles, :], spread(bias, n_tiles),
                  ALU.add, sig=done)
    ring.done[slot] = [kept]
    return kept


def gate_rows_of(st, ring, gates, rows, n_tiles, n, after):
    nc = st.nc
    turned, kept = st.sem("gates_turned"), st.sem("gates_kept")
    for t in range(0, n_tiles, 4):
        slot, bank, free = ring.take()
        for m in range(4):
            st.pe.wait(*free, *after)
            mm = st.pe(nc.tensor.transpose, bank[0:n, m * P:(m + 1) * P], gates[:, t + m, :],
                       st.core.ident[:, :], sig=turned)
        st.act.wait(mm)
        last = st.act(nc.scalar.copy, rows[:, t * P:(t + 4) * P], bank[0:n, :],
                      sig=kept)
        ring.done[slot] = [last]
    return last


E1, I1 = 16, 64


def expert_ffn(core):
    st = Stage(core, "moe1")
    nc, inp, const, nb = core.nc, core.inp, core.const, core.n_batch
    x, xc = core.x_tok, core.x_chn
    n_tiles = nb * NT
    banks = st.psum("p", 8)
    ring = Ring([banks[:, i, :] for i in range(6)])
    out_ring = Ring([banks[:, 6 + i, :] for i in range(2)])
    st.routed = st.sem("routed")
    loaded, big_loaded = st.sem("loaded"), st.sem("big_loaded")
    w_router = st.sbuf("w_router", [P, E1])
    pair_rows = st.sbuf("pair_rows", [E1, E1 // 2, P])
    st.load(w_router[:, :], inp["L1_ffn_gate_w"][:, :], loaded)
    st.load(pair_rows[:, :, :], const["pair_rows"][:, :, :], loaded)
    router_bias, small_ready = broadcast_rows(st, "router_bias", inp["L1_ffn_gate_b"], E1, loaded)
    pairs_n = E1 // 2
    wg, wu = st.sbuf("wg", [P, E1, I1]), st.sbuf("wu", [P, E1, I1])
    wd = st.sbuf("wd", [P, pairs_n, C])
    sg, su, sd = st.sbuf("sg", [P, I1]), st.sbuf("su", [P, I1]), st.sbuf("sd", [I1, C])
    st.load(sg[:, :], inp["L1_ffn_shared_wg"][:, :], big_loaded)
    st.load(su[:, :], inp["L1_ffn_shared_wu"][:, :], big_loaded)
    st.load(sd[:, :], inp["L1_ffn_shared_wd"][:, :], big_loaded)
    st.load(wg[:, :, :], inp["L1_ffn_experts_wg"].rearrange("e d i -> d e i"), big_loaded)
    st.load(wu[:, :, :], inp["L1_ffn_experts_wu"].rearrange("e d i -> d e i"), big_loaded)
    w_ready = st.load(wd[:, :, :], inp["L1_ffn_experts_wd"].rearrange("(m e) i d -> (e i) m d", e=2),
                      big_loaded)
    logits, gates = st.sbuf("logits", [P, n_tiles, E1]), st.sbuf("gates", [P, n_tiles, E1])
    gate_row = st.sbuf("gate_row", [E1, nb * T])
    r_done, sig_done = st.sem("logits_done"), st.sem("sigmoid_done")
    v = router(st, ring, w_router[:, :], router_bias[:, :], xc, n_tiles, E1, logits[:, :, :],
               r_done, [small_ready])
    st.act.wait(v)
    v = st.act(nc.scalar.activation, logits[:, :, :], logits[:, :, :], ACT.Sigmoid,
               sig=sig_done)
    top = TopTwo(st, n_tiles, E1)
    v = top(logits[:, :, :], gates[:, :, :], [v])
    row_ready = gate_rows_of(st, ring, gates, gate_row, n_tiles, E1, [v])
    act_g = Ring([st.sbuf(f"act_g{i}", [P, BANK]) for i in range(3)])
    hidden = Ring([st.sbuf(f"hidden{i}", [P, BANK]) for i in range(3)])
    up_mm, silued, lifted, scaled, down_mm = (st.sem(n) for n in
                                              ("up_mm", "silued", "lifted", "scaled", "down_mm"))
    added = st.sem("added")
    norm, turn = Norm(st), Turn(st, ring)
    for b in range(nb):
        for n in range(b * NT, (b + 1) * NT, 4):
            cols = xc[:, n * P:n * P + BANK]
            oslot, out, ofree = out_ring.take()
            late = []

            def down(m, k, h, hslot, ready):
                rows = I1 if m == 0 else P
                for i in range(4):
                    st.pe.wait(*ofree, ready, w_ready)
                    mm = st.pe(nc.tensor.matmul, banks4(out)[:, i, :], h[0:rows, i * P:(i + 1) * P],
                               k, start=m == 0 and i == 0, stop=m == pairs_n, skip_group_check=True, sig=down_mm)
                hidden.done[hslot] = [mm]
                return mm

            for m in range(pairs_n + 1):
                if m == 0:
                    g_w, u_w, k, r = sg[:, :], su[:, :], sd[:, :], I1
                else:
                    pair = slice(2 * (m - 1), 2 * m)
                    g_w = wg[:, pair, :].rearrange("p e i -> p (e i)")
                    u_w = wu[:, pair, :].rearrange("p e i -> p (e i)")
                    k, r = wd[:, m - 1, :], P
                gs, gb, gfree = ring.take()
                st.pe.wait(*gfree, w_ready)
                mm_g = st.pe(nc.tensor.matmul, gb[0:r, :], g_w, cols, start=True, stop=True, sig=up_mm)
                us, ub, ufree = ring.take()
                st.pe.wait(*ufree)
                mm_u = st.pe(nc.tensor.matmul, ub[0:r, :], u_w, cols, start=True, stop=True, sig=up_mm)
                a_s, ag, afree = act_g.take()
                st.act.wait(mm_g, *afree)
                a = st.act(nc.scalar.activation, ag[0:r, :], gb[0:r, :], ACT.Silu, sig=silued)
                ring.done[gs] = [a]
                hs, h, hfree = hidden.take()
                st.dve.wait(a, mm_u, *hfree)
                v = st.dve(nc.vector.tensor_tensor, h[0:r, :], ub[0:r, :], ag[0:r, :], ALU.mult, sig=lifted)
                ring.done[us] = [v]
                act_g.done[a_s] = [v]
                if m:
                    bs, bb, bfree = ring.take()
                    st.pe.wait(*bfree, row_ready)
                    mm = st.pe(nc.tensor.matmul, bb, pair_rows[:, m - 1, :],
                               gate_row[:, n * P:n * P + BANK], start=True, stop=True, sig=up_mm)
                    st.dve.wait(v, mm)
                    v = st.dve(nc.vector.tensor_tensor, h[:, :], bb, h[:, :], ALU.mult, sig=scaled)
                    ring.done[bs] = [v]
                late.append((m, k, h, hs, v))
                if len(late) > 1:
                    down(*late.pop(0))
            mm = down(*late.pop(0))
            st.dve.wait(mm)
            y = st.dve(nc.vector.scalar_tensor_tensor, x[:, n:n + 4, :], x[:, n:n + 4, :], 2.0,
                       banks4(out), ALU.mult, ALU.add, sig=added)
            out_ring.done[oslot] = [y]
        tiles = slice(b * NT, (b + 1) * NT)
        done = norm(x[:, tiles, :], x[:, tiles, :], [y])
        for n in range(b * NT, (b + 1) * NT, 4):
            turn(x[:, n:n + 4, :], xc[:, n * P:n * P + BANK], [done])
    st.run()


def causal_attention(core):
    st = Stage(core, "caus")
    nc, inp, const, nb = core.nc, core.inp, core.const, core.n_batch
    x, xc = core.x_tok, core.x_chn
    score_banks, small_banks, out_banks = st.psum("score", 4), st.psum("small", 3), st.psum("out", 1)
    score_ring = Ring([score_banks[:, 0:2, :], score_banks[:, 2:4, :]])
    small_ring = Ring([small_banks[:, i, :] for i in range(3)])
    out_ring = Ring([out_banks[:, 0, :]])
    st.projected = st.sem("projected")
    loaded = st.sem("loaded")
    w = st.sbuf("w", [P, 2 * C])
    bias = st.sbuf("bias", [P, 2])
    head_w = st.sbuf("head_w", [P, H, C])
    st.load(w[:, :], inp["L2_attn_W_attn"][:, :], loaded)
    st.load(bias[:, :], inp["L2_attn_b_attn_c"][:, :], loaded)
    w_ready = st.load(head_w[:, :, :], inp["L2_attn_head_weights"].rearrange("(o h) c -> o h c", o=1)
                      .broadcast_to([P, H, C]), loaded)
    heads = SmallHeads(st, 2 * (BANK // P) * 3, core.q_parts, core.k_parts, const["zero_rows"],
                       causal=True)
    q_done, k_done = st.sem("q_done"), st.sem("k_done")
    split_q, split_k = Parts(st, "q"), Parts(st, "k")
    value = {n: st.sbuf(f"value_{n}", [P, T]) for n in "qk"}
    stored = []
    for b in range(nb):
        cols = xc[:, b * T:(b + 1) * T]
        q = project_small(st, score_ring, w[:, 0:C], bias[:, 0:1], HD ** -0.5, value["q"][:, :],
                          cols, q_done, [w_ready], [split_q.last_less])
        s1 = split_q(value["q"][:, :], core.q_parts[b], [q])
        k = project_small(st, score_ring, w[:, C:2 * C], bias[:, 1:2], 1.0, value["k"][:, :],
                          cols, k_done, [w_ready], [split_k.last_less])
        s2 = split_k(value["k"][:, :], core.k_parts[b], [k])
        stored.append([s1, s2])

    x_one = [st.sbuf(f"x_one{i}", [P, NT, C + 1]) for i in range(2)]
    y = [core.attn_w[:, i * T:(i + 1) * T].rearrange("p (n c) -> p n c", c=C) for i in range(2)]
    exps = [core.big[:, i * NT * BANK:(i + 1) * NT * BANK].rearrange("p (k q) -> p k q", k=NT)
            for i in range(2)]
    x_made, y_zero, exped, weighted = (st.sem(n) for n in (
        "x_made", "y_zero", "exped", "weighted"))
    inverted, scaled, summed = st.sem("inverted"), st.sem("scaled"), st.sem("summed")
    scored = heads.scored
    r_sum = st.sbuf("r_sum", [P, 2])
    part = [st.sbuf(f"part{i}", [P, 2, C]) for i in range(3)]
    units = [(b, g) for b in range(nb) for g in range(H // GROUP)]
    QB = BANK // P
    norm, turn = Norm(st), Turn(st, small_ring)
    x_added = st.sem("x_added")
    OUTS = QB // 2
    outs_of_batch = H * HALF * OUTS
    n = {"tile": 0, "part": 0}
    behind = []

    def steps(u):
        b, g = units[u]
        i = u % heads.SLOTS
        q, k = heads.q_stack[i], heads.k_stack[i]

        def start_batch():
            st.pool.wait(weighted.at(outs_of_batch * (b - 1)))
            st.pool(nc.gpsimd.memset, x_one[b % 2][:, :, C:C + 1], 1.0, sig=x_made)
            st.pool.wait(x_made.at(2 * b + 1))
            st.pool(nc.gpsimd.tensor_copy, x_one[b % 2][:, :, 0:C], x[:, b * NT:(b + 1) * NT, :],
                    sig=x_made)
            st.pool.wait(x_added.at(b - 1))
            st.pool(nc.gpsimd.memset, y[b % 2], 0.0, sig=y_zero)

        def scores(half, j, two):
            if g == 0 and half == 0 and j == 0 and two == 0:
                start_batch()
            t, h = n["tile"], n["part"]
            n["tile"] += 1
            banks, e = score_ring.buffers[t % 2], exps[h % 2]
            diagonal = 2 * two >= half * QB
            lo = max(2 * two * P - half * BANK, 0)
            st.pe.wait(heads.row_ready[i], heads.ready[i])
            st.pe.wait(exped.at(t - 1), *(score_ring.done[t % 2] if t < 2 else ()))
            for c in range(2):
                kb = 2 * two + c
                st.pe(nc.tensor.matmul, banks[:, c, lo:BANK], k[0:STACK, j, kb * P:(kb + 1) * P],
                      q[0:STACK, j, half * BANK + lo:(half + 1) * BANK], start=True,
                      stop=not diagonal, sig=scored if c == 1 and not diagonal else None)
                if diagonal:
                    at = kb * P - half * BANK
                    st.pe(nc.tensor.matmul, banks[:, c, at:at + P], st.core.ident_bf[:, :],
                          st.core.causal_mask[:, :], start=False, stop=True,
                          sig=scored if c == 1 else None)
            st.act.wait(scored.at(t + 1), weighted.at(OUTS * (h - 1)))
            st.act(nc.scalar.activation, e[:, 2 * two:2 * two + 2, lo:BANK], banks[:, :, lo:BANK],
                   ACT.Exp, sig=exped)
            tiles = (half + 1) * QB // 2
            if behind and two % (tiles // 2) == 0:
                follow()
            if two == tiles - 1:
                n["part"] += 1
                for m in range(OUTS):
                    behind.append((b, h, half, g * GROUP + j, m, t))

        return [(scores, (half, j, two)) for half in range(HALF) for j in range(GROUP)
                for two in range((half + 1) * QB // 2)]

    def follow():
        b, h, half, head, two, t = behind.pop(0)
        o = OUTS * h + two
        out, p, e = out_ring.buffers[o % len(out_ring.buffers)], part[o % 3], exps[h % 2]
        st.pe.wait(exped.at(t + 1), x_made.at(2 * (b + 1)))
        st.pe.wait(scaled.at(2 * (o + 1 - len(out_ring.buffers))))
        for m in range(2):
            nq = 2 * two + m
            kbs = half * QB + nq + 1
            for kb in range(kbs):
                st.pe(nc.tensor.matmul, out[:, m * (C + 1):(m + 1) * (C + 1)],
                      e[:, kb, nq * P:(nq + 1) * P], x_one[b % 2][:, kb, :],
                      start=kb == 0, stop=kb == kbs - 1,
                      sig=weighted if m == 1 and kb == kbs - 1 else None)
        both = out[:, 0:2 * (C + 1)].rearrange("p (m c) -> p m c", c=C + 1)
        st.dve.wait(weighted.at(o + 1), scaled.at(2 * o))
        st.dve(nc.vector.reciprocal, r_sum[:, :], both[:, :, C], sig=inverted)
        st.dve.wait(inverted.at(o + 1), w_ready, summed.at(o - 2))
        for m in range(2):
            st.dve(nc.vector.scalar_tensor_tensor, p[:, m, :], both[:, m, 0:C],
                   r_sum[:, m:m + 1], head_w[:, head, :], ALU.mult, ALU.mult, sig=scaled)
        at = half * QB + 2 * two
        st.pool.wait(scaled.at(2 * (o + 1)), y_zero.at(b + 1), summed.at(o))
        st.pool(nc.gpsimd.tensor_tensor, y[b % 2][:, at:at + 2, :], y[b % 2][:, at:at + 2, :],
                p[:, :, :], ALU.add, sig=summed)
        if o + 1 == outs_of_batch * (b + 1):
            finish(b)

    def finish(b):
        tiles = slice(b * NT, (b + 1) * NT)
        st.dve.wait(summed.at(outs_of_batch * (b + 1)))
        st.dve(nc.vector.tensor_tensor, x[:, tiles, :], x[:, tiles, :], y[b % 2], ALU.add,
               sig=x_added)
        out = norm(x[:, tiles, :], x[:, tiles, :], [x_added.at(b + 1)])
        for m in range(b * NT, (b + 1) * NT, 4):
            turn(x[:, m:m + 4, :], xc[:, m * P:m * P + BANK], [out])

    def maxima(u):
        b, g = units[u]
        out = heads.maxima(u, small_ring)

        def first(f, args):
            if u == 0:
                heads.fill(0, b, g, stored[b])
            f(*args)

        def ahead(f, args):
            if u + 1 < len(units):
                b2, g2 = units[u + 1]
                heads.fill(u + 1, b2, g2, stored[b2])
            f(*args)
        out[0] = (first, out[0])
        out[24] = (ahead, out[24])
        return out

    interleave(range(len(units)), maxima, steps, lag=4)
    while behind:
        follow()
    st.run()


E2, FF = 8, 512


def rotary_attention(core):
    st = Stage(core, "rot")
    nc, inp, const, nb = core.nc, core.inp, core.const, core.n_batch
    x, xc, x1 = core.x_tok, core.x_chn, core.x_mid
    score_banks, small_banks, out_banks = st.psum("score", 4), st.psum("small", 3), st.psum("out", 1)
    score_ring = Ring([score_banks[:, 0:2, :], score_banks[:, 2:4, :]])
    small_ring = Ring([small_banks[:, i, :] for i in range(3)])
    out_ring = Ring([out_banks[:, 0, :]])
    st.projected = st.sem("projected")
    w_loaded = st.sem("w_loaded")
    w = {}
    for n in "qkvo":
        w[n] = st.sbuf(f"w{n}", [P, C])
        st.load(w[n][:, :], inp[f"L2_ffn_W{n}"][:, :], w_loaded)
    bq, _ = column(st, "bq", inp["L2_ffn_bq"], w_loaded)
    bk, _ = column(st, "bk", inp["L2_ffn_bk"], w_loaded)
    bv, _ = broadcast_rows(st, "bv", inp["L2_ffn_bv"], C, w_loaded)
    bo, _ = broadcast_rows(st, "bo", inp["L2_ffn_bo"], C, w_loaded)
    g1, _ = broadcast_rows(st, "g1", inp["L2_ffn_g1"], C, w_loaded)
    be1, _ = broadcast_rows(st, "be1", inp["L2_ffn_be1"], C, w_loaded)
    rotate = st.sbuf("rotate", [P, C])
    angle = core.big[:, 2 * T:4 * T].rearrange("p (a t) -> p a t", a=2)
    st.load(rotate[:, :], const["rotate"][:, :], w_loaded)
    w_ready = st.load(angle, const["angle"][:, :, :], w_loaded)
    heads = SmallHeads(st, HALF * NT * 2, core.q_parts, core.k_parts, const["zero_rows"])
    done = {n: st.sem(f"{n}_done") for n in "qkv"}
    split = {n: Parts(st, n) for n in "qk"}
    value = {n: st.sbuf(f"value_{n}", [P, T]) for n in "qk"}
    turned = Ring([core.big[:, i * T:(i + 1) * T] for i in range(2)])
    v_tok = core.big[:, 4 * T:4 * T + nb * T].rearrange("p (n c) -> p n c", c=C)
    rot_mm, rot_v = st.sem("rot_mm"), st.sem("rot_v")
    bias = {"q": bq, "k": bk}
    scale = {"q": HD ** -0.5, "k": 1.0}
    dram = {"q": core.q_parts, "k": core.k_parts}
    stored, v_ready = [], []

    def two(ap):
        return ap.rearrange("p (a b) -> p a b", a=HALF)

    for b in range(nb):
        cols = xc[:, b * T:(b + 1) * T]
        both = []
        for n in "qk":
            val = value[n]
            ready = project_small(st, score_ring, w[n][:, :], bias[n][:, 0:1], scale[n], val[:, :],
                                  cols, done[n], [w_ready], [split[n].last_less])
            slot, bank, free = score_ring.take()
            for half in range(HALF):
                st.pe.wait(*free, ready)
                mm = st.pe(nc.tensor.matmul, bank[:, half, :], rotate[:, :],
                           val[:, half * BANK:(half + 1) * BANK], start=True, stop=True, sig=rot_mm)
            ts, t, tfree = turned.take()
            st.dve.wait(mm, *tfree)
            r = st.dve(nc.vector.tensor_tensor, two(t), bank, two(angle[:, 1, :]), ALU.mult, sig=rot_v)
            score_ring.done[slot] = [r]
            st.dve.wait(r)
            v = st.dve(nc.vector.tensor_tensor, val[:, :], val[:, :], angle[:, 0, :], ALU.mult, sig=rot_v)
            st.dve.wait(v)
            v = st.dve(nc.vector.tensor_tensor, val[:, :], val[:, :], t, ALU.add,
                       sig=rot_v)
            turned.done[ts] = [v]
            both.append(split[n](val[:, :], dram[n][b], [v]))
        stored.append(both)
        v_ready.append(values_small(st, score_ring, w["v"][:, :], bv[:, :],
                                    v_tok[:, b * NT:(b + 1) * NT, :], cols, done["v"], [w_ready]))
    units = [(b, g) for b in range(nb) for g in range(H // GROUP)]
    exps = [core.attn_w[:, i * T:(i + 1) * T].rearrange("p (a q) -> p a q", a=2) for i in range(4)]
    ctx = [st.sbuf(f"ctx{i}", [P, NT, C]) for i in range(2)]
    at = {"b": 0}
    weighted = Weighted(st, heads, score_ring, out_ring, small_ring, exps,
                        lambda: v_tok, lambda: ctx[at["b"] % 2])
    ctx_chn = Ring(weighted.out_chn)
    turn, turn_ctx = Turn(st, small_ring), Turn(st, small_ring, "_ctx")
    rows, norm = Rows(st, small_ring), Norm(st)
    affine = st.sem("affine")

    def finish(b):
        c = ctx[b % 2]
        done_b = weighted.context.at(4 * HALF * (H // GROUP) * (b + 1))
        for n in range(0, NT, 4):
            cslot, chn, free = ctx_chn.take()
            kept = turn_ctx(c[:, n:n + 4, :], chn[:, :], [done_b] + free)
            m0 = b * NT + n
            y = rows(lambda k, m: chn[:, m * P:(m + 1) * P], lambda k: w["o"][:, :], bo[:, :],
                     x[:, m0:m0 + 4, :], x1[:, m0:m0 + 4, :], [kept, w_ready])
            ctx_chn.done[cslot] = [y]
        tiles = slice(b * NT, (b + 1) * NT)
        out = norm(x1[:, tiles, :], x1[:, tiles, :], [y])
        st.dve.wait(out)
        v = st.dve(nc.vector.tensor_tensor, x1[:, tiles, :], x1[:, tiles, :], spread(g1[:, :], NT),
                   ALU.mult, sig=affine)
        st.dve.wait(v)
        v = st.dve(nc.vector.tensor_tensor, x1[:, tiles, :], x1[:, tiles, :], spread(be1[:, :], NT),
                   ALU.add, sig=affine)
        for n in range(b * NT, (b + 1) * NT, 4):
            turn(x1[:, n:n + 4, :], xc[:, n * P:n * P + BANK], [v])

    def maxima(u):
        b, g = units[u]
        out = heads.maxima(u, small_ring)

        def first(f, args):
            if u == 0:
                heads.fill(0, b, g, stored[b])
            f(*args)

        def ahead(f, args):
            if u + 1 < len(units):
                b2, g2 = units[u + 1]
                heads.fill(u + 1, b2, g2, stored[b2])
            f(*args)
        out[0] = (first, out[0])
        out[24] = (ahead, out[24])
        return out

    def exp_steps(u):
        b, g = units[u]
        out = weighted.steps(u, b * NT, 0, g, lambda: v_ready[b])

        def mark(f, args):
            at["b"] = b
            f(*args)
        out[0] = (mark, out[0])
        if g == H // GROUP - 1:
            f, a = out[-1]
            out[-1] = (lambda *args: (f(*args), finish(b)), a)
        return out

    interleave(range(len(units)), maxima, exp_steps, lag=6)
    st.run()


class Experts:

    def __init__(self, st, w1, w2, b1, b2, ready, func, hidden):
        self.st, self.w1, self.w2, self.b1, self.b2 = st, w1, w2, b1, b2
        self.ready, self.func = ready, func
        banks = st.psum("experts", 5)
        self.up_ring = Ring([banks[:, i, :] for i in range(3)])
        self.down_ring = Ring([banks[:, 3 + i, :] for i in range(2)])
        self.hidden = Ring(hidden)
        self.up, self.acted, self.down, self.gated = (st.sem(n) for n in (
            "up", "acted", "down", "gated"))

    def __call__(self, cols, gates, gate_rows, gates_ready, rows_ready, acc, base, base_ready):
        st, nc = self.st, self.st.nc
        slot, bank, free = self.down_ring.take()
        for i in range(4):
            st.pe.wait(*free, rows_ready, self.ready)
            mm = st.pe(nc.tensor.matmul, banks4(bank)[:, i, :], gate_rows(i), self.b2, start=True,
                       stop=True, sig=self.down)
        st.dve.wait(mm, *base_ready)
        v = st.dve(nc.vector.tensor_tensor, acc, banks4(bank), base, ALU.add, sig=self.gated)
        self.down_ring.done[slot] = [v]
        late = []

        def down():
            e, hs = late.pop(0)
            slot, bank, free = self.down_ring.take()
            for i in range(4):
                for c in range(FF // P):
                    hslot, h, a = hs[c]
                    st.pe.wait(*free, a)
                    mm = st.pe(nc.tensor.matmul, banks4(bank)[:, i, :], h[:, i * P:(i + 1) * P],
                               self.w2[:, e, c, :], start=c == 0, stop=c == FF // P - 1, sig=self.down)
            for hslot, _, _ in hs:
                self.hidden.done[hslot] = [mm]
            for i in range(4):
                st.dve.wait(mm, gates_ready, self.last_acc)
                v = st.dve(nc.vector.scalar_tensor_tensor, acc[:, i, :], banks4(bank)[:, i, :],
                           gates(e, i), acc[:, i, :], ALU.mult, ALU.add, sig=self.gated)
            self.last_acc = v
            self.down_ring.done[slot] = [v]

        self.last_acc = v
        for e in range(E2):
            hs = []
            for c in range(FF // P):
                uslot, ub, ufree = self.up_ring.take()
                st.pe.wait(*ufree, self.ready)
                mm = st.pe(nc.tensor.matmul, ub, self.w1[:, e, c * P:(c + 1) * P], cols, start=True,
                           stop=True, sig=self.up)
                hslot, h, hfree = self.hidden.take()
                st.act.wait(mm, self.ready, *hfree)
                a = st.act(nc.scalar.activation, h, ub, self.func, bias=self.b1[:, e, c:c + 1], sig=self.acted)
                self.up_ring.done[uslot] = [a]
                hs.append((hslot, h, a))
            late.append((e, hs))
            if len(late) > 1:
                down()
        down()
        return self.last_acc


def load_experts(st, core, name, small):
    inp = core.inp
    loaded = st.sem("experts_loaded")
    w1 = core.big[:, 0:E2 * FF].rearrange("p (e f) -> p e f", e=E2)
    w2 = core.big[:, E2 * FF:2 * E2 * FF].rearrange("p (e c d) -> p e c d", e=E2, d=C)
    b1, b2 = st.sbuf("b1", [P, E2, FF // P]), st.sbuf("b2", [E2, C])
    for e in range(E2):
        st.load(w1[:, e, :], inp[f"{name}_W1"][e], loaded)
        st.load(w2[:, e, :, :], inp[f"{name}_W2"][e].rearrange("(c p) d -> p c d", p=P), loaded)
    st.load(b1[:, :, :], inp[f"{name}_b1_c"][:, :, :], loaded)
    ready = st.load(b2[:, :], inp[f"{name}_b2"][:, :], loaded)
    return w1, w2, b1, b2, ready


def block_experts(core):
    st = Stage(core, "moe2")
    nc, inp, const, nb = core.nc, core.inp, core.const, core.n_batch
    x, xc, x1 = core.x_tok, core.x_chn, core.x_mid
    n_tiles = nb * NT
    small_banks = st.psum("small", 3)
    ring = Ring([small_banks[:, i, :] for i in range(3)])
    st.routed = st.sem("routed")
    loaded = st.sem("loaded")
    w_router = st.sbuf("w_router", [P, E2])
    st.load(w_router[:, :], inp["L2_ffn_Wg"][:, :], loaded)
    router_bias, _ = broadcast_rows(st, "router_bias", inp["L2_ffn_bg"], E2, loaded)
    g2, _ = broadcast_rows(st, "g2", inp["L2_ffn_g2"], C, loaded)
    be2, small_ready = broadcast_rows(st, "be2", inp["L2_ffn_be2"], C, loaded)
    w1, w2, b1, b2, w_ready = load_experts(st, core, "L2_ffn", None)
    logits, gates = st.sbuf("logits", [P, n_tiles, E2]), st.sbuf("gates", [P, n_tiles, E2])
    total = st.sbuf("total", [P, n_tiles])
    gate_row = st.sbuf("gate_row", [E2, nb * T])
    r_done, sm, ex = st.sem("logits_done"), st.sem("softmax"), st.sem("exp_done")
    v = router(st, ring, w_router[:, :], router_bias[:, :], xc, n_tiles, E2, logits[:, :, :],
               r_done, [small_ready])
    st.dve.wait(v)
    v = st.dve(nc.vector.tensor_reduce, total[:, :], logits[:, :, :], AX.X, ALU.max,
               sig=sm)
    st.dve.wait(v)
    v = st.dve(nc.vector.tensor_tensor, logits[:, :, :], logits[:, :, :], along(total[:, :], E2),
               ALU.subtract, sig=sm)
    st.act.wait(v)
    v = st.act(nc.scalar.activation, logits[:, :, :], logits[:, :, :], ACT.Exp, sig=ex)
    st.dve.wait(v)
    v = st.dve(nc.vector.tensor_reduce, total[:, :], logits[:, :, :], AX.X, ALU.add,
               sig=sm)
    st.dve.wait(v)
    v = st.dve(nc.vector.reciprocal, total[:, :], total[:, :], sig=sm)
    st.dve.wait(v)
    v = st.dve(nc.vector.tensor_tensor, logits[:, :, :], logits[:, :, :], along(total[:, :], E2),
               ALU.mult, sig=sm)
    top = TopTwo(st, n_tiles, E2)
    gates_ready = top(logits[:, :, :], gates[:, :, :], [v])
    rows_ready = gate_rows_of(st, ring, gates, gate_row, n_tiles, E2, [gates_ready])
    hidden = [st.sbuf(f"hidden{i}", [P, BANK]) for i in range(8)]
    experts = Experts(st, w1, w2, b1, b2[:, :], w_ready, ACT.Gelu, [h[:, :] for h in hidden])
    norm, turn = Norm(st), Turn(st, ring)
    affine = st.sem("affine")
    for b in range(nb):
        for n in range(b * NT, (b + 1) * NT, 4):
            v = experts(xc[:, n * P:n * P + BANK], lambda e, i: gates[:, n + i, e:e + 1],
                        lambda i: gate_row[:, (n + i) * P:(n + i + 1) * P], gates_ready, rows_ready,
                        x1[:, n:n + 4, :], x1[:, n:n + 4, :], [])
        tiles = slice(b * NT, (b + 1) * NT)
        v = norm(x1[:, tiles, :], x1[:, tiles, :], [v])
        st.dve.wait(v, small_ready)
        v = st.dve(nc.vector.tensor_tensor, x1[:, tiles, :], x1[:, tiles, :], spread(g2[:, :], NT),
                   ALU.mult, sig=affine)
        st.dve.wait(v)
        v = st.dve(nc.vector.tensor_tensor, x1[:, tiles, :], x1[:, tiles, :], spread(be2[:, :], NT),
                   ALU.add, sig=affine)
        st.dve.wait(v)
        v = st.dve(nc.vector.tensor_tensor, x[:, tiles, :], x[:, tiles, :], x1[:, tiles, :],
                   ALU.add, sig=affine)
        v = norm(x[:, tiles, :], x[:, tiles, :], [v])
        for n in range(b * NT, (b + 1) * NT, 4):
            turn(x[:, n:n + 4, :], xc[:, n * P:n * P + BANK], [v])
    st.run()


WIDE = 64
PAIRS = H // 2


def wide_attention(core):
    st = Stage(core, "wide")
    nc, inp, const, nb = core.nc, core.inp, core.const, core.n_batch
    x, xc = core.x_tok, core.x_chn
    banks = st.psum("p", 8)
    score_banks = [banks[:, 0:2, :], banks[:, 2:4, :]]
    out = banks[:, 4:6, :]
    side = Ring([banks[:, 6:8, :]])
    loaded = st.sem("loaded")
    wide_w = {n: core.big[:, i * 8 * C:(i + 1) * 8 * C] for i, n in enumerate("qkvo")}
    for n in "qkv":
        st.load(wide_w[n], inp[f"L3_attn_W{n}_t"][:, :], loaded)
    w_o = wide_w["o"].rearrange("p (m c) -> p m c", c=C)
    st.load(w_o, inp["L3_attn_Wo_t"].rearrange("(m p) c -> p m c", p=P), loaded)
    bq, bk = st.sbuf("bq", [P, PAIRS]), st.sbuf("bk", [P, PAIRS])
    st.load(bq[:, :], inp["L3_attn_bq_c"][:, :], loaded)
    st.load(bk[:, :], inp["L3_attn_bk_c"][:, :], loaded)
    scale = st.sbuf("scale", [P, PAIRS])
    two_heads = inp["L3_attn_adaptive_scale_c"]
    own = [slice(a * WIDE, (a + 1) * WIDE) for a in range(2)]
    other = own[::-1]
    max_row = [WIDE, 0]
    for a in range(2):
        st.load(scale[own[a], :], two_heads[a:a + 1, :].broadcast_to([WIDE, PAIRS]), loaded)
    bv, _ = broadcast_rows(st, "bv", inp["L3_attn_bv"], H * WIDE, loaded)
    bo, _ = broadcast_rows(st, "bo", inp["L3_attn_bo"], C, loaded)
    gamma, _ = broadcast_rows(st, "gamma", inp["L3_attn_gamma"], C, loaded)
    beta, ready = broadcast_rows(st, "beta", inp["L3_attn_beta"], C, loaded)
    st.dve.wait(ready)
    scaled = st.dve(nc.vector.tensor_scalar, scale[:, :], scale[:, :], WIDE ** -0.5, None,
                    ALU.mult, sig=st.sem("scaled"))
    q_pad = [[st.sbuf(f"q_pad{i}{a}", [P, T]) for a in range(2)] for i in range(2)]
    k_pad = [[st.sbuf(f"k_pad{i}{a}", [P, T]) for a in range(2)] for i in range(2)]
    q_bf = [st.sbuf(f"q_bf{a}", [P, T], BF16) for a in range(2)]
    k_bf = st.sbuf("k_bf", [P, T], BF16)
    v_tok = [st.sbuf(f"v_tok{i}", [P, NT, C]) for i in range(2)]
    zeroed = st.sem("zeroed")
    for a in range(2):
        st.pool(nc.gpsimd.memset, q_bf[a][other[a], :], 0.0, sig=zeroed)
        for i in range(2):
            st.pool(nc.gpsimd.memset, q_pad[i][a][other[a], :], 0.0, sig=zeroed)
            zero = st.pool(nc.gpsimd.memset, k_pad[i][a][other[a], :], 0.0, sig=zeroed)
    st.pool.wait(zero)
    for a in range(2):
        for i in range(2):
            row = slice(max_row[a], max_row[a] + 1)
            zero = st.pool(nc.gpsimd.memset, k_pad[i][a][row, :], 1.0, sig=zeroed)
    E_BUFS = 4
    exps = [core.attn_w[:, i * T:(i + 1) * T] for i in range(E_BUFS)]
    acc = [core.big[:, (4 + a) * T:(5 + a) * T] for a in range(2)]
    sums = core.big[:, 6 * T:7 * T]
    att = st.sbuf("att", [P, PAIRS, T])
    neg_max = st.sbuf("neg_max", [P, 2 * NT])
    max_rows = st.sbuf("max_rows", [2 * NT, P])
    projected, q_kept, k_kept, v_kept, cast = (st.sem(n) for n in (
        "projected", "q_kept", "k_kept", "v_kept", "cast"))
    max_scored, maxed, max_turned, rows_kept, row_sent = (st.sem(n) for n in (
        "max_scored", "maxed", "max_turned", "rows_kept", "row_sent"))
    scored, exped, summed, weighted, out_kept = (st.sem(n) for n in (
        "scored", "exped", "summed", "weighted", "out_kept"))
    total, sums_kept, inverted, divided = (st.sem(n) for n in (
        "total", "sums_kept", "inverted", "divided"))
    units = [(b, m) for b in range(nb) for m in range(PAIRS)]
    TILES = 2 * NT
    ADDS = 2 * (NT - 1)

    def two(ap):
        return ap.rearrange("p (h t) -> p h t", h=HALF)

    def project_q(u):
        b, m = units[u]
        slot, bank, emptied = side.take()
        st.pe.wait(*emptied, ready)
        for half in range(HALF):
            st.pe(nc.tensor.matmul, bank[:, half, :], wide_w["q"][:, m * P:(m + 1) * P],
                  xc[:, b * T + half * BANK:b * T + (half + 1) * BANK], start=True, stop=True,
                  sig=projected)
        st.dve.wait(projected.at(12 * u + 2), scaled, scored.at(TILES * (u - 1)))
        for a in range(2):
            st.dve(nc.vector.tensor_scalar, two(q_pad[u % 2][a][own[a], :]), bank[own[a], :, :],
                   bq[own[a], m:m + 1], scale[own[a], m:m + 1], ALU.add, ALU.mult, sig=q_kept)
        side.done[slot] = [q_kept.at(2 * u + 2)]
        st.act.wait(q_kept.at(2 * u + 2), max_scored.at(TILES * u))
        for a in range(2):
            st.act(nc.scalar.copy, q_bf[a][own[a], :], q_pad[u % 2][a][own[a], :], sig=cast)

    def project_k(u):
        b, m = units[u]
        slot, bank, emptied = side.take()
        st.pe.wait(*emptied)
        for half in range(HALF):
            st.pe(nc.tensor.matmul, bank[:, half, :], wide_w["k"][:, m * P:(m + 1) * P],
                  xc[:, b * T + half * BANK:b * T + (half + 1) * BANK], start=True, stop=True,
                  sig=projected)
        st.act.wait(projected.at(12 * u + 4), ready, scored.at(TILES * (u - 1)))
        for a in range(2):
            st.act(nc.scalar.activation, two(k_pad[u % 2][a][own[a], :]), bank[own[a], :, :],
                   ACT.Identity, bias=bk[own[a], m:m + 1], sig=k_kept)
        st.act.wait(max_scored.at(TILES * u))
        st.act(nc.scalar.activation, two(k_bf[:, :]), bank, ACT.Identity, bias=bk[:, m:m + 1],
               sig=cast)
        side.done[slot] = [cast.at(3 * u + 3)]

    def project_v(u):
        b, m = units[u]
        pair = slice(m * P, (m + 1) * P)
        slot, bank, emptied = side.take()
        st.pe.wait(*emptied)
        for n in range(NT):
            st.pe(nc.tensor.matmul, bank[:, n // 4, (n % 4) * P:(n % 4 + 1) * P],
                  xc[:, b * T + n * P:b * T + (n + 1) * P], wide_w["v"][:, pair], start=True,
                  stop=True, sig=projected)
        st.dve.wait(projected.at(12 * u + 12), weighted.at(NT * (u - 1)))
        st.dve(nc.vector.tensor_tensor, v_tok[u % 2][:, :, :],
               bank.rearrange("p a (n c) -> p (a n) c", c=C), spread(bv[:, pair], NT), ALU.add,
               sig=v_kept)
        side.done[slot] = [v_kept.at(u + 1)]

    def maximum(u, t):
        a, n = t // NT, t % NT
        slot, bank, emptied = side.take()
        st.pe.wait(*emptied, cast.at(3 * u + 3), zero)
        for half in range(HALF):
            st.pe(nc.tensor.matmul, bank[:, half, :], q_bf[a][:, n * P:(n + 1) * P],
                  k_bf[:, half * BANK:(half + 1) * BANK], start=True, stop=True,
                  sig=max_scored if half == HALF - 1 else None)
        st.dve.wait(max_scored.at(TILES * u + t + 1), max_turned.at(u))
        st.dve(nc.vector.tensor_reduce, neg_max[:, t:t + 1], bank, AX.XY, ALU.max, negate=True,
               sig=maxed)
        side.done[slot] = [maxed.at(TILES * u + t + 1)]

    def send_maxima(u):
        slot, bank, emptied = side.take()
        st.pe.wait(*emptied)
        st.pe(nc.tensor.transpose, bank[0:2 * NT, 0, 0:P], neg_max[:, :], core.ident[:, :],
              sig=max_turned)
        st.dve.wait(max_turned.at(u + 1), row_sent.at(32 * u))
        st.dve(nc.vector.tensor_copy, max_rows[:, :], bank[0:2 * NT, 0, 0:P], sig=rows_kept)
        side.done[slot] = [rows_kept.at(u + 1)]
        st.sp.wait(rows_kept.at(u + 1), scored.at(TILES * (u - 1)), zero)
        for a in range(2):
            row = slice(max_row[a], max_row[a] + 1)
            st.load(q_pad[u % 2][a][row, :].rearrange("o (n t) -> o n t", t=P),
                    max_rows[a * NT:(a + 1) * NT, :], row_sent)

    def score(u, kb, a):
        i, t = u % 2, TILES * u + 2 * kb + a
        bank, e = score_banks[t % 2], exps[t % E_BUFS]
        st.pe.wait(q_kept.at(2 * u + 2), k_kept.at(2 * u + 2), row_sent.at(32 * (u + 1)), zero)
        st.pe.wait(exped.at(t - 1))
        for half in range(HALF):
            st.pe(nc.tensor.matmul, bank[:, half, :], k_pad[i][a][:, kb * P:(kb + 1) * P],
                  q_pad[i][a][:, half * BANK:(half + 1) * BANK], start=True, stop=True,
                  sig=scored if half == HALF - 1 else None)
        before = t - E_BUFS
        bu, bkb = before // TILES, before % TILES // 2
        st.act.wait(scored.at(t + 1), weighted.at(NT * bu + bkb + 1),
                    summed.at(ADDS * bu + 2 * max(bkb - 1, 0) + before % 2 + 1))
        st.act(nc.scalar.activation, two(e), bank, ACT.Exp, sig=exped)

    def add(t):
        u, kb, a = t // TILES, t % TILES // 2, t % 2
        if kb == 0:
            return
        st.dve.wait(exped.at(t + 1))
        if kb == 1:
            st.dve.wait(total.at(u))
            first = exps[(t - 2) % E_BUFS]
        else:
            st.dve.wait(summed.at(ADDS * u + 2 * (kb - 2) + a + 1))
            first = acc[a]
        st.dve(nc.vector.tensor_tensor, acc[a], first, exps[t % E_BUFS], ALU.add, sig=summed)

    def weigh(u, kb):
        t = TILES * u + 2 * kb
        st.pe.wait(exped.at(t + 2), v_kept.at(u + 1), out_kept.at(u))
        for half in range(HALF):
            for a in range(2):
                last = half == HALF - 1 and a == 1
                st.pe(nc.tensor.matmul, out[own[a], half, :], v_tok[u % 2][:, kb, own[a]],
                      exps[(t + a) % E_BUFS][:, half * BANK:(half + 1) * BANK], start=kb == 0,
                      stop=kb == NT - 1, sig=weighted if last else None)

    def take_sums(u):
        b, m = units[u]
        st.act.wait(weighted.at(NT * (u + 1)), att_used[b])
        st.act(nc.scalar.copy, two(att[:, m, :]), out, sig=out_kept)
        slot, bank, emptied = side.take()
        st.pe.wait(*emptied, summed.at(ADDS * (u + 1)), core.const_ready)
        for half in range(HALF):
            for a in range(2):
                last = half == HALF - 1 and a == 1
                st.pe(nc.tensor.matmul, bank[own[a], half, :], core.ones[:, 0:WIDE],
                      acc[a][:, half * BANK:(half + 1) * BANK], start=True, stop=True,
                      sig=total if last else None)
        st.act.wait(total.at(u + 1), divided.at(u))
        st.act(nc.scalar.copy, two(sums), bank, sig=sums_kept)
        side.done[slot] = [sums_kept.at(u + 1)]

    def invert(u, piece):
        cols = slice(piece * P, (piece + 1) * P)
        st.dve.wait(sums_kept.at(u + 1))
        st.dve(nc.vector.reciprocal, sums[:, cols], sums[:, cols], sig=inverted)

    def divide(u):
        b, m = units[u]
        st.pool.wait(out_kept.at(u + 1), inverted.at(NT * (u + 1)))
        st.pool(nc.gpsimd.tensor_tensor, att[:, m, :], att[:, m, :], sums, ALU.mult, sig=divided)
        if m == PAIRS - 1:
            finish(b)

    one_bank = FirstBank(side)
    rows, norm, turn = Rows(st, one_bank), Norm(st), Turn(st, one_bank)
    mid = st.sbuf("mid", [P, NT, C])
    affine = st.sem("affine")
    att_used = [None]

    def finish(b):
        tiles = slice(b * NT, (b + 1) * NT)
        st.dve.wait(affine.at(3 * b))
        for n in range(0, NT, 4):
            y = rows(lambda k, m: att[:, k, (n + m) * P:(n + m + 1) * P], lambda k: w_o[:, k, :],
                     bo[:, :], x[:, b * NT + n:b * NT + n + 4, :], mid[:, n:n + 4, :],
                     [divided.at(PAIRS * (b + 1))], n_k=PAIRS)
        att_used.append(y)
        norm(mid[:, :, :], mid[:, :, :], [y])
        st.dve.wait(norm.last)
        st.dve(nc.vector.tensor_tensor, mid[:, :, :], mid[:, :, :], spread(gamma[:, :], NT),
               ALU.mult, sig=affine)
        st.dve.wait(affine.at(3 * b + 1))
        st.dve(nc.vector.tensor_tensor, mid[:, :, :], mid[:, :, :], spread(beta[:, :], NT),
               ALU.add, sig=affine)
        st.dve.wait(affine.at(3 * b + 2))
        st.dve(nc.vector.tensor_tensor, x[:, tiles, :], x[:, tiles, :], mid[:, :, :], ALU.add,
               sig=affine)
        v = norm(x[:, tiles, :], x[:, tiles, :], [affine.at(3 * b + 3)])
        for n in range(b * NT, (b + 1) * NT, 4):
            turn(x[:, n:n + 4, :], xc[:, n * P:n * P + BANK], [v])

    project_q(0), project_k(0), project_v(0)
    for t in range(TILES):
        maximum(0, t)
    send_maxima(0)
    FIRST_MAX = 3
    for u in range(len(units)):
        ahead = u + 1 < len(units)
        todo = list(range(TILES)) if ahead else []
        for step in range(TILES):
            kb, a = step // 2, step % 2
            if ahead and step in (0, 1, 2):
                (project_q, project_k, project_v)[step](u + 1)
            if todo and step >= FIRST_MAX:
                maximum(u + 1, todo.pop(0))
            score(u, kb, a)
            if step:
                add(TILES * u + step - 1)
            if todo and step >= FIRST_MAX and len(todo) > TILES - 2 - step:
                maximum(u + 1, todo.pop(0))
            if ahead and not todo and step == TILES - 2:
                send_maxima(u + 1)
            if a == 1 and kb:
                weigh(u, kb - 1)
            elif a == 1 and u:
                weigh(u - 1, NT - 1)
                take_sums(u - 1)
            if u and 2 <= step < 2 + NT:
                invert(u - 1, step - 2)
            if u and step == 2 + NT:
                divide(u - 1)
        add(TILES * u + TILES - 1)
    weigh(len(units) - 1, NT - 1)
    take_sums(len(units) - 1)
    for piece in range(NT):
        invert(len(units) - 1, piece)
    divide(len(units) - 1)
    st.run()


ENTMAX_ITER = 25
GATE_FLOOR = 1e-9


def entmax(st, logits, gates, n_tiles, after):
    nc, n = st.nc, E2
    s = st.sem("entmax")
    xs, diff, power, p = (st.sbuf(f"ent_{i}", [P, n_tiles, n]) for i in ("x", "diff", "power", "p"))
    low, width, mid, f_low, f, keep = (st.sbuf(f"ent_{i}", [P, n_tiles]) for i in (
        "low", "width", "mid", "f_low", "f", "keep"))
    high = st.sbuf("ent_high", [P, n_tiles])

    def dve(method, *args, **kw):
        nonlocal v
        st.dve.wait(v)
        v = st.dve(method, *args, sig=s, **kw)

    def mass(tau, out):
        dve(nc.vector.tensor_tensor, diff[:, :, :], xs[:, :, :], along(tau[:, :], n), ALU.subtract)
        dve(nc.vector.scalar_tensor_tensor, power[:, :, :], diff[:, :, :], 0.0, diff[:, :, :],
            ALU.max, ALU.mult)
        dve(nc.vector.tensor_reduce, out[:, :], power[:, :, :], AX.X, ALU.add)

    v = after
    dve(nc.vector.tensor_scalar, xs[:, :, :], logits, 0.5, None, ALU.mult)
    dve(nc.vector.tensor_reduce, high[:, :], xs[:, :, :], AX.X, ALU.max)
    dve(nc.vector.tensor_scalar, low[:, :], high[:, :], 1.0, None, ALU.subtract)
    dve(nc.vector.tensor_scalar, high[:, :], high[:, :], (1.0 / n) ** 0.5, None, ALU.subtract)
    dve(nc.vector.tensor_tensor, width[:, :], high[:, :], low[:, :], ALU.subtract)
    mass(low, f_low)
    dve(nc.vector.tensor_scalar, f_low[:, :], f_low[:, :], 1.0, None, ALU.subtract)
    for _ in range(ENTMAX_ITER):
        dve(nc.vector.tensor_scalar, width[:, :], width[:, :], 0.5, None, ALU.mult)
        dve(nc.vector.tensor_tensor, mid[:, :], low[:, :], width[:, :], ALU.add)
        mass(mid, f)
        dve(nc.vector.scalar_tensor_tensor, f[:, :], f[:, :], 1.0, f_low[:, :], ALU.subtract,
            ALU.mult)
        dve(nc.vector.tensor_scalar, keep[:, :], f[:, :], 0.0, None, ALU.is_ge)
        dve(nc.vector.copy_predicated, low[:, :], keep[:, :].bitcast(mybir.dt.uint32), mid[:, :])
    mass(mid, f)
    dve(nc.vector.reciprocal, f[:, :], f[:, :])
    dve(nc.vector.tensor_tensor, p[:, :, :], power[:, :, :], along(f[:, :], n), ALU.mult)
    dve(nc.vector.scalar_tensor_tensor, gates, p[:, :, :], GATE_FLOOR, p[:, :, :], ALU.is_gt,
        ALU.mult)
    return v


def entmax_experts(core):
    st = Stage(core, "moe3")
    nc, inp, nb = core.nc, core.inp, core.n_batch
    x, xc, acc = core.x_tok, core.x_chn, core.x_mid
    n_tiles = nb * NT
    small_banks = st.psum("small", 3)
    ring = Ring([small_banks[:, i, :] for i in range(3)])
    st.routed = st.sem("routed")
    loaded = st.sem("loaded")
    w_router = st.sbuf("w_router", [P, E2])
    st.load(w_router[:, :], inp["L3_ffn_Wr"][:, :], loaded)
    router_bias, small_ready = broadcast_rows(st, "router_bias", inp["L3_ffn_br"], E2, loaded)
    w1, w2, b1, b2, w_ready = load_experts(st, core, "L3_ffn", None)
    logits, gates = st.sbuf("logits", [P, n_tiles, E2]), st.sbuf("gates", [P, n_tiles, E2])
    gate_row = st.sbuf("gate_row", [E2, nb * T])
    v = router(st, ring, w_router[:, :], router_bias[:, :], xc, n_tiles, E2, logits[:, :, :],
               st.sem("logits_done"), [small_ready])
    gates_ready = entmax(st, logits[:, :, :], gates[:, :, :], n_tiles, v)
    rows_ready = gate_rows_of(st, ring, gates, gate_row, n_tiles, E2, [gates_ready])
    hidden = [st.sbuf(f"hidden{i}", [P, BANK]) for i in range(8)]
    experts = Experts(st, w1, w2, b1, b2[:, :], w_ready, ACT.Relu, [h[:, :] for h in hidden])
    norm = Norm(st)
    stored = st.sem("stored")
    for b in range(nb):
        for n in range(b * NT, (b + 1) * NT, 4):
            v = experts(xc[:, n * P:n * P + BANK], lambda e, i: gates[:, n + i, e:e + 1],
                        lambda i: gate_row[:, (n + i) * P:(n + i + 1) * P], gates_ready, rows_ready,
                        acc[:, n:n + 4, :], x[:, n:n + 4, :], [])
        tiles = slice(b * NT, (b + 1) * NT)
        v = norm(acc[:, tiles, :], x[:, tiles, :], [v])
    st.run()


def constants():
    bf16 = np.dtype("bfloat16")
    f = np.float32
    c = {"ident": np.eye(P, dtype=f), "ones": np.ones((P, P), f),
         "flip": np.ascontiguousarray(np.eye(P, dtype=f)[::-1])}
    tok_block = np.arange(T) // P
    rows = np.zeros((STACK - STACK_QK, GROUP, T), f)
    for s in range(SPLITS):
        for j in range(NT):
            rows[s * NT + j] = tok_block == j
    rows[STACK_FAR:] = 1.0
    c["key_rows"] = rows.astype(bf16)
    c["zero_rows"] = np.zeros((STACK_FAR, H, T), bf16)
    d = np.arange(ROW) - (P - 1)
    rp = np.maximum(d, 0)
    exact = N_BUCKETS // 2
    big = exact + (np.log(np.maximum(rp, 1).astype(f) / f(exact)) / f(np.log(MAX_DISTANCE / exact))
                   * f(N_BUCKETS - exact)).astype(np.int32)
    bucket = np.where(rp < exact, rp, np.minimum(big, N_BUCKETS - 1))
    hot = np.zeros((N_BUCKETS, 2, ROW), f)
    hot[bucket, 0, np.arange(ROW)] = 1.0
    back = np.arange(ROW)
    at = 2 * P - 1 - back + (P - 1)
    ok = at >= 0
    hot[bucket[np.maximum(at, 0)][ok], 1, back[ok]] = 1.0
    c["bucket_hot"] = hot
    part = np.arange(STACK_FAR) // NT
    key = np.arange(STACK_FAR) % NT
    c["far_level"] = np.stack([part > 0, part > 1], 1).astype(f)
    place = np.zeros((STACK_FAR, 2, NT), f)
    for n in range(NT):
        place[:, 0, n] = n < key
        place[:, 1, n] = n >= key + 2
    c["far_place"] = place
    i = np.arange(P)
    head, chan = i // HD, i % HD
    same = head[:, None] == head[None, :]
    c["same_head"] = same.astype(f)
    v = np.arange(HD)[None, :, None]
    c["pick_v"] = (same[:, None, :] & (chan[:, None, None] == v)).astype(f)
    c["place_v"] = (same[:, None, :] & (chan[None, None, :] == v)).astype(f)
    gate = np.zeros((2 * H, 2, C), f)
    for n in range(2):
        gate[n * H + head, n, i] = 1.0
    c["gate_rows"] = gate
    pair = np.zeros((E1, E1 // 2, P), f)
    for e in range(E1):
        pair[e, e // 2, (e % 2) * I1:(e % 2 + 1) * I1] = 1.0
    c["pair_rows"] = pair
    rotate = np.zeros((P, C), f)
    half = HD // 2
    low = i[chan < half]
    rotate[low + half, low] = -1.0
    rotate[low, low + half] = 1.0
    c["rotate"] = rotate
    freq = f(1.0) / f(10000.0) ** (np.arange(0, HD, 2, dtype=f) / f(HD))
    turn = np.arange(T, dtype=f)[:, None] * freq[None, :].astype(f)
    turn = np.concatenate([turn, turn], axis=-1)[:, chan].T
    c["angle"] = np.stack([np.cos(turn), np.sin(turn)], 1).astype(f)
    c["head_rows"] = (np.arange(2)[:, None] == i[None, :] // WIDE).astype(f)
    for n in (8, E1):
        c[f"ramp{n}"] = np.tile(np.arange(n, 0, -1, dtype=f), (P, 1))
    strip = np.zeros((P, BANK), f)
    strip[:, BANK - P:] = np.where(i[None, :] > i[:, None], f(-1e30), f(0))
    c["causal_strip"] = strip
    c["causal_mask"] = np.where(i[:, None] > i[None, :], f(-1e30), f(0)).astype(bf16)
    return c


def build(nc, inp, const, out, n_batch, upto=99):
    core = Core()
    core.nc, core.inp, core.const, core.n_batch = nc, inp, const, n_batch
    with ExitStack() as ctx:
        def sbuf(name, shape, dtype=F32):
            return ctx.enter_context(nc.sbuf_tensor(name, shape, dtype))

        def dram(name, shape, dtype=F32):
            return nc.dram_tensor(name, shape, dtype, kind="Internal").ap()

        names = iter(range(256))
        core.counts = []
        core.new_count = lambda: Count(ctx.enter_context(nc.semaphore(f"count{next(names)}")))
        core.x_tok = sbuf("x_tok", [P, n_batch * NT, C])
        core.x_chn = sbuf("x_chn", [P, n_batch * T])
        core.x_mid = None
        core.big = sbuf("big", [P, 2 * 4 * T])
        core.attn_w = sbuf("attn_w", [P, 4 * T])
        core.ident, core.ident_bf = sbuf("ident", [P, P]), sbuf("ident_bf", [P, P], BF16)
        core.flip, core.flip_bf = sbuf("flip", [P, P]), sbuf("flip_bf", [P, P], BF16)
        core.ones, core.eps = sbuf("ones", [P, P]), sbuf("eps", [P, 1])
        core.causal_strip = sbuf("causal_strip", [P, BANK])
        core.causal_mask = sbuf("causal_mask", [P, P], BF16)
        core.q_parts = dram("q_parts", (n_batch, SPLITS, C, T), BF16)
        core.k_parts = dram("k_parts", (n_batch, SPLITS, C, T), BF16)
        core.far_bias = dram("far_bias", (STACK_FAR, H, T), BF16)
        core.near_rev = dram("near_rev", (H, ROW))
        core.near_parts = dram("near_parts", (SPLITS, H, ROW), BF16)
        core.bias_stored = Count(ctx.enter_context(nc.semaphore("bias_stored")))

        st = Stage(core, "start")
        loaded, made = Count(ctx.enter_context(nc.semaphore("const_loaded"))), st.sem("made")
        for name, dst in (("ident", core.ident), ("ones", core.ones), ("flip", core.flip),
                          ("causal_strip", core.causal_strip), ("causal_mask", core.causal_mask)):
            t = st.load(dst[:, :], const[name][:, :], loaded)
        core.const_ready = core.ident_ready = t
        core.eps_ready = None
        st.pool(nc.gpsimd.memset, core.eps[:, :], LN_EPS, sig=made)
        st.act.wait(t)
        st.act(nc.scalar.copy, core.ident_bf[:, :], core.ident[:, :], sig=made)
        st.act.wait(t)
        st.act(nc.scalar.copy, core.flip_bf[:, :], core.flip[:, :], sig=made)
        st.run()

        stages = [position_bias, layer0, ternary_ffn, linear_attention, expert_ffn,
                  causal_attention, rotary_attention, block_experts, wide_attention,
                  entmax_experts]
        for n, stage in enumerate(stages):
            if n < upto:
                with ExitStack() as inner:
                    if stage is rotary_attention:
                        mid_ctx = ctx.enter_context(ExitStack())
                        core.x_mid = mid_ctx.enter_context(
                            nc.sbuf_tensor("x_mid", [P, n_batch * NT, C], F32))
                    if stage is entmax_experts:
                        core.x_mid = inner.enter_context(
                            nc.sbuf_tensor("x_sum", [P, n_batch * NT, C], F32))
                    stage(core)
                    if stage is block_experts:
                        mid_ctx.close()
        st = Stage(core, "end")
        stored = st.sem("stored")
        for b in range(n_batch):
            t = st.load(out[b].rearrange("(n p) c -> p n c", p=P),
                        core.x_tok[:, b * NT:(b + 1) * NT, :], stored)
        st.sp.wait(t)
        st.run()


def layout(inputs):
    out = {}
    for name, a in inputs.items():
        if name == "L0_ffn_weight":
            out["L0_ffn_weight_t"] = a.T
        elif name in ("L1_attn_W_qkv", "L1_attn_W_z", "L1_attn_W_b", "L1_attn_W_a",
                      "L1_attn_W_out", "L3_attn_Wq", "L3_attn_Wk", "L3_attn_Wv", "L3_attn_Wo"):
            out[name + "_t"] = a.T
        elif name in ("L2_attn_b_attn", "L3_attn_bq", "L3_attn_bk"):
            out[name + "_c"] = a.reshape(-1, P).T
        elif name == "L3_attn_adaptive_scale":
            out[name + "_c"] = a.reshape(-1, 2).T
        elif name in ("L2_ffn_b1", "L3_ffn_b1"):
            out[name + "_c"] = a.reshape(E2, -1, P).transpose(2, 0, 1)
        else:
            out[name] = a
    return out


def kernel(**inputs):
    from concourse import bacc
    from concourse.bass_utils import run_bass_kernel_spmd

    nc = bacc.Bacc("TRN2", target_bir_lowering=False, num_devices=1)
    n_batch = inputs["L0_attn_hidden_states"].shape[0]
    arrays, inp, const = {}, {}, {}
    for tensors, source, prefix in ((inp, layout(inputs), "in_"), (const, constants(), "const_")):
        for name, a in source.items():
            a = np.ascontiguousarray(a)
            arrays[prefix + name] = a
            tensors[name] = nc.dram_tensor(prefix + name, a.shape, mybir.dt.from_np(a.dtype),
                                           kind="ExternalInput").ap()
    out = nc.dram_tensor("out", (n_batch, T, C), F32, kind="ExternalOutput").ap()
    build(nc, inp, const, out, n_batch)
    r = run_bass_kernel_spmd(nc, [arrays], core_ids=[0])
    return r.results[0]["out"]
```

```python
from contextlib import ExitStack

import numpy as np
import concourse.bass as bass
from concourse import mybir

P = 128
T = 1024
C = 128
H = 16
NT = T // P
BANK = 512
HALF = T // BANK
LN_EPS = 1e-5

F32 = mybir.dt.float32
BF16 = mybir.dt.bfloat16
ALU = mybir.AluOpType
ACT = mybir.ActivationFunctionType
AX = mybir.AxisListType

SPLITS = 3
HD = C // H
STACK_QK = SPLITS * SPLITS * HD
STACK_FAR = SPLITS * NT
ROW_MAX = STACK_QK + STACK_FAR
STACK = ROW_MAX + 2
GROUP = 4
NEAR = 2 * P


class Count:

    def __init__(self, handle):
        self.handle, self.value, self.start = handle, 0, 0

    def at(self, n):
        return (self, self.start + n) if n > 0 else None


class Lane:

    def __init__(self):
        self.items, self.passed = [], {}

    def wait(self, *marks):
        for mark in marks:
            if mark is not None and self.passed.get(mark[0], 0) < mark[1]:
                self.passed[mark[0]] = mark[1]
                self.items.append((mark[0].handle, mark[1]))

    def __call__(self, method, *args, sig=None, step=1, **kw):
        self.items.append((method, args, kw, sig and sig.handle, step))
        if sig is None:
            return None
        sig.value += step
        return sig, sig.value

    def issue(self, engine):
        for item in self.items:
            if len(item) == 2:
                engine.wait_ge(*item)
                continue
            method, args, kw, sig, step = item
            instruction = method(*args, **kw)
            if sig is not None:
                instruction.then_inc(sig, step)


class Ring:

    def __init__(self, buffers):
        self.buffers, self.done, self.at = buffers, [[] for _ in buffers], -1

    def take(self):
        self.at = (self.at + 1) % len(self.buffers)
        return self.at, self.buffers[self.at], self.done[self.at]


class Core:
    pass


class Stage:

    def __init__(self, core, name):
        self.core, self.name, self.nc, self.ctx = core, name, core.nc, ExitStack()
        self.pe, self.act, self.dve, self.pool, self.sp = (Lane() for _ in range(5))
        self.counts = []

    def sbuf(self, name, shape, dtype=F32):
        return self.ctx.enter_context(self.nc.sbuf_tensor(f"{self.name}_{name}", shape, dtype))

    def psum(self, name, n):
        return self.ctx.enter_context(self.nc.psum_tensor(f"{self.name}_{name}", [P, n, BANK], F32))

    def sem(self, name):
        count = self.core.counts.pop() if self.core.counts else self.core.new_count()
        count.start = count.value
        self.counts.append(count)
        return count

    def load(self, out, in_, count):
        return self.sp(self.nc.sync.dma_start, out, in_, sig=count, step=16)

    def run(self):
        nc = self.nc
        with nc.Block() as block:
            @block.tensor
            def _(e):
                self.pe.issue(e)

            @block.scalar
            def _(e):
                self.act.issue(e)

            @block.vector
            def _(e):
                self.dve.issue(e)

            @block.gpsimd
            def _(e):
                self.pool.issue(e)

            @block.sync
            def _(e):
                self.sp.issue(e)
        self.core.counts += reversed(self.counts)
        self.ctx.close()


def banks4(bank):
    return bank.rearrange("p (n c) -> p n c", c=C)


def spread(ap, n):
    return ap[:, None, :].broadcast_to([ap.shape[0], n, ap.shape[1]])


def along(ap, n):
    return ap[:, :, None].broadcast_to([ap.shape[0], ap.shape[1], n])


class Norm:

    def __init__(self, st, tag=""):
        self.st = st
        self.stats = st.sbuf(f"stats{tag}", [P, NT, 6])
        self.mv = st.sbuf(f"mv{tag}", [P, NT, 2])
        self.std = st.sbuf(f"std{tag}", [P, NT])
        self.rstd = st.sbuf(f"rstd{tag}", [P, NT])
        self.n_stats = st.sem(f"n_stats{tag}")
        self.n_mv = st.sem(f"n_mv{tag}")
        self.n_std = st.sem(f"n_std{tag}")
        self.n_rstd = st.sem(f"n_rstd{tag}")
        self.n_out = st.sem(f"n_out{tag}")
        self.last = None

    def __call__(self, src, dst, after):
        st, nc, n = self.st, self.st.nc, src.shape[1]
        for i in range(n):
            st.dve.wait(*after, self.last)
            seen = st.dve(nc.vector.bn_stats, self.stats[:, i, :], src[:, i, :], sig=self.n_stats)
        for i in range(n):
            st.dve.wait((seen[0], seen[1] - n + 1 + i))
            mv = st.dve(nc.vector.bn_aggr, self.mv[:, i, :], self.stats[:, i, :], sig=self.n_mv)
        st.act.wait(mv, st.core.eps_ready)
        std = st.act(nc.scalar.activation, self.std[:, 0:n], self.mv[:, 0:n, 1], ACT.Sqrt,
                     bias=st.core.eps[:, 0:1], sig=self.n_std)
        st.dve.wait(std)
        rstd = st.dve(nc.vector.reciprocal, self.rstd[:, 0:n], self.std[:, 0:n],
                      sig=self.n_rstd)
        for i in range(n):
            st.dve.wait(rstd)
            out = st.dve(nc.vector.tensor_scalar, dst[:, i, :], src[:, i, :], self.mv[:, i, 0:1],
                         self.rstd[:, i:i + 1], ALU.subtract, ALU.mult,
                         sig=self.n_out)
        self.last = out
        return out


class Turn:

    def __init__(self, st, banks, tag=""):
        self.st, self.banks = st, banks
        self.turned = st.sem(f"turned{tag}")
        self.kept = st.sem(f"kept{tag}")

    def __call__(self, src, dst, after, copy_on="act"):
        st, nc = self.st, self.st.nc
        slot, bank, free = self.banks.take()
        for i in range(4):
            st.pe.wait(*after, *free, st.core.ident_ready)
            t = st.pe(nc.tensor.transpose, banks4(bank)[:, i, :], src[:, i, :], st.core.ident[:, :], sig=self.turned if i == 3 else None)
        if copy_on == "act":
            st.act.wait(t)
            kept = st.act(nc.scalar.copy, dst, bank, sig=self.kept)
        else:
            st.dve.wait(t)
            kept = st.dve(nc.vector.tensor_copy, dst, bank, sig=self.kept)
        self.banks.done[slot] = [kept]
        return kept


class SmallHeads:

    SLOTS = 3

    def __init__(self, st, per_unit, q_dram, k_dram, far_dram, near=None, strip=None, causal=False):
        self.st, self.q_dram, self.k_dram, self.far_dram = st, q_dram, k_dram, far_dram
        self.near, self.strip, self.causal = near, strip, causal
        self.scored, self.per_unit = st.sem("scored"), per_unit
        n = self.SLOTS
        self.q_stack = [st.sbuf(f"q_stack{i}", [STACK, GROUP, T], BF16) for i in range(n)]
        self.k_stack = [st.sbuf(f"k_stack{i}", [STACK, GROUP, T], BF16) for i in range(n)]
        self.loaded = [st.sem(f"stack_loaded{i}") for i in range(n)]
        self.max_row = [st.sem(f"max_row{i}") for i in range(n)]
        self.ready = [None] * n
        self.row_ready = [None] * n
        self.max_parts = st.sbuf("max_parts", [P, GROUP, NT, HALF])
        self.neg_max = st.sbuf("neg_max", [P, GROUP * NT])
        self.max_hi = st.sbuf("max_hi", [GROUP * NT, P], BF16)
        self.max_lo = st.sbuf("max_lo", [GROUP * NT, P], BF16)
        self.fixed = st.sem("fixed_rows")
        self.max_scored = st.sem("max_scored")
        self.maxed = st.sem("maxed")
        self.joined = st.sem("max_joined")
        self.turned = st.sem("max_turned")
        self.hi_kept = st.sem("max_hi_kept")
        self.lo_kept = st.sem("max_lo_kept")
        self.sent, self.to_send, self.last_unit = None, [], None
        for i in range(n):
            self.fixed_ready = st.load(self.k_stack[i][STACK_QK:STACK, :, :],
                                       st.core.const["key_rows"][:, :, :], self.fixed)
        self.last_joined = st.dve(st.nc.vector.memset, self.max_parts[:, :, :, :], -3e38,
                                  sig=self.joined)

    def fill(self, u, b, g, stored):
        st, i = self.st, u % self.SLOTS
        hs = slice(g * GROUP * HD, (g + 1) * GROUP * HD)
        st.sp.wait(self.scored.at(self.per_unit * (u - self.SLOTS + 1)), *stored)
        for s in range(SPLITS):
            q = self.q_dram[b, s, hs, :].rearrange("(h d) t -> d h t", d=HD)
            for r in range(SPLITS):
                row = (s * SPLITS + r) * HD
                k = self.k_dram[b, r, hs, :].rearrange("(h d) t -> d h t", d=HD)
                st.load(self.q_stack[i][row:row + HD, :, :], q, self.loaded[i])
                st.load(self.k_stack[i][row:row + HD, :, :], k, self.loaded[i])
        far = self.far_dram[:, g * GROUP:(g + 1) * GROUP, :]
        self.ready[i] = st.load(self.q_stack[i][STACK_QK:ROW_MAX, :, :], far, self.loaded[i])

    def maxima(self, u, ring):
        st, nc, i = self.st, self.st.nc, u % self.SLOTS
        q, k = self.q_stack[i], self.k_stack[i]

        def tile(j, n, half):
            width = min(BANK, (n + 1) * P - half * BANK) if self.causal else BANK
            slot, bank, free = ring.take()
            st.pe.wait(*free, self.ready[i], self.fixed_ready)
            scored = st.pe(nc.tensor.matmul, bank[:, 0:width], q[0:ROW_MAX, j, n * P:(n + 1) * P],
                           k[0:ROW_MAX, j, half * BANK:half * BANK + width], start=True, stop=True,
                           sig=self.max_scored)
            out = self.max_parts[:, j, n, half:half + 1]
            wait = [scored, self.last_joined]
            bias = None
            if self.strip is not None and n - 1 <= half * (BANK // P) + BANK // P - 1 \
                    and n >= half * (BANK // P):
                bias, more = self.strip(u, j, n, half)
                wait += more
            elif self.causal and half == n // (BANK // P):
                bias = st.core.causal_strip[:, BANK - width:BANK]
                wait.append(st.core.const_ready)
            if bias is None:
                st.dve.wait(*wait)
                maxed = st.dve(nc.vector.tensor_reduce, out, bank[:, 0:width], AX.X, ALU.max, sig=self.maxed)
            else:
                st.dve.wait(*wait)
                maxed = st.dve(nc.vector.tensor_tensor_reduce, bank[:, 0:width], bank[:, 0:width],
                               bias, 1.0, -3e38, ALU.add, ALU.max, out,
                               sig=self.maxed)
            ring.done[slot] = [maxed]
            self.last_maxed = maxed

        def join():
            st.dve.wait(self.last_maxed, self.turned.at(u))
            self.last_joined = st.dve(
                nc.vector.tensor_reduce, self.neg_max[:, :],
                self.max_parts[:, :, :, :].rearrange("p j n h -> p (j n) h"), AX.X, ALU.max,
                negate=True, sig=self.joined)

        def send():
            slot, bank, emptied = ring.take()
            st.pe.wait(*emptied, self.joined.at(u + 2))
            st.pe(nc.tensor.transpose, bank[0:GROUP * NT, 0:P], self.neg_max[:, :],
                  st.core.ident[:, :], sig=self.turned)
            st.dve.wait(self.turned.at(u + 1), self.sent)
            st.dve(nc.vector.tensor_copy, self.max_hi[:, :], bank[0:GROUP * NT, 0:P],
                   sig=self.hi_kept)
            st.dve.wait(self.hi_kept.at(u + 1))
            st.dve(nc.vector.tensor_tensor, self.max_lo[:, :], bank[0:GROUP * NT, 0:P],
                   self.max_hi[:, :], ALU.subtract, sig=self.lo_kept)
            ring.done[slot] = [self.lo_kept.at(u + 1)]
            st.sp.wait(self.lo_kept.at(u + 1))
            for row, part in ((ROW_MAX, self.max_hi), (ROW_MAX + 1, self.max_lo)):
                self.sent = st.load(q[row:row + 1, :, :].rearrange("o j (n t) -> o (j n) t", t=P),
                                    part[:, :], self.max_row[i])
            self.row_ready[i] = self.sent

        steps = []
        for j in range(GROUP):
            for n in range(NT):
                for half in range(HALF):
                    if not self.causal or half * BANK < (n + 1) * P:
                        steps.append((tile, (j, n, half)))
        if self.to_send:
            before(steps, 2, self.to_send.pop())
        f, a = steps[-1]
        steps[-1] = (lambda *args: (tile(*args), join()), a)
        if u == self.last_unit:
            steps.append((send, ()))
        else:
            self.to_send.append(send)
        return steps


def interleave(units, maxima, exps, lag):
    m_steps = [step for u in units for step in maxima(u)]
    per_m = len(m_steps) // len(units)
    e_steps = [(u, step) for u in units for step in exps(u)]
    per_e = len(e_steps) // len(units)
    at = 0
    for m, (f, args) in enumerate(m_steps):
        f(*args)
        while at < len(e_steps) and (at + per_e + lag) * per_m <= (m + 1) * per_e:
            f, args = e_steps[at][1]
            f(*args)
            at += 1
    for _, (f, args) in e_steps[at:]:
        f(*args)


def before(steps, at, work):
    def both(step):
        work()
        f, args = step
        f(*args)
    steps[at] = (both, (steps[at],))


class Projections:

    def __init__(self, st, ring, w, bias, w_ready, x_ready, rotary=None, values=None):
        self.st, self.ring, self.w, self.bias = st, ring, w, bias
        self.w_ready, self.x_ready, self.rotary, self.values = w_ready, x_ready, rotary, values
        self.scale = {"q": float(HD ** -0.5), "k": 1.0}
        self.dram = {"q": st.core.q_parts, "k": st.core.k_parts}
        self.value, self.rest, self.parts = ({n: st.sbuf(f"{name}_{n}", shape, kind) for n in "qk"}
                                             for name, shape, kind in (
            ("value", [P, T], F32), ("rest", [P, T], F32), ("parts", [P, SPLITS, T], BF16)))
        self.multiplied, self.kept, self.rotated, self.turned, self.cast, self.less, self.stored = (
            {n: st.sem(f"{name}_{n}") for n in "qk"} for name in (
                "multiplied", "kept", "rotated", "turned", "cast", "less", "stored"))
        self.v_multiplied, self.v_kept = st.sem("v_multiplied"), st.sem("v_kept")

    def pieces(self, b):
        out = []
        for n in "qk":
            out += [lambda n=n, half=half: self.project(n, b, half) for half in range(HALF)]
            if self.rotary:
                out += [lambda n=n, half=half: self.rotate(n, b, half) for half in range(HALF)]
            out += [lambda n=n, s=s: self.split(n, b, s) for s in range(SPLITS)]
        if self.values:
            out += [lambda half=half: self.value_rows(b, half) for half in range(HALF)]
        return out

    def project(self, n, b, half):
        st, nc, i = self.st, self.st.nc, HALF * b + half
        cols = slice(b * T + half * BANK, b * T + (half + 1) * BANK)
        slot, bank, emptied = self.ring.take()
        st.pe.wait(*emptied, self.w_ready, self.x_ready(b))
        st.pe(nc.tensor.matmul, bank, self.w[n], st.core.x_chn[:, cols], start=True, stop=True,
              sig=self.multiplied[n])
        st.dve.wait(self.multiplied[n].at(i + 1), self.less[n].at((SPLITS - 1) * (b - 1) + 1))
        st.dve(nc.vector.tensor_scalar, self.value[n][:, half * BANK:(half + 1) * BANK], bank,
               self.bias[n], self.scale[n], ALU.add, ALU.mult, sig=self.kept[n])
        self.ring.done[slot] = [self.kept[n].at(i + 1)]

    def rotate(self, n, b, half):
        st, nc, i = self.st, self.st.nc, HALF * b + half
        cols = slice(half * BANK, (half + 1) * BANK)
        value, t = self.value[n][:, cols], self.rest[n][:, cols]
        rotate, angle = self.rotary
        slot, bank, emptied = self.ring.take()
        st.pe.wait(*emptied, self.kept[n].at(i + 1))
        st.pe(nc.tensor.matmul, bank, rotate, value, start=True, stop=True, sig=self.rotated[n])
        st.dve.wait(self.rotated[n].at(i + 1), self.cast[n].at(SPLITS * b))
        st.dve(nc.vector.tensor_tensor, t, bank, angle[:, 1, cols], ALU.mult, sig=self.turned[n])
        self.ring.done[slot] = [self.turned[n].at(3 * i + 1)]
        st.dve(nc.vector.tensor_tensor, value, value, angle[:, 0, cols], ALU.mult,
               sig=self.turned[n])
        st.dve.wait(self.turned[n].at(3 * i + 2))
        st.dve(nc.vector.tensor_tensor, value, value, t, ALU.add, sig=self.turned[n])

    def split(self, n, b, s):
        st, nc = self.st, self.st.nc
        value, rest, parts = self.value[n][:, :], self.rest[n][:, :], self.parts[n]
        if s == 0:
            st.act.wait(self.turned[n].at(3 * HALF * (b + 1)) if self.rotary
                        else self.kept[n].at(HALF * (b + 1)), self.stored[n].at(16 * b))
            st.act(nc.scalar.copy, parts[:, s, :], value, sig=self.cast[n])
            return
        st.dve.wait(self.cast[n].at(SPLITS * b + s), self.less[n].at((SPLITS - 1) * b + s - 1))
        st.dve(nc.vector.tensor_tensor, rest, value if s == 1 else rest, parts[:, s - 1, :],
               ALU.subtract, sig=self.less[n])
        st.act.wait(self.less[n].at((SPLITS - 1) * b + s))
        st.act(nc.scalar.copy, parts[:, s, :], rest, sig=self.cast[n])
        if s == SPLITS - 1:
            st.sp.wait(self.cast[n].at(SPLITS * (b + 1)))
            st.load(self.dram[n][b].rearrange("s c t -> c s t"), parts[:, :, :], self.stored[n])

    def stored_of(self, b):
        return [self.stored[n].at(16 * (b + 1)) for n in "qk"]

    def value_rows(self, b, half):
        st, nc, i = self.st, self.st.nc, HALF * b + half
        w, bias, v_tok = self.values
        slot, bank, emptied = self.ring.take()
        st.pe.wait(*emptied, self.w_ready, self.x_ready(b))
        for m in range(4):
            tile = b * NT + half * 4 + m
            st.pe(nc.tensor.matmul, bank[:, m * C:(m + 1) * C],
                  st.core.x_chn[:, tile * P:(tile + 1) * P], w, start=True, stop=True,
                  sig=self.v_multiplied if m == 3 else None)
        st.dve.wait(self.v_multiplied.at(i + 1))
        st.dve(nc.vector.tensor_tensor, v_tok[:, 4 * i:4 * i + 4, :], banks4(bank), spread(bias, 4),
               ALU.add, sig=self.v_kept)
        self.ring.done[slot] = [self.v_kept.at(i + 1)]

    def v_ready(self, b):
        return self.v_kept.at(HALF * (b + 1))


class Weighted:

    W = 32

    def __init__(self, st, heads, score_banks, out_ring, small_ring, exps, v_tok, ctx):
        self.st, self.heads, self.v_tok, self.ctx = st, heads, v_tok, ctx
        self.score_banks, self.out_ring, self.small_ring = score_banks, out_ring, small_ring
        self.exps, self.n_tile, self.n_half = exps, 0, 0
        self.late = []
        self.v_one = [st.sbuf(f"v_one{i}", [P, NT, GROUP, self.W]) for i in range(2)]
        self.out_chn = [st.sbuf(f"out_chn{i}", [P, BANK]) for i in range(2)]
        self.r_sum = st.sbuf("r_sum", [P, 4 * GROUP])
        self.v_filled = st.sem("v_filled")
        self.scored = heads.scored
        self.exped = st.sem("exped")
        self.weighted = st.sem("weighted")
        self.kept = st.sem("out_kept")
        self.turned = st.sem("out_turned")
        self.inverted = st.sem("sum_inverted")
        self.context = st.sem("context")
        self.per_unit = HALF * NT * 2
        nc = st.nc
        for i in range(2):
            z = st.pool(nc.gpsimd.memset, self.v_one[i][:, :, :, :], 0.0, sig=self.v_filled)
            st.pool.wait(z)
            z = st.pool(nc.gpsimd.memset, self.v_one[i][:, :, :, HD:HD + 1], 1.0,
                        sig=self.v_filled)
        self.zeroed = z

    def steps(self, u, v_at, c_at, g, v_ready):
        st, nc, heads = self.st, self.st.nc, self.heads
        i, vs = u % heads.SLOTS, u % 2
        q, k, v = heads.q_stack[i], heads.k_stack[i], self.v_one[vs]
        pending = []

        def fill_values():
            st.pool.wait(self.zeroed, self.weighted.at(self.per_unit * (u - 1)), v_ready())
            self.filled = st.pool(
                nc.gpsimd.tensor_copy, v[:, :, :, 0:HD],
                self.v_tok()[:, v_at:v_at + NT, g * GROUP * HD:(g + 1) * GROUP * HD]
                .rearrange("p n (j d) -> p n j d", d=HD), sig=self.v_filled)

        def scores(half, kb, pair):
            if half == 0 and kb == 0 and pair == 0:
                fill_values()
            n = self.n_tile
            self.n_tile += 1
            banks = self.score_banks[n % 2]
            lo = max(kb * P, half * BANK)
            hi = min(kb * P + NEAR, (half + 1) * BANK)
            near = heads.near is not None and lo < hi
            st.pe.wait(heads.row_ready[i], heads.ready[i])
            st.pe.wait(self.exped.at(n - 1))
            for a in range(2):
                j = 2 * pair + a
                st.pe(nc.tensor.matmul, banks[:, a, :], k[0:STACK, j, kb * P:(kb + 1) * P],
                      q[0:STACK, j, half * BANK:(half + 1) * BANK], start=True, stop=not near,
                      sig=None if near or a == 0 else self.scored)
                if near:
                    bias, loaded = heads.near(u, j, lo - kb * P, hi - kb * P)
                    st.pe.wait(loaded)
                    for s in range(SPLITS):
                        last = s == SPLITS - 1
                        st.pe(nc.tensor.matmul, banks[:, a, lo - half * BANK:hi - half * BANK],
                              st.core.flip_bf[:, :], bias[s], start=False, stop=last,
                              sig=self.scored if last and a == 1 else None)
            st.act.wait(self.scored.at(n + 1), self.weighted.at(n + 1 - len(self.exps)))
            st.act(nc.scalar.activation, self.exps[n % len(self.exps)], banks, ACT.Exp,
                   sig=self.exped)
            if self.late:
                self.late.pop(0)()
            pending.append((kb, pair, n))
            if pair == 1 and kb > 0:
                weigh()
            if pair == 1 and kb == NT - 1:
                weigh()
                finish(half)

        def weigh():
            m = self.n_half
            out = self.out_ring.buffers[m % len(self.out_ring.buffers)]
            st.pe.wait(self.kept.at(m + 1 - len(self.out_ring.buffers)), self.filled)
            for _ in range(2):
                kb, pair, n = pending.pop(0)
                st.pe.wait(self.exped.at(n + 1))
                for a in range(2):
                    j = 2 * pair + a
                    st.pe(nc.tensor.matmul, out[self.W * j:self.W * (j + 1), :],
                          v[:, kb, j, :], self.exps[n % len(self.exps)][:, a, :], start=kb == 0,
                          stop=kb == NT - 1, sig=self.weighted if a == 1 else None)

        def finish(half):
            m = self.n_half
            self.n_half += 1
            out, chn = self.out_ring.buffers[m % len(self.out_ring.buffers)], self.out_chn[m % 2]
            st.dve.wait(self.weighted.at(NT * 2 * (m + 1)), self.turned.at(m - 1))
            st.dve(nc.vector.tensor_copy, chn[:, :], out, sig=self.kept)
            ctx = self.ctx()
            self.late.append(lambda: normalise(half, m, chn, ctx))

        def normalise(half, m, chn, ctx):
            tslot, bank, emptied = self.small_ring.take()
            st.pe.wait(*emptied)
            st.pe.wait(self.kept.at(m + 1))
            for n in range(4):
                st.pe(nc.tensor.transpose, banks4(bank)[:, n, :], chn[:, n * P:(n + 1) * P],
                      st.core.ident[:, :], sig=self.turned if n == 3 else None)
            rows = bank.rearrange("p (m w) -> p m w", w=self.W)
            st.dve.wait(self.turned.at(m + 1), self.context.at(4 * m))
            st.dve(nc.vector.reciprocal, self.r_sum[:, :], rows[:, :, HD], sig=self.inverted)
            at = c_at + half * (BANK // P)
            dst = ctx[:, at:at + 4, g * GROUP * HD:(g + 1) * GROUP * HD]
            st.dve.wait(self.inverted.at(m + 1))
            for n in range(4):
                st.dve(nc.vector.tensor_tensor, dst[:, n, :].rearrange("p (j d) -> p j d", d=HD),
                       rows[:, n * GROUP:(n + 1) * GROUP, 0:HD],
                       along(self.r_sum[:, n * GROUP:(n + 1) * GROUP], HD), ALU.mult,
                       sig=self.context)
            self.small_ring.done[tslot] = [self.context.at(4 * (m + 1))]

        return [(scores, (half, kb, pair)) for half in range(HALF) for kb in range(NT)
                for pair in range(2)]


class Rows:

    def __init__(self, st, ring, tag=""):
        self.st, self.ring = st, ring
        self.multiplied = st.sem(f"rows_multiplied{tag}")
        self.added = st.sem(f"rows_added{tag}")

    def __call__(self, chn, w, bias, residual, out, after, n_k=1):
        st, nc = self.st, self.st.nc
        slot, bank, free = self.ring.take()
        tiles = banks4(bank)
        for n in range(4):
            for k in range(n_k):
                st.pe.wait(*free, *after)
                mm = st.pe(nc.tensor.matmul, tiles[:, n, :], chn(k, n), w(k), start=k == 0,
                           stop=k == n_k - 1,
                           sig=self.multiplied if n == 3 and k == n_k - 1 else None)
        st.dve.wait(mm, *after)
        added = st.dve(nc.vector.tensor_tensor, out, tiles, residual, ALU.add,
                       sig=self.added)
        self.ring.done[slot] = [added]
        if bias is not None:
            st.dve.wait(added)
            added = st.dve(nc.vector.tensor_tensor, out, out, spread(bias, 4), ALU.add, sig=self.added)
        return added


N_BUCKETS = 32
MAX_DISTANCE = 64
BIAS_SCALE = 8.0
ROW = 3 * P


def position_bias(core):
    st = Stage(core, "bias")
    nc, const = core.nc, core.const
    ring = st.psum("p", 2)
    table = st.sbuf("table", [N_BUCKETS, H])
    hot = st.sbuf("hot", [N_BUCKETS, 2, ROW])
    level = st.sbuf("level", [STACK_FAR, 2])
    place = st.sbuf("place", [STACK_FAR, 2, NT])
    ends = st.sbuf("ends", [STACK_FAR, 2, H])
    part = st.sbuf("part", [STACK_FAR, 2, H], BF16)
    by_block = st.sbuf("by_block", [STACK_FAR, 2, H, NT])
    far_small = st.sbuf("far_small", [STACK_FAR, H, NT])
    far = st.sbuf("far", [STACK_FAR, H, T], BF16)
    near = st.sbuf("near", [H, 2, ROW])
    near_part = st.sbuf("near_part", [H, SPLITS, ROW], BF16)
    loaded, done, chain = st.sem("loaded"), st.sem("multiplied"), st.sem("chain")
    a_chain, stored = st.sem("a_chain"), core.bias_stored
    st.load(table[:, :], core.inp["L0_attn_rel_bias"][:, :], loaded)
    st.load(hot[:, :, :], const["bucket_hot"][:, :, :], loaded)
    st.load(level[:, :], const["far_level"][:, :], loaded)
    st.load(place[:, :, :], const["far_place"][:, :, :], loaded)
    rel = core.inp["L0_attn_rel_bias"]
    for e, row in enumerate((0, N_BUCKETS - 1)):
        t = st.load(ends[:, e, :], rel[row:row + 1, :].broadcast_to([STACK_FAR, H]), loaded)
    for e in range(2):
        st.pe.wait(t)
        mm = st.pe(nc.tensor.matmul, ring[0:H, e, 0:ROW], table[:, :], hot[:, e, :], start=True,
                   stop=True, sig=done)
    st.dve.wait(mm)
    v = st.dve(nc.vector.tensor_scalar, near[:, :, :], ring[0:H, :, 0:ROW], BIAS_SCALE, None,
               ALU.mult, sig=chain)
    st.sp.wait(v)
    st.load(core.near_rev[:, :], near[:, 1, :], stored)
    for s in range(SPLITS):
        st.dve.wait(v)
        v = st.dve(nc.vector.tensor_copy, near_part[:, s, :], near[:, 0, :], sig=chain)
        if s < SPLITS - 1:
            st.dve.wait(v)
            v = st.dve(nc.vector.tensor_tensor, near[:, 0, :], near[:, 0, :], near_part[:, s, :],
                       ALU.subtract, sig=chain)
    st.sp.wait(v)
    st.load(core.near_parts.rearrange("s h x -> h s x"), near_part[:, :, :], stored)
    st.dve.wait(t, v)
    v = st.dve(nc.vector.tensor_scalar, ends[:, :, :], ends[:, :, :], BIAS_SCALE, None, ALU.mult, sig=chain)
    for s in range(SPLITS - 1):
        st.dve.wait(v)
        v = st.dve(nc.vector.tensor_scalar, part[:, :, :], ends[:, :, :], level[:, s:s + 1], None,
                   ALU.mult, sig=chain)
        st.dve.wait(v)
        v = st.dve(nc.vector.tensor_tensor, ends[:, :, :], ends[:, :, :], part[:, :, :],
                   ALU.subtract, sig=chain)
    for e in range(2):
        st.dve.wait(v)
        v = st.dve(nc.vector.tensor_tensor, by_block[:, e, :, :], along(ends[:, e, :], NT),
                   spread(place[:, e, :], H), ALU.mult, sig=chain)
    st.dve.wait(v)
    v = st.dve(nc.vector.tensor_tensor, far_small[:, :, :], by_block[:, 0, :, :],
               by_block[:, 1, :, :], ALU.add, sig=chain)
    for n in range(2):
        hs = slice(n * H // 2, (n + 1) * H // 2)
        dst = far[:, hs, :].rearrange("p h (n t) -> p (h n) t", t=P)
        src = along(far_small[:, hs, :].rearrange("p h n -> p (h n)"), P)
        if n:
            st.dve.wait(v)
            f = st.dve(nc.vector.tensor_copy, dst, src, sig=chain)
        else:
            st.act.wait(v)
            f = st.act(nc.scalar.copy, dst, src, sig=a_chain)
        st.sp.wait(f)
        t = st.load(core.far_bias[:, hs, :], far[:, hs, :], stored)
    core.bias_ready = t
    st.sp.wait(t)
    st.run()


def broadcast_rows(st, name, src, n, count, lane=None):
    out = st.sbuf(name, [P, n])
    t = st.load(out[:, :], src.rearrange("(o n) -> o n", o=1).broadcast_to([P, n]), count)
    return out, t


def column(st, name, src, count):
    out = st.sbuf(name, [P, 1])
    t = st.load(out[:, :], src.rearrange("(p o) -> p o", o=1), count)
    return out, t


def near_window(handle, row):
    ap = handle[row]
    n = row.stop - row.start
    return bass.AP(tensor=ap.tensor, offset=ap.offset, ap=[[1, P], [ROW, n], [1, NEAR]])


def layer0(core):
    st = Stage(core, "l0")
    nc, inp, const = core.nc, core.inp, core.const
    nb = core.n_batch
    score_banks, small_banks, out_banks = st.psum("score", 4), st.psum("small", 3), st.psum("out", 1)
    score_pair = [score_banks[:, 0:2, :], score_banks[:, 2:4, :]]
    small_ring = Ring([small_banks[:, i, :] for i in range(3)])
    out_ring = Ring([out_banks[:, 0, :]])
    w_loaded = st.sem("w_loaded")
    w = {}
    for n in "qkvo":
        w[n] = st.sbuf(f"w{n}", [P, C])
        st.load(w[n][:, :], inp[f"L0_attn_W{n}"][:, :], w_loaded)
    bq, _ = column(st, "bq", inp["L0_attn_bq"], w_loaded)
    bk, _ = column(st, "bk", inp["L0_attn_bk"], w_loaded)
    bv, _ = broadcast_rows(st, "bv", inp["L0_attn_bv"], C, w_loaded)
    bo, w_ready = broadcast_rows(st, "bo", inp["L0_attn_bo"], C, w_loaded)
    x, xc = core.x_tok, core.x_chn
    x_loaded = [st.sem(f"x_loaded{b}") for b in range(nb)]
    turn = Turn(st, small_ring)
    x_ready = []
    for b in range(nb):
        t = st.load(x[:, b * NT:(b + 1) * NT, :],
                    inp["L0_attn_hidden_states"][b].rearrange("(n p) c -> p n c", p=P), x_loaded[b])
        for n in range(b * NT, (b + 1) * NT, 4):
            t2 = turn(x[:, n:n + 4, :], xc[:, n * P:n * P + BANK], [t])
        x_ready.append(t2)
    heads = SmallHeads(st, HALF * NT * 2, core.q_parts, core.k_parts, core.far_bias,
                       near=lambda u, j, lo, hi: near_of(u, j, lo, hi),
                       strip=lambda u, j, n, half: strip_of(u, j, n, half))
    v_tok, ctx_tok = core.big[:, 0:nb * T], core.big[:, nb * T:2 * nb * T]
    v_tok = v_tok.rearrange("p (n c) -> p n c", c=C)
    ctx_tok = ctx_tok.rearrange("p (n c) -> p n c", c=C)
    proj = Projections(st, small_ring, {n: w[n][:, :] for n in "qk"},
                       {"q": bq[:, 0:1], "k": bk[:, 0:1]}, w_ready, lambda b: x_ready[b],
                       values=(w["v"][:, :], bv[:, :], v_tok))
    for work in proj.pieces(0):
        work()
    strip = core.attn_w[:, 0:GROUP * T].rearrange("p (j x) -> p j x", x=T)
    strip_at = 3 * P
    near = [st.sbuf(f"near{i}", [P, SPLITS, GROUP, NEAR], BF16) for i in range(2)]
    strip_zero, strip_loaded = st.sem("strip_zero"), st.sem("strip_loaded")
    strip_flipped, strip_kept = st.sem("strip_flipped"), st.sem("strip_kept")
    raw = st.sbuf("raw", [P, BANK])
    near_loaded = [st.sem(f"near_loaded{i}") for i in range(2)]
    zero = st.pool(nc.gpsimd.memset, strip, 0.0, sig=strip_zero)
    units = [(g, b) for g in range(H // GROUP) for b in range(nb)]
    heads.last_unit = len(units) - 1
    near_ready = {}

    def load_strip(g):
        for half in range(HALF):
            flips = HALF * g + half + 1
            st.sp.wait(strip_flipped.at(flips - 1))
            first = g * GROUP + 2 * half
            st.load(raw[:, :].rearrange("p (j x) -> p j x", x=NEAR),
                    near_window(core.near_rev, slice(first, first + 2)), strip_loaded)
            slot, bank, emptied = small_ring.take()
            st.pe.wait(*emptied, strip_loaded.at(16 * flips))
            st.pe(nc.tensor.matmul, bank, core.flip[:, :], raw[:, :], start=True, stop=True,
                  sig=strip_flipped)
            st.act.wait(strip_flipped.at(flips), zero, heads.last_maxed if g else None)
            st.act(nc.scalar.copy, strip[:, 2 * half:2 * half + 2, strip_at:strip_at + NEAR],
                   bank.rearrange("p (j x) -> p j x", x=NEAR), sig=strip_kept)
            small_ring.done[slot] = [strip_kept.at(flips)]

    def load_near(g):
        for s in range(SPLITS):
            st.sp.wait(heads.scored.at(heads.per_unit * nb * (g - 1)))
            near_ready[g] = st.load(near[g % 2][:, s, :, :],
                                    near_window(core.near_parts[s],
                                                slice(g * GROUP, (g + 1) * GROUP)),
                                    near_loaded[g % 2])

    def near_of(u, j, lo, hi):
        g = units[u][0]
        return [near[g % 2][:, s, j, lo:hi] for s in range(SPLITS)], near_ready[g]

    def strip_of(u, j, n, half):
        g = units[u][0]
        at = BANK - n * P + half * BANK
        return strip[:, j, at:at + BANK], [strip_kept.at(HALF * (g + 1))]

    exps = [st.sbuf(f"exps{i}", [P, 2, BANK]) for i in range(4)]
    weighted = Weighted(st, heads, score_pair, out_ring, small_ring, [e[:, :, :] for e in exps],
                        lambda: v_tok, lambda: ctx_tok)

    def maxima(u):
        g, b = units[u]
        steps = heads.maxima(u, small_ring)

        def first(f, args):
            if b == 0:
                load_strip(g)
            if u == 0:
                heads.fill(0, b, g, proj.stored_of(b))
            f(*args)

        def ahead():
            if b == 0:
                load_near(g)
            if u + 1 < len(units):
                g2, b2 = units[u + 1]
                heads.fill(u + 1, b2, g2, proj.stored_of(b2))
        if g == 0 and b + 1 < nb:
            for i, work in enumerate(proj.pieces(b + 1)):
                before(steps, 2 + 3 * i, work)
        before(steps, 40 if g == 0 else 24, ahead)
        steps[0] = (first, steps[0])
        return steps

    interleave(range(len(units)), maxima,
               lambda u: weighted.steps(u, units[u][1] * NT, units[u][1] * NT, units[u][0],
                                        lambda: proj.v_ready(units[u][1])), lag=6)

    while weighted.late:
        weighted.late.pop(0)()
    ctx_chn = Ring(weighted.out_chn)
    turn_ctx = Turn(st, small_ring, "_ctx")
    rows, norm = Rows(st, small_ring), Norm(st)
    done = weighted.context.at(4 * HALF * len(units))
    for b in range(nb):
        for n in range(b * NT, (b + 1) * NT, 4):
            cslot, chn, free = ctx_chn.take()
            kept = turn_ctx(ctx_tok[:, n:n + 4, :], chn[:, :], [done] + free)
            y = rows(lambda k, m: chn[:, m * P:(m + 1) * P], lambda k: w["o"][:, :], bo[:, :],
                     x[:, n:n + 4, :], x[:, n:n + 4, :], [kept, w_ready])
            ctx_chn.done[cslot] = [y]
        tiles = slice(b * NT, (b + 1) * NT)
        out = norm(x[:, tiles, :], x[:, tiles, :], [y])
        for n in range(b * NT, (b + 1) * NT, 4):
            kept = turn(x[:, n:n + 4, :], xc[:, n * P:n * P + BANK], [out])
    st.run()


def ternary_ffn(core):
    st = Stage(core, "tern")
    nc, inp = core.nc, core.inp
    x, xc, nb = core.x_tok, core.x_chn, core.n_batch
    banks = st.psum("p", 4)
    ring = Ring([banks[:, i, :] for i in range(4)])
    loaded, chain, summed = st.sem("loaded"), st.sem("chain"), st.sem("summed")
    w = st.sbuf("w", [P, C])
    up, down, total, delta = (st.sbuf(n, s) for n, s in (("up", [P, C]), ("down", [P, C]),
                                                         ("total", [P, 1]), ("delta", [P, 2])))
    st.load(w[:, :], inp["L0_ffn_weight_t"][:, :], loaded)
    alpha = st.sbuf("alpha", [P, 1])
    st.load(alpha[:, :], inp["L0_ffn_alpha"].rearrange("(o n) -> o n", o=1).broadcast_to([P, 1]),
            loaded)
    bias, t = broadcast_rows(st, "bias", inp["L0_ffn_bias"], C, loaded)
    st.dve.wait(t)
    v = st.dve(nc.vector.tensor_reduce, total[:, :], w[:, :], AX.X, ALU.add,
               apply_absolute_value=True, sig=chain)
    slot, bank, free = ring.take()
    st.pe.wait(v, core.const_ready)
    mm = st.pe(nc.tensor.matmul, bank[:, 0:1], core.ones[:, :], total[:, :], start=True, stop=True, sig=summed)
    st.dve.wait(mm)
    v = st.dve(nc.vector.tensor_scalar, delta[:, 0:1], bank[:, 0:1], 1.0 / (C * C), 0.7, ALU.mult,
               ALU.mult, sig=chain)
    ring.done[slot] = [v]
    st.dve.wait(v)
    v = st.dve(nc.vector.tensor_scalar, delta[:, 1:2], delta[:, 0:1], -1.0, None, ALU.mult, sig=chain)
    st.dve.wait(v)
    v = st.dve(nc.vector.tensor_scalar, up[:, :], w[:, :], delta[:, 0:1], None, ALU.is_gt, sig=chain)
    st.dve.wait(v)
    v = st.dve(nc.vector.tensor_scalar, down[:, :], w[:, :], delta[:, 1:2], None, ALU.is_lt, sig=chain)
    st.dve.wait(v)
    v = st.dve(nc.vector.tensor_tensor, up[:, :], up[:, :], down[:, :], ALU.subtract,
               sig=chain)
    st.dve.wait(v)
    w_ready = st.dve(nc.vector.tensor_scalar, up[:, :], up[:, :], alpha[:, 0:1], None, ALU.mult, sig=chain)
    rows, norm, turn = Rows(st, ring), Norm(st), Turn(st, ring)
    for b in range(nb):
        for n in range(b * NT, (b + 1) * NT, 4):
            y = rows(lambda k, m: xc[:, (n + m) * P:(n + m + 1) * P], lambda k: up[:, :],
                     bias[:, :], x[:, n:n + 4, :], x[:, n:n + 4, :], [w_ready])
        tiles = slice(b * NT, (b + 1) * NT)
        out = norm(x[:, tiles, :], x[:, tiles, :], [y])
        for n in range(b * NT, (b + 1) * NT, 4):
            turn(x[:, n:n + 4, :], xc[:, n * P:n * P + BANK], [out])
    st.run()


TAPS = 4
LOG1P_TERMS = 9


def linear_attention(core):
    st = Stage(core, "lin")
    nc, inp, const, nb = core.nc, core.inp, core.const, core.n_batch
    x, xc = core.x_tok, core.x_chn
    work_banks, out_banks = st.psum("work", 6), st.psum("out", 2)
    pairs = Ring([work_banks[:, 2 * i:2 * i + 2, :] for i in range(3)])
    loaded = st.sem("loaded")
    w_qkv = st.sbuf("w_qkv", [P, 3 * C])
    w_z, w_out = st.sbuf("w_z", [P, C]), st.sbuf("w_out", [P, C])
    w_gate = st.sbuf("w_gate", [P, 2 * H])
    taps = st.sbuf("taps", [P, 3, TAPS])
    st.load(w_qkv[:, :], inp["L1_attn_W_qkv_t"][:, :], loaded)
    st.load(w_z[:, :], inp["L1_attn_W_z_t"][:, :], loaded)
    st.load(w_out[:, :], inp["L1_attn_W_out_t"][:, :], loaded)
    st.load(w_gate[:, 0:H], inp["L1_attn_W_b_t"][:, :], loaded)
    st.load(w_gate[:, H:2 * H], inp["L1_attn_W_a_t"][:, :], loaded)
    st.load(taps[:, :, :], inp["L1_attn_conv_w"].rearrange("(g p) o k -> p g (o k)", p=P), loaded)
    same_head = st.sbuf("same_head", [P, C])
    pick_v, place_v = st.sbuf("pick_v", [P, HD, C]), st.sbuf("place_v", [P, HD, C])
    gate_rows = st.sbuf("gate_rows", [2 * H, 2, C])
    st.load(same_head[:, :], const["same_head"][:, :], loaded)
    st.load(pick_v[:, :, :], const["pick_v"][:, :, :], loaded)
    st.load(place_v[:, :, :], const["place_v"][:, :, :], loaded)
    st.load(gate_rows[:, :, :], const["gate_rows"][:, :, :], loaded)
    dt_bias, _ = broadcast_rows(st, "dt_bias", inp["L1_attn_dt_bias"], H, loaded)
    a_log, ready = broadcast_rows(st, "a_log", inp["L1_attn_A_log"], H, loaded)
    ready = [ready, core.const_ready]
    small = st.sbuf("small", [P, 1])
    small_ready = st.pool(nc.gpsimd.memset, small[:, :], 1e-6, sig=st.sem("small_ready"))

    n_tiles = nb * NT
    gates = st.sbuf("gates", [P, n_tiles, 2 * H])
    z, e, s, s2, poly = (st.sbuf(n, [P, n_tiles, H]) for n in ("gz", "ge", "gs", "gs2", "gpoly"))
    rate = st.sbuf("rate", [P, H])
    g_mm, dv, av = st.sem("g_mm"), st.sem("g_dve"), st.sem("g_act")
    per_bank = BANK // (2 * H)
    slot, bank, free = pairs.take()
    flat = bank.rearrange("p a (n h) -> p (a n) h", h=2 * H)
    for n in range(n_tiles):
        st.pe.wait(*ready)
        mm = st.pe(nc.tensor.matmul, flat[:, n, :], xc[:, n * P:(n + 1) * P], w_gate[:, :],
                   start=True, stop=True, sig=g_mm)
    flat = flat[:, 0:n_tiles, :]
    st.dve.wait(mm, *ready)
    v = st.dve(nc.vector.tensor_tensor, z[:, :, :], flat[:, :, H:2 * H], spread(dt_bias[:, :], n_tiles),
               ALU.add, sig=dv)
    st.dve.wait(v)
    v = st.dve(nc.vector.scalar_tensor_tensor, s[:, :, :], z[:, :, :], -1.0, z[:, :, :], ALU.mult,
               ALU.max, sig=dv)
    st.act.wait(v)
    beta = st.act(nc.scalar.activation, gates[:, :, 0:H], flat[:, :, 0:H], ACT.Sigmoid, sig=av)
    pairs.done[slot] = [v, beta]
    st.act.wait(v)
    a = st.act(nc.scalar.activation, e[:, :, :], s[:, :, :], ACT.Exp, scale=-1.0, sig=av)
    r = st.act(nc.scalar.activation, rate[:, :], a_log[:, :], ACT.Exp, sig=av)
    st.dve.wait(a)
    v = st.dve(nc.vector.tensor_scalar, s[:, :, :], e[:, :, :], 2.0, None, ALU.add,
               sig=dv)
    st.dve.wait(v)
    v = st.dve(nc.vector.reciprocal, s[:, :, :], s[:, :, :], sig=dv)
    st.dve.wait(v)
    v = st.dve(nc.vector.tensor_tensor, s[:, :, :], s[:, :, :], e[:, :, :], ALU.mult,
               sig=dv)
    st.dve.wait(v)
    v = st.dve(nc.vector.tensor_tensor, s2[:, :, :], s[:, :, :], s[:, :, :], ALU.mult,
               sig=dv)
    top = LOG1P_TERMS - 1
    st.dve.wait(v)
    v = st.dve(nc.vector.tensor_scalar, poly[:, :, :], s2[:, :, :], 2.0 / (2 * top + 1), None,
               ALU.mult, sig=dv)
    for n in range(top - 1, 0, -1):
        st.dve.wait(v)
        v = st.dve(nc.vector.scalar_tensor_tensor, poly[:, :, :], poly[:, :, :],
                   2.0 / (2 * n + 1), s2[:, :, :], ALU.add, ALU.mult, sig=dv)
    st.dve.wait(v)
    v = st.dve(nc.vector.scalar_tensor_tensor, poly[:, :, :], poly[:, :, :], 2.0, s[:, :, :],
               ALU.add, ALU.mult, sig=dv)
    st.dve.wait(v)
    v = st.dve(nc.vector.scalar_tensor_tensor, poly[:, :, :], z[:, :, :], 0.0, poly[:, :, :],
               ALU.max, ALU.add, sig=dv)
    st.dve.wait(v, r)
    v = st.dve(nc.vector.tensor_tensor, poly[:, :, :], poly[:, :, :], spread(rate[:, :], n_tiles),
               ALU.mult, sig=dv)
    st.act.wait(v)
    decay = st.act(nc.scalar.activation, gates[:, :, H:2 * H], poly[:, :, :], ACT.Exp, scale=-1.0, sig=av)
    gates_row = st.sbuf("gates_row", [2 * H, nb * T])
    g_turn = st.sem("g_turned")
    for n in range(0, n_tiles, 8):
        slot, bank, free = pairs.take()
        for m in range(8):
            st.pe.wait(*free, decay, beta)
            t = st.pe(nc.tensor.transpose, bank[0:2 * H, m // 4, (m % 4) * P:(m % 4 + 1) * P],
                      gates[:, n + m, :], core.ident[:, :], sig=g_turn)
        st.act.wait(t)
        gates_ready = st.act(nc.scalar.copy,
                             gates_row[:, n * P:(n + 8) * P].rearrange("p (a b) -> p a b", a=2),
                             bank[0:2 * H, :, :], sig=av)
        pairs.done[slot] = [gates_ready]

    PAD = TAPS - 1
    mixed = [st.sbuf(f"mixed{g}", [P, PAD + T]) for g in range(3)]
    conv_v = st.sbuf("conv_v", [P, T])
    q_chn, k_chn, silu_z, beta_v, decay_b = (
        [st.sbuf(n, [P, T])[:, :], core.big[:, i * T:(i + 1) * T]]
        for i, n in enumerate(("q_chn", "k_chn", "silu_z", "beta_v", "decay_b")))
    square, norm_r = st.sbuf("square", [P, T]), st.sbuf("norm_r", [P, T])
    drive = Ring([st.sbuf(f"drive{i}", [P, T]) for i in range(2)])
    state = Ring([st.sbuf(f"state{i}", [P, T]) for i in range(2)])
    read_out = Ring([st.sbuf(f"read_out{i}", [P, T]) for i in range(2)])
    o = st.sbuf("o", [P, T])
    mm_s, act_s, dve_s, pool_s = (st.sem(n) for n in ("mm", "act", "dve", "pool"))
    row_ring = Ring([work_banks[:, i, :] for i in range(2)])
    for g in range(3):
        pad = st.pool(nc.gpsimd.memset, mixed[g][:, 0:PAD], 0.0, sig=pool_s)

    def two(ap):
        return ap.rearrange("p (a b) -> p a b", a=HALF)

    def product(w, rhs, after, **kw):
        slot, bank, free = pairs.take()
        for half in range(HALF):
            st.pe.wait(*free, *after)
            mm = st.pe(nc.tensor.matmul, bank[:, half, :], w, rhs[:, half * BANK:(half + 1) * BANK],
                       start=True, stop=True, sig=mm_s)
        return slot, bank, mm

    root_ready = {}

    def head_root(src, scale, after):
        st.dve.wait(*after)
        sq = st.dve(nc.vector.tensor_tensor, square[:, :], src, src, ALU.mult, sig=dve_s)
        slot, bank, mm = product(same_head[:, :], square, [sq])
        st.act.wait(mm, small_ready)
        root = st.act(nc.scalar.activation, two(norm_r[:, :]), bank, ACT.Sqrt, bias=small[:, 0:1],
                      scale=scale, sig=act_s)
        pairs.done[slot] = [root]
        root_ready["last"] = root

    def head_norm(src, out_scale):
        st.dve.wait(root_ready["last"])
        inv = st.dve(nc.vector.reciprocal, norm_r[:, :], norm_r[:, :], sig=dve_s)
        st.dve.wait(inv)
        return st.dve(nc.vector.scalar_tensor_tensor, src, src, out_scale, norm_r[:, :], ALU.mult,
                      ALU.mult, sig=dve_s)

    rows, norm = Rows(st, FirstBank(pairs)), Norm(st)
    turn = Turn(st, rows.ring)
    gated = st.sbuf("gated", [P, T])
    done, ready_of = {-2: pad, -1: pad}, {}
    conv_done = [None] * 3

    def front(b):
        i, marks, silued = b % 2, {"beta": None}, []
        cols, row = xc[:, b * T:(b + 1) * T], gates_row[:, b * T:(b + 1) * T]
        conv = [q_chn[i], k_chn[i], conv_v[:, :]]
        ready_of[b] = marks

        def convolve(g):
            slot, bank, mm = product(w_qkv[:, g * C:(g + 1) * C], cols, ready)
            st.act.wait(mm, pad, conv_done[g])
            kept = st.act(nc.scalar.copy, two(mixed[g][:, PAD:PAD + T]), bank, sig=act_s)
            pairs.done[slot] = [kept]
            st.dve.wait(kept, done[b - 2], ready_of[b - 1]["beta"] if b and g == 2 else None)
            v = st.dve(nc.vector.tensor_scalar, conv[g], mixed[g][:, PAD:PAD + T],
                       taps[:, g, PAD:PAD + 1], None, ALU.mult, sig=dve_s)
            for k in range(PAD):
                st.dve.wait(v)
                v = st.dve(nc.vector.scalar_tensor_tensor, conv[g], mixed[g][:, k:k + T],
                           taps[:, g, k:k + 1], conv[g], ALU.mult, ALU.add, sig=dve_s)
            conv_done[g] = v

        def silu():
            slot, bank, mm = product(w_z[:, :], cols, ready)
            for g in range(3):
                st.act.wait(conv_done[g])
                silued.append(st.act(nc.scalar.activation, conv[g], conv[g], ACT.Silu, sig=act_s))
            st.act.wait(mm, done[b - 2])
            marks["z"] = st.act(nc.scalar.activation, two(silu_z[i]), bank, ACT.Silu, sig=act_s)
            pairs.done[slot] = [marks["z"]]

        def root_of(g):
            head_root(conv[g], 1.0, [silued[g]])

        def norm_of(g):
            marks["qk"[g]] = head_norm(conv[g], (HD ** -0.5, 1.0)[g])

        def beta():
            slot, bank, mm = product(gate_rows[:, 0, :], row, [gates_ready])
            st.dve.wait(mm, silued[2], done[b - 2])
            marks["beta"] = st.dve(nc.vector.tensor_tensor, two(beta_v[i]), bank, two(conv[2]),
                                   ALU.mult, sig=dve_s)
            pairs.done[slot] = [marks["beta"]]

        def decays():
            slot, bank, mm = product(gate_rows[:, 1, :], row, [gates_ready])
            st.act.wait(mm, done[b - 2])
            marks["decay"] = st.act(nc.scalar.copy, two(decay_b[i]), bank, sig=act_s)
            pairs.done[slot] = [marks["decay"]]

        return [[], [lambda: convolve(0)], [lambda: convolve(1)], [lambda: convolve(2)],
                [silu, lambda: root_of(1)], [lambda: norm_of(1), beta],
                [lambda: root_of(0), decays], [lambda: norm_of(0)]]

    def tail(b, mm):
        def root_of_o():
            st.act.wait(mm, done[b - 1])
            out_kept[0] = st.act(nc.scalar.copy, two(o[:, :]), out_banks[:, :, :], sig=act_s)
            head_root(o[:, :], 1.0 / HD, [out_kept[0]])

        def gate():
            v = head_norm(o[:, :], 1.0)
            st.dve.wait(v, ready_of[b]["z"])
            done[b] = st.dve(nc.vector.tensor_tensor, gated[:, :], o[:, :], silu_z[b % 2],
                             ALU.mult, sig=dve_s)

        def project():
            for n in range(0, NT, 4):
                y = rows(lambda k, m: gated[:, (n + m) * P:(n + m + 1) * P],
                         lambda k: w_out[:, :], None, x[:, b * NT + n:b * NT + n + 4, :],
                         x[:, b * NT + n:b * NT + n + 4, :], [done[b]])
            tiles = slice(b * NT, (b + 1) * NT)
            norm(x[:, tiles, :], x[:, tiles, :], [y])

        def turn_x():
            for n in range(b * NT, (b + 1) * NT, 4):
                turn(x[:, n:n + 4, :], xc[:, n * P:n * P + BANK], [norm.last])

        return [[root_of_o], [gate], [project], [turn_x]] + [[]] * (HD - 4)

    def put(vi, ro, read, out_free):
        st.pe.wait(out_free, read)
        for half in range(HALF):
            mm = st.pe(nc.tensor.matmul, out_banks[:, half, :], place_v[:, vi, :],
                       ro[:, half * BANK:(half + 1) * BANK], start=vi == 0, stop=vi == HD - 1,
                       sig=mm_s)
        return mm

    out_kept = [None]
    idle = [[]] * HD
    for pieces in front(0):
        for work in pieces:
            work()
    behind = idle
    for b in range(nb):
        i, marks = b % 2, ready_of[b]
        ahead = front(b + 1) if b + 1 < nb else idle
        waiting = []
        for vi in range(HD):
            slot, bank, mm = product(pick_v[:, vi, :], beta_v[i], [marks["beta"]])
            ds, dr, dfree = drive.take()
            st.dve.wait(mm, marks["k"], *dfree)
            v = st.dve(nc.vector.tensor_tensor, two(dr[:, :]), bank, two(k_chn[i]), ALU.mult,
                       sig=dve_s)
            pairs.done[slot] = [v]
            ss, sc, sfree = state.take()
            st.dve.wait(v, marks["decay"], *sfree)
            v = st.dve(nc.vector.tensor_tensor_scan, sc[:, :], decay_b[i], dr[:, :], 0.0,
                       ALU.mult, ALU.add, sig=dve_s)
            drive.done[ds] = [v]
            rs, ro, rfree = read_out.take()
            st.pool.wait(v, marks["q"], *rfree)
            r = st.pool(nc.gpsimd.tensor_tensor, ro[:, :], sc[:, :], q_chn[i], ALU.mult,
                        sig=pool_s)
            state.done[ss] = [r]
            waiting.append((vi, ro, r, rs))
            for work in behind[vi] + ahead[vi]:
                work()
            if len(waiting) > 1:
                a = waiting.pop(0)
                read_out.done[a[3]] = [put(*a[:3], out_kept[0])]
        a = waiting.pop(0)
        mm = put(*a[:3], out_kept[0])
        read_out.done[a[3]] = [mm]
        behind = tail(b, mm)
    for pieces in behind:
        for work in pieces:
            work()
    st.run()


class FirstBank:

    def __init__(self, pairs):
        self.pairs, self.done = pairs, pairs.done

    def take(self):
        slot, bank, free = self.pairs.take()
        return slot, bank[:, 0, :], free


class TopTwo:

    def __init__(self, st, tiles, n):
        self.st, self.tiles, self.n = st, tiles, n
        self.a, self.b, self.first, self.second = (st.sbuf(f"top_{i}", [P, tiles, n])
                                                   for i in ("a", "b", "first", "second"))
        self.m1, self.m2, self.key = (st.sbuf(f"top_{i}", [P, tiles]) for i in ("m1", "m2", "key"))
        self.ramp = st.sbuf("top_ramp", [P, n])
        self.loaded, self.dv = st.sem("top_loaded"), st.sem("top_dve")
        self.ramp_ready = st.load(self.ramp[:, :], st.core.const[f"ramp{n}"][:, :], self.loaded)

    def pick(self, scores, peak, hot, after):
        st, nc, n = self.st, self.st.nc, self.n
        st.dve.wait(*after)
        v = st.dve(nc.vector.tensor_reduce, peak[:, :], scores, AX.X, ALU.max,
                   sig=self.dv)
        st.dve.wait(v)
        v = st.dve(nc.vector.tensor_tensor, self.a[:, :, :], scores, along(peak[:, :], n),
                   ALU.is_equal, sig=self.dv)
        st.dve.wait(v, self.ramp_ready)
        v = st.dve(nc.vector.tensor_tensor, self.a[:, :, :], self.a[:, :, :],
                   spread(self.ramp[:, :], self.tiles), ALU.mult,
                   sig=self.dv)
        st.dve.wait(v)
        v = st.dve(nc.vector.tensor_reduce, self.key[:, :], self.a[:, :, :], AX.X, ALU.max, sig=self.dv)
        st.dve.wait(v)
        return st.dve(nc.vector.tensor_tensor, hot[:, :, :], self.a[:, :, :],
                      along(self.key[:, :], n), ALU.is_equal, sig=self.dv)

    def __call__(self, scores, gates, after):
        st, nc, n = self.st, self.st.nc, self.n
        v = self.pick(scores, self.m1, self.first, after)
        st.dve.wait(v)
        v = st.dve(nc.vector.scalar_tensor_tensor, self.b[:, :, :], self.first[:, :, :], -4.0,
                   scores, ALU.mult, ALU.add, sig=self.dv)
        v = self.pick(self.b[:, :, :], self.m2, self.second, [v])
        st.dve.wait(v)
        v = st.dve(nc.vector.tensor_tensor, self.key[:, :], self.m1[:, :], self.m2[:, :], ALU.add, sig=self.dv)
        st.dve.wait(v)
        v = st.dve(nc.vector.reciprocal, self.key[:, :], self.key[:, :], sig=self.dv)
        for m, hot in ((self.m1, self.first), (self.m2, self.second)):
            st.dve.wait(v)
            v = st.dve(nc.vector.tensor_tensor, m[:, :], m[:, :], self.key[:, :], ALU.mult, sig=self.dv)
            st.dve.wait(v)
            v = st.dve(nc.vector.tensor_tensor, hot[:, :, :], hot[:, :, :], along(m[:, :], n),
                       ALU.mult, sig=self.dv)
        st.dve.wait(v)
        return st.dve(nc.vector.tensor_tensor, gates, self.first[:, :, :], self.second[:, :, :],
                      ALU.add, sig=self.dv)


def router(st, ring, w, bias, chn, n_tiles, n, out, done, after):
    nc = st.nc
    slot, bank, free = ring.take()
    flat = bank.rearrange("p (t e) -> p t e", e=n)
    for t in range(n_tiles):
        st.pe.wait(*after, *free)
        mm = st.pe(nc.tensor.matmul, flat[:, t, :], chn[:, t * P:(t + 1) * P], w, start=True,
                   stop=True, sig=st.routed)
    st.dve.wait(mm, *after)
    kept = st.dve(nc.vector.tensor_tensor, out, flat[:, 0:n_tiles, :], spread(bias, n_tiles),
                  ALU.add, sig=done)
    ring.done[slot] = [kept]
    return kept


def gate_rows_of(st, ring, gates, rows, tiles, n, after, turned, kept):
    nc = st.nc
    for t in range(tiles.start, tiles.stop, 4):
        slot, bank, free = ring.take()
        for m in range(4):
            st.pe.wait(*free, *after)
            mm = st.pe(nc.tensor.transpose, bank[0:n, m * P:(m + 1) * P], gates[:, t + m, :],
                       st.core.ident[:, :], sig=turned)
        st.act.wait(mm)
        last = st.act(nc.scalar.copy, rows[:, t * P:(t + 4) * P], bank[0:n, :],
                      sig=kept)
        ring.done[slot] = [last]
    return last


E1, I1 = 16, 64


def expert_ffn(core):
    st = Stage(core, "moe1")
    nc, inp, const, nb = core.nc, core.inp, core.const, core.n_batch
    x, xc = core.x_tok, core.x_chn
    n_tiles = nb * NT
    banks = st.psum("p", 8)
    ring = Ring([banks[:, i, :] for i in range(6)])
    out_ring = Ring([banks[:, 6 + i, :] for i in range(2)])
    st.routed = st.sem("routed")
    loaded, big_loaded = st.sem("loaded"), st.sem("big_loaded")
    w_router = st.sbuf("w_router", [P, E1])
    pair_rows = st.sbuf("pair_rows", [E1, E1 // 2, P])
    st.load(w_router[:, :], inp["L1_ffn_gate_w"][:, :], loaded)
    st.load(pair_rows[:, :, :], const["pair_rows"][:, :, :], loaded)
    router_bias, small_ready = broadcast_rows(st, "router_bias", inp["L1_ffn_gate_b"], E1, loaded)
    pairs_n = E1 // 2
    wg, wu = st.sbuf("wg", [P, E1, I1]), st.sbuf("wu", [P, E1, I1])
    wd = st.sbuf("wd", [P, pairs_n, C])
    sg, su, sd = st.sbuf("sg", [P, I1]), st.sbuf("su", [P, I1]), st.sbuf("sd", [I1, C])
    st.load(sg[:, :], inp["L1_ffn_shared_wg"][:, :], big_loaded)
    st.load(su[:, :], inp["L1_ffn_shared_wu"][:, :], big_loaded)
    st.load(sd[:, :], inp["L1_ffn_shared_wd"][:, :], big_loaded)
    st.load(wg[:, :, :], inp["L1_ffn_experts_wg"].rearrange("e d i -> d e i"), big_loaded)
    st.load(wu[:, :, :], inp["L1_ffn_experts_wu"].rearrange("e d i -> d e i"), big_loaded)
    w_ready = st.load(wd[:, :, :], inp["L1_ffn_experts_wd"].rearrange("(m e) i d -> (e i) m d", e=2),
                      big_loaded)
    logits, gates = st.sbuf("logits", [P, n_tiles, E1]), st.sbuf("gates", [P, n_tiles, E1])
    gate_row = st.sbuf("gate_row", [E1, nb * T])
    r_done, sig_done = st.sem("logits_done"), st.sem("sigmoid_done")
    v = router(st, ring, w_router[:, :], router_bias[:, :], xc, n_tiles, E1, logits[:, :, :],
               r_done, [small_ready])
    st.act.wait(v)
    v = st.act(nc.scalar.activation, logits[:, :, :], logits[:, :, :], ACT.Sigmoid,
               sig=sig_done)
    top = TopTwo(st, n_tiles, E1)
    v = top(logits[:, :, :], gates[:, :, :], [v])
    row_ready = gate_rows_of(st, ring, gates, gate_row, range(n_tiles), E1, [v],
                             st.sem("gates_turned"), st.sem("gates_kept"))
    act_g = Ring([st.sbuf(f"act_g{i}", [P, BANK]) for i in range(3)])
    hidden = Ring([st.sbuf(f"hidden{i}", [P, BANK]) for i in range(3)])
    up_mm, silued, lifted, scaled, down_mm = (st.sem(n) for n in
                                              ("up_mm", "silued", "lifted", "scaled", "down_mm"))
    added = st.sem("added")
    norm, turn = Norm(st), Turn(st, ring)
    for b in range(nb):
        for n in range(b * NT, (b + 1) * NT, 4):
            cols = xc[:, n * P:n * P + BANK]
            oslot, out, ofree = out_ring.take()
            late = []

            def down(m, k, h, hslot, ready):
                rows = I1 if m == 0 else P
                for i in range(4):
                    st.pe.wait(*ofree, ready, w_ready)
                    mm = st.pe(nc.tensor.matmul, banks4(out)[:, i, :], h[0:rows, i * P:(i + 1) * P],
                               k, start=m == 0 and i == 0, stop=m == pairs_n, skip_group_check=True, sig=down_mm)
                hidden.done[hslot] = [mm]
                return mm

            for m in range(pairs_n + 1):
                if m == 0:
                    g_w, u_w, k, r = sg[:, :], su[:, :], sd[:, :], I1
                else:
                    pair = slice(2 * (m - 1), 2 * m)
                    g_w = wg[:, pair, :].rearrange("p e i -> p (e i)")
                    u_w = wu[:, pair, :].rearrange("p e i -> p (e i)")
                    k, r = wd[:, m - 1, :], P
                gs, gb, gfree = ring.take()
                st.pe.wait(*gfree, w_ready)
                mm_g = st.pe(nc.tensor.matmul, gb[0:r, :], g_w, cols, start=True, stop=True, sig=up_mm)
                us, ub, ufree = ring.take()
                st.pe.wait(*ufree)
                mm_u = st.pe(nc.tensor.matmul, ub[0:r, :], u_w, cols, start=True, stop=True, sig=up_mm)
                a_s, ag, afree = act_g.take()
                st.act.wait(mm_g, *afree)
                a = st.act(nc.scalar.activation, ag[0:r, :], gb[0:r, :], ACT.Silu, sig=silued)
                ring.done[gs] = [a]
                hs, h, hfree = hidden.take()
                st.dve.wait(a, mm_u, *hfree)
                v = st.dve(nc.vector.tensor_tensor, h[0:r, :], ub[0:r, :], ag[0:r, :], ALU.mult, sig=lifted)
                ring.done[us] = [v]
                act_g.done[a_s] = [v]
                if m:
                    bs, bb, bfree = ring.take()
                    st.pe.wait(*bfree, row_ready)
                    mm = st.pe(nc.tensor.matmul, bb, pair_rows[:, m - 1, :],
                               gate_row[:, n * P:n * P + BANK], start=True, stop=True, sig=up_mm)
                    st.dve.wait(v, mm)
                    v = st.dve(nc.vector.tensor_tensor, h[:, :], bb, h[:, :], ALU.mult, sig=scaled)
                    ring.done[bs] = [v]
                late.append((m, k, h, hs, v))
                if len(late) > 1:
                    down(*late.pop(0))
            mm = down(*late.pop(0))
            st.dve.wait(mm)
            y = st.dve(nc.vector.scalar_tensor_tensor, x[:, n:n + 4, :], x[:, n:n + 4, :], 2.0,
                       banks4(out), ALU.mult, ALU.add, sig=added)
            out_ring.done[oslot] = [y]
        tiles = slice(b * NT, (b + 1) * NT)
        done = norm(x[:, tiles, :], x[:, tiles, :], [y])
        for n in range(b * NT, (b + 1) * NT, 4):
            turn(x[:, n:n + 4, :], xc[:, n * P:n * P + BANK], [done])
    st.run()


def causal_attention(core):
    st = Stage(core, "caus")
    nc, inp, const, nb = core.nc, core.inp, core.const, core.n_batch
    x, xc = core.x_tok, core.x_chn
    score_banks, small_banks, out_banks = st.psum("score", 4), st.psum("small", 3), st.psum("out", 1)
    score_pair = [score_banks[:, 0:2, :], score_banks[:, 2:4, :]]
    small_ring = Ring([small_banks[:, i, :] for i in range(3)])
    out_ring = Ring([out_banks[:, 0, :]])
    loaded = st.sem("loaded")
    w = st.sbuf("w", [P, 2 * C])
    bias = st.sbuf("bias", [P, 2])
    head_w = st.sbuf("head_w", [P, H, C])
    st.load(w[:, :], inp["L2_attn_W_attn"][:, :], loaded)
    st.load(bias[:, :], inp["L2_attn_b_attn_c"][:, :], loaded)
    w_ready = st.load(head_w[:, :, :], inp["L2_attn_head_weights"].rearrange("(o h) c -> o h c", o=1)
                      .broadcast_to([P, H, C]), loaded)
    heads = SmallHeads(st, 2 * (BANK // P) * 3, core.q_parts, core.k_parts, const["zero_rows"],
                       causal=True)
    proj = Projections(st, small_ring, {"q": w[:, 0:C], "k": w[:, C:2 * C]},
                       {"q": bias[:, 0:1], "k": bias[:, 1:2]}, w_ready, lambda b: None)
    for work in proj.pieces(0):
        work()

    x_one = [st.sbuf(f"x_one{i}", [P, NT, C + 1]) for i in range(2)]
    y = [core.attn_w[:, i * T:(i + 1) * T].rearrange("p (n c) -> p n c", c=C) for i in range(2)]
    exps = [core.big[:, i * NT * BANK:(i + 1) * NT * BANK].rearrange("p (k q) -> p k q", k=NT)
            for i in range(2)]
    x_made, y_zero, exped, weighted = (st.sem(n) for n in (
        "x_made", "y_zero", "exped", "weighted"))
    inverted, scaled, summed = st.sem("inverted"), st.sem("scaled"), st.sem("summed")
    scored = heads.scored
    r_sum = st.sbuf("r_sum", [P, 2])
    part = [st.sbuf(f"part{i}", [P, 2, C]) for i in range(3)]
    units = [(b, g) for b in range(nb) for g in range(H // GROUP)]
    heads.last_unit = len(units) - 1
    QB = BANK // P
    norm, turn = Norm(st), Turn(st, small_ring)
    x_added = st.sem("x_added")
    OUTS = QB // 2
    outs_of_batch = H * HALF * OUTS
    n = {"tile": 0, "part": 0}
    behind = []

    def steps(u):
        b, g = units[u]
        i = u % heads.SLOTS
        q, k = heads.q_stack[i], heads.k_stack[i]

        def start_batch():
            st.pool.wait(weighted.at(outs_of_batch * (b - 1)))
            st.pool(nc.gpsimd.memset, x_one[b % 2][:, :, C:C + 1], 1.0, sig=x_made)
            st.pool.wait(x_made.at(2 * b + 1))
            st.pool(nc.gpsimd.tensor_copy, x_one[b % 2][:, :, 0:C], x[:, b * NT:(b + 1) * NT, :],
                    sig=x_made)
            st.pool.wait(x_added.at(b - 1))
            st.pool(nc.gpsimd.memset, y[b % 2], 0.0, sig=y_zero)

        def scores(half, j, two):
            if g == 0 and half == 0 and j == 0 and two == 0:
                start_batch()
            t, h = n["tile"], n["part"]
            n["tile"] += 1
            banks, e = score_pair[t % 2], exps[h % 2]
            diagonal = 2 * two >= half * QB
            lo = max(2 * two * P - half * BANK, 0)
            st.pe.wait(heads.row_ready[i], heads.ready[i])
            st.pe.wait(exped.at(t - 1))
            for c in range(2):
                kb = 2 * two + c
                st.pe(nc.tensor.matmul, banks[:, c, lo:BANK], k[0:STACK, j, kb * P:(kb + 1) * P],
                      q[0:STACK, j, half * BANK + lo:(half + 1) * BANK], start=True,
                      stop=not diagonal, sig=scored if c == 1 and not diagonal else None)
                if diagonal:
                    at = kb * P - half * BANK
                    st.pe(nc.tensor.matmul, banks[:, c, at:at + P], st.core.ident_bf[:, :],
                          st.core.causal_mask[:, :], start=False, stop=True,
                          sig=scored if c == 1 else None)
            st.act.wait(scored.at(t + 1), weighted.at(OUTS * (h - 1)))
            st.act(nc.scalar.activation, e[:, 2 * two:2 * two + 2, lo:BANK], banks[:, :, lo:BANK],
                   ACT.Exp, sig=exped)
            tiles = (half + 1) * QB // 2
            if behind and two % (tiles // 2) == 0:
                follow()
            if two == tiles - 1:
                n["part"] += 1
                for m in range(OUTS):
                    behind.append((b, h, half, g * GROUP + j, m, t))

        return [(scores, (half, j, two)) for half in range(HALF) for j in range(GROUP)
                for two in range((half + 1) * QB // 2)]

    def follow():
        b, h, half, head, two, t = behind.pop(0)
        o = OUTS * h + two
        out, p, e = out_ring.buffers[o % len(out_ring.buffers)], part[o % 3], exps[h % 2]
        st.pe.wait(exped.at(t + 1), x_made.at(2 * (b + 1)))
        st.pe.wait(scaled.at(2 * (o + 1 - len(out_ring.buffers))))
        for m in range(2):
            nq = 2 * two + m
            kbs = half * QB + nq + 1
            for kb in range(kbs):
                st.pe(nc.tensor.matmul, out[:, m * (C + 1):(m + 1) * (C + 1)],
                      e[:, kb, nq * P:(nq + 1) * P], x_one[b % 2][:, kb, :],
                      start=kb == 0, stop=kb == kbs - 1,
                      sig=weighted if m == 1 and kb == kbs - 1 else None)
        both = out[:, 0:2 * (C + 1)].rearrange("p (m c) -> p m c", c=C + 1)
        st.dve.wait(weighted.at(o + 1), scaled.at(2 * o))
        st.dve(nc.vector.reciprocal, r_sum[:, :], both[:, :, C], sig=inverted)
        st.dve.wait(inverted.at(o + 1), w_ready, summed.at(o - 2))
        for m in range(2):
            st.dve(nc.vector.scalar_tensor_tensor, p[:, m, :], both[:, m, 0:C],
                   r_sum[:, m:m + 1], head_w[:, head, :], ALU.mult, ALU.mult, sig=scaled)
        at = half * QB + 2 * two
        st.pool.wait(scaled.at(2 * (o + 1)), y_zero.at(b + 1), summed.at(o))
        st.pool(nc.gpsimd.tensor_tensor, y[b % 2][:, at:at + 2, :], y[b % 2][:, at:at + 2, :],
                p[:, :, :], ALU.add, sig=summed)
        if o + 1 == outs_of_batch * (b + 1):
            finish(b)

    def finish(b):
        tiles = slice(b * NT, (b + 1) * NT)
        st.dve.wait(summed.at(outs_of_batch * (b + 1)))
        st.dve(nc.vector.tensor_tensor, x[:, tiles, :], x[:, tiles, :], y[b % 2], ALU.add,
               sig=x_added)
        out = norm(x[:, tiles, :], x[:, tiles, :], [x_added.at(b + 1)])
        for m in range(b * NT, (b + 1) * NT, 4):
            turn(x[:, m:m + 4, :], xc[:, m * P:m * P + BANK], [out])

    def maxima(u):
        b, g = units[u]
        out = heads.maxima(u, small_ring)

        def first(f, args):
            if u == 0:
                heads.fill(0, b, g, proj.stored_of(b))
            f(*args)

        def ahead():
            if u + 1 < len(units):
                b2, g2 = units[u + 1]
                heads.fill(u + 1, b2, g2, proj.stored_of(b2))
        if g == 1 and b + 1 < nb:
            for i, work in enumerate(proj.pieces(b + 1)):
                before(out, 2 + 4 * i, work)
        before(out, 24, ahead)
        out[0] = (first, out[0])
        return out

    interleave(range(len(units)), maxima, steps, lag=4)
    while behind:
        follow()
    st.run()


E2, FF = 8, 512


def rotary_attention(core):
    st = Stage(core, "rot")
    nc, inp, const, nb = core.nc, core.inp, core.const, core.n_batch
    x, xc, x1 = core.x_tok, core.x_chn, core.x_mid
    score_banks, small_banks, out_banks = st.psum("score", 4), st.psum("small", 3), st.psum("out", 1)
    score_pair = [score_banks[:, 0:2, :], score_banks[:, 2:4, :]]
    small_ring = Ring([small_banks[:, i, :] for i in range(3)])
    out_ring = Ring([out_banks[:, 0, :]])
    w_loaded = st.sem("w_loaded")
    w = {}
    for n in "qkvo":
        w[n] = st.sbuf(f"w{n}", [P, C])
        st.load(w[n][:, :], inp[f"L2_ffn_W{n}"][:, :], w_loaded)
    bq, _ = column(st, "bq", inp["L2_ffn_bq"], w_loaded)
    bk, _ = column(st, "bk", inp["L2_ffn_bk"], w_loaded)
    bv, _ = broadcast_rows(st, "bv", inp["L2_ffn_bv"], C, w_loaded)
    bo, _ = broadcast_rows(st, "bo", inp["L2_ffn_bo"], C, w_loaded)
    g1, _ = broadcast_rows(st, "g1", inp["L2_ffn_g1"], C, w_loaded)
    be1, _ = broadcast_rows(st, "be1", inp["L2_ffn_be1"], C, w_loaded)
    rotate = st.sbuf("rotate", [P, C])
    angle = core.big[:, 2 * T:4 * T].rearrange("p (a t) -> p a t", a=2)
    st.load(rotate[:, :], const["rotate"][:, :], w_loaded)
    w_ready = st.load(angle, const["angle"][:, :, :], w_loaded)
    heads = SmallHeads(st, HALF * NT * 2, core.q_parts, core.k_parts, const["zero_rows"])
    v_tok = core.big[:, 4 * T:4 * T + nb * T].rearrange("p (n c) -> p n c", c=C)
    proj = Projections(st, small_ring, {n: w[n][:, :] for n in "qk"},
                       {"q": bq[:, 0:1], "k": bk[:, 0:1]}, w_ready, lambda b: None,
                       rotary=(rotate[:, :], angle), values=(w["v"][:, :], bv[:, :], v_tok))
    for work in proj.pieces(0):
        work()
    units = [(b, g) for b in range(nb) for g in range(H // GROUP)]
    heads.last_unit = len(units) - 1
    exps = [core.attn_w[:, i * T:(i + 1) * T].rearrange("p (a q) -> p a q", a=2) for i in range(4)]
    ctx = [st.sbuf(f"ctx{i}", [P, NT, C]) for i in range(2)]
    at = {"b": 0}
    weighted = Weighted(st, heads, score_pair, out_ring, small_ring, exps,
                        lambda: v_tok, lambda: ctx[at["b"] % 2])
    ctx_chn = Ring(weighted.out_chn)
    turn, turn_ctx = Turn(st, small_ring), Turn(st, small_ring, "_ctx")
    rows, norm = Rows(st, small_ring), Norm(st)
    affine = st.sem("affine")

    def finish(b):
        c = ctx[b % 2]
        done_b = weighted.context.at(4 * HALF * (H // GROUP) * (b + 1))
        for n in range(0, NT, 4):
            cslot, chn, free = ctx_chn.take()
            kept = turn_ctx(c[:, n:n + 4, :], chn[:, :], [done_b] + free)
            m0 = b * NT + n
            y = rows(lambda k, m: chn[:, m * P:(m + 1) * P], lambda k: w["o"][:, :], bo[:, :],
                     x[:, m0:m0 + 4, :], x1[:, m0:m0 + 4, :], [kept, w_ready])
            ctx_chn.done[cslot] = [y]
        tiles = slice(b * NT, (b + 1) * NT)
        out = norm(x1[:, tiles, :], x1[:, tiles, :], [y])
        st.dve.wait(out)
        v = st.dve(nc.vector.tensor_tensor, x1[:, tiles, :], x1[:, tiles, :], spread(g1[:, :], NT),
                   ALU.mult, sig=affine)
        st.dve.wait(v)
        v = st.dve(nc.vector.tensor_tensor, x1[:, tiles, :], x1[:, tiles, :], spread(be1[:, :], NT),
                   ALU.add, sig=affine)
        for n in range(b * NT, (b + 1) * NT, 4):
            turn(x1[:, n:n + 4, :], xc[:, n * P:n * P + BANK], [v])

    def maxima(u):
        b, g = units[u]
        out = heads.maxima(u, small_ring)

        def first(f, args):
            if u == 0:
                heads.fill(0, b, g, proj.stored_of(b))
            f(*args)

        def ahead():
            if u + 1 < len(units):
                b2, g2 = units[u + 1]
                heads.fill(u + 1, b2, g2, proj.stored_of(b2))
        if g == 1 and b + 1 < nb:
            for i, work in enumerate(proj.pieces(b + 1)):
                before(out, 2 + 3 * i, work)
        before(out, 24, ahead)
        out[0] = (first, out[0])
        return out

    def exp_steps(u):
        b, g = units[u]
        out = weighted.steps(u, b * NT, 0, g, lambda: proj.v_ready(b))

        def mark(f, args):
            at["b"] = b
            f(*args)
        out[0] = (mark, out[0])
        if g == H // GROUP - 1:
            f, a = out[-1]
            out[-1] = (lambda *args: (f(*args), weighted.late.append(lambda: finish(b))), a)
        return out

    interleave(range(len(units)), maxima, exp_steps, lag=6)
    while weighted.late:
        weighted.late.pop(0)()
    st.run()


class Experts:

    def __init__(self, st, w1, w2, b1, b2, ready, func, hidden, among=lambda: None):
        self.st, self.w1, self.w2, self.b1, self.b2 = st, w1, w2, b1, b2
        self.ready, self.func, self.among = ready, func, among
        banks = st.psum("experts", 5)
        self.up_ring = Ring([banks[:, i, :] for i in range(3)])
        self.down_ring = Ring([banks[:, 3 + i, :] for i in range(2)])
        self.hidden = Ring(hidden)
        self.up, self.acted, self.down, self.gated = (st.sem(n) for n in (
            "up", "acted", "down", "gated"))

    def __call__(self, cols, gates, gate_rows, gates_ready, rows_ready, acc, base, base_ready):
        st, nc = self.st, self.st.nc
        slot, bank, free = self.down_ring.take()
        for i in range(4):
            st.pe.wait(*free, rows_ready, self.ready[0][0])
            mm = st.pe(nc.tensor.matmul, banks4(bank)[:, i, :], gate_rows(i), self.b2, start=True,
                       stop=True, sig=self.down)
        st.dve.wait(mm, *base_ready)
        v = st.dve(nc.vector.tensor_tensor, acc, banks4(bank), base, ALU.add, sig=self.gated)
        self.down_ring.done[slot] = [v]
        late = []

        def down():
            e, hs = late.pop(0)
            slot, bank, free = self.down_ring.take()
            for i in range(4):
                for c in range(FF // P):
                    hslot, h, a = hs[c]
                    st.pe.wait(*free, a)
                    mm = st.pe(nc.tensor.matmul, banks4(bank)[:, i, :], h[:, i * P:(i + 1) * P],
                               self.w2[:, e, c, :], start=c == 0, stop=c == FF // P - 1, sig=self.down)
            for hslot, _, _ in hs:
                self.hidden.done[hslot] = [mm]
            for i in range(4):
                st.dve.wait(mm, gates_ready, self.last_acc)
                v = st.dve(nc.vector.scalar_tensor_tensor, acc[:, i, :], banks4(bank)[:, i, :],
                           gates(e, i), acc[:, i, :], ALU.mult, ALU.add, sig=self.gated)
            self.last_acc = v
            self.down_ring.done[slot] = [v]
            self.among()

        self.last_acc = v
        for e in range(E2):
            hs = []
            for c in range(FF // P):
                uslot, ub, ufree = self.up_ring.take()
                st.pe.wait(*ufree, *self.ready[e])
                mm = st.pe(nc.tensor.matmul, ub, self.w1[:, e, c * P:(c + 1) * P], cols, start=True,
                           stop=True, sig=self.up)
                hslot, h, hfree = self.hidden.take()
                st.act.wait(mm, *self.ready[e], *hfree)
                a = st.act(nc.scalar.activation, h, ub, self.func, bias=self.b1[:, e, c:c + 1], sig=self.acted)
                self.up_ring.done[uslot] = [a]
                hs.append((hslot, h, a))
            late.append((e, hs))
            if len(late) > 1:
                down()
        down()
        return self.last_acc


def load_experts(st, core, name, small):
    inp = core.inp
    loaded = st.sem("experts_loaded")
    w1 = core.big[:, 0:E2 * FF].rearrange("p (e f) -> p e f", e=E2)
    w2 = core.big[:, E2 * FF:2 * E2 * FF].rearrange("p (e c d) -> p e c d", e=E2, d=C)
    b1, b2 = st.sbuf("b1", [P, E2, FF // P]), st.sbuf("b2", [E2, C])
    st.load(b1[:, :, :], inp[f"{name}_b1_c"][:, :, :], loaded)
    biases = st.load(b2[:, :], inp[f"{name}_b2"][:, :], loaded)
    ready = []
    for e in range(E2):
        mine = st.sem(f"expert{e}_loaded")
        st.load(w1[:, e, :], inp[f"{name}_W1"][e], mine)
        w = st.load(w2[:, e, :, :], inp[f"{name}_W2"][e].rearrange("(c p) d -> p c d", p=P), mine)
        ready.append((biases, w))
    return w1, w2, b1, b2, ready


def block_experts(core):
    st = Stage(core, "moe2")
    nc, inp, const, nb = core.nc, core.inp, core.const, core.n_batch
    x, xc, x1 = core.x_tok, core.x_chn, core.x_mid
    n_tiles = nb * NT
    small_banks = st.psum("small", 3)
    ring = Ring([small_banks[:, i, :] for i in range(3)])
    st.routed = st.sem("routed")
    loaded = st.sem("loaded")
    w_router = st.sbuf("w_router", [P, E2])
    st.load(w_router[:, :], inp["L2_ffn_Wg"][:, :], loaded)
    router_bias, _ = broadcast_rows(st, "router_bias", inp["L2_ffn_bg"], E2, loaded)
    g2, _ = broadcast_rows(st, "g2", inp["L2_ffn_g2"], C, loaded)
    be2, small_ready = broadcast_rows(st, "be2", inp["L2_ffn_be2"], C, loaded)
    w1, w2, b1, b2, w_ready = load_experts(st, core, "L2_ffn", None)
    logits, gates = st.sbuf("logits", [P, n_tiles, E2]), st.sbuf("gates", [P, n_tiles, E2])
    total = st.sbuf("total", [P, n_tiles])
    gate_row = st.sbuf("gate_row", [E2, nb * T])
    r_done, sm, ex = st.sem("logits_done"), st.sem("softmax"), st.sem("exp_done")
    v = router(st, ring, w_router[:, :], router_bias[:, :], xc, n_tiles, E2, logits[:, :, :],
               r_done, [small_ready])
    st.dve.wait(v)
    v = st.dve(nc.vector.tensor_reduce, total[:, :], logits[:, :, :], AX.X, ALU.max,
               sig=sm)
    st.dve.wait(v)
    v = st.dve(nc.vector.tensor_tensor, logits[:, :, :], logits[:, :, :], along(total[:, :], E2),
               ALU.subtract, sig=sm)
    st.act.wait(v)
    v = st.act(nc.scalar.activation, logits[:, :, :], logits[:, :, :], ACT.Exp, sig=ex)
    st.dve.wait(v)
    v = st.dve(nc.vector.tensor_reduce, total[:, :], logits[:, :, :], AX.X, ALU.add,
               sig=sm)
    st.dve.wait(v)
    v = st.dve(nc.vector.reciprocal, total[:, :], total[:, :], sig=sm)
    st.dve.wait(v)
    v = st.dve(nc.vector.tensor_tensor, logits[:, :, :], logits[:, :, :], along(total[:, :], E2),
               ALU.mult, sig=sm)
    top = TopTwo(st, n_tiles, E2)
    gates_ready = top(logits[:, :, :], gates[:, :, :], [v])
    rows_ready = gate_rows_of(st, ring, gates, gate_row, range(n_tiles), E2, [gates_ready],
                              st.sem("gates_turned"), st.sem("gates_kept"))
    hidden = [st.sbuf(f"hidden{i}", [P, BANK]) for i in range(8)]
    experts = Experts(st, w1, w2, b1, b2[:, :], w_ready, ACT.Gelu, [h[:, :] for h in hidden])
    norm, turn = Norm(st), Turn(st, ring)
    affine = st.sem("affine")
    for b in range(nb):
        for n in range(b * NT, (b + 1) * NT, 4):
            v = experts(xc[:, n * P:n * P + BANK], lambda e, i: gates[:, n + i, e:e + 1],
                        lambda i: gate_row[:, (n + i) * P:(n + i + 1) * P], gates_ready, rows_ready,
                        x1[:, n:n + 4, :], x1[:, n:n + 4, :], [])
        tiles = slice(b * NT, (b + 1) * NT)
        v = norm(x1[:, tiles, :], x1[:, tiles, :], [v])
        st.dve.wait(v, small_ready)
        v = st.dve(nc.vector.tensor_tensor, x1[:, tiles, :], x1[:, tiles, :], spread(g2[:, :], NT),
                   ALU.mult, sig=affine)
        st.dve.wait(v)
        v = st.dve(nc.vector.tensor_tensor, x1[:, tiles, :], x1[:, tiles, :], spread(be2[:, :], NT),
                   ALU.add, sig=affine)
        st.dve.wait(v)
        v = st.dve(nc.vector.tensor_tensor, x[:, tiles, :], x[:, tiles, :], x1[:, tiles, :],
                   ALU.add, sig=affine)
        v = norm(x[:, tiles, :], x[:, tiles, :], [v])
        for n in range(b * NT, (b + 1) * NT, 4):
            turn(x[:, n:n + 4, :], xc[:, n * P:n * P + BANK], [v])
    st.run()


ENTMAX_ITER = 25
GATE_FLOOR = 1e-9


class Entmax:

    def __init__(self, st, ring):
        self.st, self.ring, self.n = st, ring, 0
        inp = st.core.inp
        loaded = st.sem("router_loaded")
        self.w = st.sbuf("w_router", [P, E2])
        st.load(self.w[:, :], inp["L3_ffn_Wr"][:, :], loaded)
        self.bias, self.w_ready = broadcast_rows(st, "router_bias", inp["L3_ffn_br"], E2, loaded)
        self.step, self.logits_done, st.routed = (st.sem(n) for n in (
            "entmax_step", "logits_done", "routed"))
        self.logits, self.xs, self.diff, self.power, self.p = (
            st.sbuf(f"ent_{i}", [P, NT, E2])[:, :, :] for i in (
                "logits", "x", "diff", "power", "p"))
        self.low, self.high, self.width, self.mid, self.f_low, self.f, self.keep = (
            st.sbuf(f"ent_{i}", [P, NT])[:, :] for i in (
                "low", "high", "width", "mid", "f_low", "f", "keep"))

    def pieces(self, b, x_ready):
        st, nc, out = self.st, self.st.nc, []
        xs, diff, power, p = self.xs, self.diff, self.power, self.p
        low, high, width, mid, f_low, f, keep = (
            self.low, self.high, self.width, self.mid, self.f_low, self.f, self.keep)

        def route():
            router(st, self.ring, self.w[:, :], self.bias[:, :],
                   st.core.x_chn[:, b * T:(b + 1) * T], NT, E2, self.logits, self.logits_done,
                   [x_ready(), self.w_ready])

        def dve(method, *args, **kw):
            def piece():
                st.dve.wait(self.logits_done.at(self.routed), self.step.at(self.n))
                st.dve(method, *args, sig=self.step, **kw)
                self.n += 1
            out.append(piece)

        def mass(tau, total):
            dve(nc.vector.tensor_tensor, diff, xs, along(tau, E2), ALU.subtract)
            dve(nc.vector.scalar_tensor_tensor, power, diff, 0.0, diff, ALU.max, ALU.mult)
            dve(nc.vector.tensor_reduce, total, power, AX.X, ALU.add)

        def first():
            route()
            self.routed = self.logits_done.value - self.logits_done.start

        dve(nc.vector.tensor_scalar, xs, self.logits, 0.5, None, ALU.mult)
        dve(nc.vector.tensor_reduce, high, xs, AX.X, ALU.max)
        dve(nc.vector.tensor_scalar, low, high, 1.0, None, ALU.subtract)
        dve(nc.vector.tensor_scalar, high, high, (1.0 / E2) ** 0.5, None, ALU.subtract)
        dve(nc.vector.tensor_tensor, width, high, low, ALU.subtract)
        mass(low, f_low)
        dve(nc.vector.tensor_scalar, f_low, f_low, 1.0, None, ALU.subtract)
        for _ in range(ENTMAX_ITER):
            dve(nc.vector.tensor_scalar, width, width, 0.5, None, ALU.mult)
            dve(nc.vector.tensor_tensor, mid, low, width, ALU.add)
            mass(mid, f)
            dve(nc.vector.scalar_tensor_tensor, f, f, 1.0, f_low, ALU.subtract, ALU.mult)
            dve(nc.vector.tensor_scalar, keep, f, 0.0, None, ALU.is_ge)
            dve(nc.vector.copy_predicated, low, keep.bitcast(mybir.dt.uint32), mid)
        mass(mid, f)
        dve(nc.vector.reciprocal, f, f)
        dve(nc.vector.tensor_tensor, p, power, along(f, E2), ALU.mult)
        dve(nc.vector.scalar_tensor_tensor, st.core.gates[:, b * NT:(b + 1) * NT, :], p,
            GATE_FLOOR, p, ALU.is_gt, ALU.mult)
        return [first] + out


WIDE = 64
PAIRS = H // 2


def wide_attention(core):
    st = Stage(core, "wide")
    nc, inp, const, nb = core.nc, core.inp, core.const, core.n_batch
    x, xc = core.x_tok, core.x_chn
    banks = st.psum("p", 8)
    score_banks = [banks[:, 0:2, :], banks[:, 2:4, :]]
    out = banks[:, 4:6, :]
    side = Ring([banks[:, 6:8, :]])
    loaded = st.sem("loaded")
    wide_w = {n: core.big[:, i * 8 * C:(i + 1) * 8 * C] for i, n in enumerate("qkvo")}
    for n in "qkv":
        st.load(wide_w[n], inp[f"L3_attn_W{n}_t"][:, :], loaded)
    w_o = wide_w["o"].rearrange("p (m c) -> p m c", c=C)
    st.load(w_o, inp["L3_attn_Wo_t"].rearrange("(m p) c -> p m c", p=P), loaded)
    bq, bk = st.sbuf("bq", [P, PAIRS]), st.sbuf("bk", [P, PAIRS])
    st.load(bq[:, :], inp["L3_attn_bq_c"][:, :], loaded)
    st.load(bk[:, :], inp["L3_attn_bk_c"][:, :], loaded)
    scale = st.sbuf("scale", [P, PAIRS])
    two_heads = inp["L3_attn_adaptive_scale_c"]
    own = [slice(a * WIDE, (a + 1) * WIDE) for a in range(2)]
    other = own[::-1]
    max_row = [WIDE, 0]
    for a in range(2):
        st.load(scale[own[a], :], two_heads[a:a + 1, :].broadcast_to([WIDE, PAIRS]), loaded)
    bv, _ = broadcast_rows(st, "bv", inp["L3_attn_bv"], H * WIDE, loaded)
    bo, _ = broadcast_rows(st, "bo", inp["L3_attn_bo"], C, loaded)
    gamma, _ = broadcast_rows(st, "gamma", inp["L3_attn_gamma"], C, loaded)
    beta, ready = broadcast_rows(st, "beta", inp["L3_attn_beta"], C, loaded)
    st.dve.wait(ready)
    scaled = st.dve(nc.vector.tensor_scalar, scale[:, :], scale[:, :], WIDE ** -0.5, None,
                    ALU.mult, sig=st.sem("scaled"))
    q_pad = [[st.sbuf(f"q_pad{i}{a}", [P, T]) for a in range(2)] for i in range(2)]
    k_pad = [[st.sbuf(f"k_pad{i}{a}", [P, T]) for a in range(2)] for i in range(2)]
    q_bf = [st.sbuf(f"q_bf{a}", [P, T], BF16) for a in range(2)]
    k_bf = st.sbuf("k_bf", [P, T], BF16)
    v_tok = [st.sbuf(f"v_tok{i}", [P, NT, C]) for i in range(2)]
    zeroed = st.sem("zeroed")
    for a in range(2):
        st.pool(nc.gpsimd.memset, q_bf[a][other[a], :], 0.0, sig=zeroed)
        for i in range(2):
            st.pool(nc.gpsimd.memset, q_pad[i][a][other[a], :], 0.0, sig=zeroed)
            zero = st.pool(nc.gpsimd.memset, k_pad[i][a][other[a], :], 0.0, sig=zeroed)
    st.pool.wait(zero)
    for a in range(2):
        for i in range(2):
            row = slice(max_row[a], max_row[a] + 1)
            zero = st.pool(nc.gpsimd.memset, k_pad[i][a][row, :], 1.0, sig=zeroed)
    E_BUFS = 4
    exps = [core.attn_w[:, i * T:(i + 1) * T] for i in range(E_BUFS)]
    acc = [core.big[:, (4 + a) * T:(5 + a) * T] for a in range(2)]
    sums = core.big[:, 6 * T:7 * T]
    att = st.sbuf("att", [P, PAIRS, T])
    neg_max = st.sbuf("neg_max", [P, 2 * NT])
    max_rows = st.sbuf("max_rows", [2 * NT, P])
    projected, q_kept, k_kept, v_kept, cast = (st.sem(n) for n in (
        "projected", "q_kept", "k_kept", "v_kept", "cast"))
    max_scored, maxed, max_turned, rows_kept, row_sent = (st.sem(n) for n in (
        "max_scored", "maxed", "max_turned", "rows_kept", "row_sent"))
    scored, exped, summed, weighted, out_kept = (st.sem(n) for n in (
        "scored", "exped", "summed", "weighted", "out_kept"))
    total, sums_kept, inverted, divided = (st.sem(n) for n in (
        "total", "sums_kept", "inverted", "divided"))
    units = [(b, m) for b in range(nb) for m in range(PAIRS)]
    TILES = 2 * NT
    ADDS = 2 * (NT - 1)

    def two(ap):
        return ap.rearrange("p (h t) -> p h t", h=HALF)

    def project_q(u):
        b, m = units[u]
        slot, bank, emptied = side.take()
        st.pe.wait(*emptied, ready)
        for half in range(HALF):
            st.pe(nc.tensor.matmul, bank[:, half, :], wide_w["q"][:, m * P:(m + 1) * P],
                  xc[:, b * T + half * BANK:b * T + (half + 1) * BANK], start=True, stop=True,
                  sig=projected)
        st.dve.wait(projected.at(12 * u + 2), scaled, scored.at(TILES * (u - 1)))
        for a in range(2):
            st.dve(nc.vector.tensor_scalar, two(q_pad[u % 2][a][own[a], :]), bank[own[a], :, :],
                   bq[own[a], m:m + 1], scale[own[a], m:m + 1], ALU.add, ALU.mult, sig=q_kept)
        side.done[slot] = [q_kept.at(2 * u + 2)]
        st.act.wait(q_kept.at(2 * u + 2), max_scored.at(TILES * u))
        for a in range(2):
            st.act(nc.scalar.copy, q_bf[a][own[a], :], q_pad[u % 2][a][own[a], :], sig=cast)

    def project_k(u):
        b, m = units[u]
        slot, bank, emptied = side.take()
        st.pe.wait(*emptied)
        for half in range(HALF):
            st.pe(nc.tensor.matmul, bank[:, half, :], wide_w["k"][:, m * P:(m + 1) * P],
                  xc[:, b * T + half * BANK:b * T + (half + 1) * BANK], start=True, stop=True,
                  sig=projected)
        st.act.wait(projected.at(12 * u + 4), ready, scored.at(TILES * (u - 1)))
        for a in range(2):
            st.act(nc.scalar.activation, two(k_pad[u % 2][a][own[a], :]), bank[own[a], :, :],
                   ACT.Identity, bias=bk[own[a], m:m + 1], sig=k_kept)
        st.act.wait(max_scored.at(TILES * u))
        st.act(nc.scalar.activation, two(k_bf[:, :]), bank, ACT.Identity, bias=bk[:, m:m + 1],
               sig=cast)
        side.done[slot] = [cast.at(3 * u + 3)]

    def project_v(u):
        b, m = units[u]
        pair = slice(m * P, (m + 1) * P)
        slot, bank, emptied = side.take()
        st.pe.wait(*emptied)
        for n in range(NT):
            st.pe(nc.tensor.matmul, bank[:, n // 4, (n % 4) * P:(n % 4 + 1) * P],
                  xc[:, b * T + n * P:b * T + (n + 1) * P], wide_w["v"][:, pair], start=True,
                  stop=True, sig=projected)
        st.dve.wait(projected.at(12 * u + 12), weighted.at(NT * (u - 1)))
        st.dve(nc.vector.tensor_tensor, v_tok[u % 2][:, :, :],
               bank.rearrange("p a (n c) -> p (a n) c", c=C), spread(bv[:, pair], NT), ALU.add,
               sig=v_kept)
        side.done[slot] = [v_kept.at(u + 1)]

    def maximum(u, t):
        a, n = t // NT, t % NT
        slot, bank, emptied = side.take()
        st.pe.wait(*emptied, cast.at(3 * u + 3), zero)
        for half in range(HALF):
            st.pe(nc.tensor.matmul, bank[:, half, :], q_bf[a][:, n * P:(n + 1) * P],
                  k_bf[:, half * BANK:(half + 1) * BANK], start=True, stop=True,
                  sig=max_scored if half == HALF - 1 else None)
        st.dve.wait(max_scored.at(TILES * u + t + 1), max_turned.at(u))
        st.dve(nc.vector.tensor_reduce, neg_max[:, t:t + 1], bank, AX.XY, ALU.max, negate=True,
               sig=maxed)
        side.done[slot] = [maxed.at(TILES * u + t + 1)]

    def send_maxima(u):
        slot, bank, emptied = side.take()
        st.pe.wait(*emptied)
        st.pe(nc.tensor.transpose, bank[0:2 * NT, 0, 0:P], neg_max[:, :], core.ident[:, :],
              sig=max_turned)
        st.dve.wait(max_turned.at(u + 1), row_sent.at(32 * u))
        st.dve(nc.vector.tensor_copy, max_rows[:, :], bank[0:2 * NT, 0, 0:P], sig=rows_kept)
        side.done[slot] = [rows_kept.at(u + 1)]
        st.sp.wait(rows_kept.at(u + 1), scored.at(TILES * (u - 1)), zero)
        for a in range(2):
            row = slice(max_row[a], max_row[a] + 1)
            st.load(q_pad[u % 2][a][row, :].rearrange("o (n t) -> o n t", t=P),
                    max_rows[a * NT:(a + 1) * NT, :], row_sent)

    def score(u, kb, a):
        i, t = u % 2, TILES * u + 2 * kb + a
        bank, e = score_banks[t % 2], exps[t % E_BUFS]
        st.pe.wait(q_kept.at(2 * u + 2), k_kept.at(2 * u + 2), row_sent.at(32 * (u + 1)), zero)
        st.pe.wait(exped.at(t - 1))
        for half in range(HALF):
            st.pe(nc.tensor.matmul, bank[:, half, :], k_pad[i][a][:, kb * P:(kb + 1) * P],
                  q_pad[i][a][:, half * BANK:(half + 1) * BANK], start=True, stop=True,
                  sig=scored if half == HALF - 1 else None)
        before = t - E_BUFS
        bu, bkb = before // TILES, before % TILES // 2
        st.act.wait(scored.at(t + 1), weighted.at(NT * bu + bkb + 1),
                    summed.at(ADDS * bu + 2 * max(bkb - 1, 0) + before % 2 + 1))
        st.act(nc.scalar.activation, two(e), bank, ACT.Exp, sig=exped)

    def add(t):
        u, kb, a = t // TILES, t % TILES // 2, t % 2
        if kb == 0:
            return
        st.dve.wait(exped.at(t + 1))
        if kb == 1:
            st.dve.wait(total.at(u))
            first = exps[(t - 2) % E_BUFS]
        else:
            st.dve.wait(summed.at(ADDS * u + 2 * (kb - 2) + a + 1))
            first = acc[a]
        st.dve(nc.vector.tensor_tensor, acc[a], first, exps[t % E_BUFS], ALU.add, sig=summed)

    def weigh(u, kb):
        t = TILES * u + 2 * kb
        st.pe.wait(exped.at(t + 2), v_kept.at(u + 1), out_kept.at(u))
        for half in range(HALF):
            for a in range(2):
                last = half == HALF - 1 and a == 1
                st.pe(nc.tensor.matmul, out[own[a], half, :], v_tok[u % 2][:, kb, own[a]],
                      exps[(t + a) % E_BUFS][:, half * BANK:(half + 1) * BANK], start=kb == 0,
                      stop=kb == NT - 1, sig=weighted if last else None)

    def take_sums(u):
        b, m = units[u]
        st.act.wait(weighted.at(NT * (u + 1)), att_used[b])
        st.act(nc.scalar.copy, two(att[:, m, :]), out, sig=out_kept)
        slot, bank, emptied = side.take()
        st.pe.wait(*emptied, summed.at(ADDS * (u + 1)), core.const_ready)
        for half in range(HALF):
            for a in range(2):
                last = half == HALF - 1 and a == 1
                st.pe(nc.tensor.matmul, bank[own[a], half, :], core.ones[:, 0:WIDE],
                      acc[a][:, half * BANK:(half + 1) * BANK], start=True, stop=True,
                      sig=total if last else None)
        st.act.wait(total.at(u + 1), divided.at(u))
        st.act(nc.scalar.copy, two(sums), bank, sig=sums_kept)
        side.done[slot] = [sums_kept.at(u + 1)]

    def invert(u, piece):
        cols = slice(piece * P, (piece + 1) * P)
        st.dve.wait(sums_kept.at(u + 1))
        st.dve(nc.vector.reciprocal, sums[:, cols], sums[:, cols], sig=inverted)

    def divide(u):
        b, m = units[u]
        st.pool.wait(out_kept.at(u + 1), inverted.at(NT * (u + 1)))
        st.pool(nc.gpsimd.tensor_tensor, att[:, m, :], att[:, m, :], sums, ALU.mult, sig=divided)
        if m == PAIRS - 1:
            finish(b)

    one_bank = FirstBank(side)
    rows, norm, turn = Rows(st, one_bank), Norm(st), Turn(st, one_bank)
    entmax, gate_work = Entmax(st, one_bank), []
    mid = st.sbuf("mid", [P, NT, C])
    affine = st.sem("affine")
    att_used = [None]

    def finish(b):
        tiles = slice(b * NT, (b + 1) * NT)
        st.dve.wait(affine.at(3 * b))
        for n in range(0, NT, 4):
            y = rows(lambda k, m: att[:, k, (n + m) * P:(n + m + 1) * P], lambda k: w_o[:, k, :],
                     bo[:, :], x[:, b * NT + n:b * NT + n + 4, :], mid[:, n:n + 4, :],
                     [divided.at(PAIRS * (b + 1))], n_k=PAIRS)
        att_used.append(y)
        norm(mid[:, :, :], mid[:, :, :], [y])
        st.dve.wait(norm.last)
        st.dve(nc.vector.tensor_tensor, mid[:, :, :], mid[:, :, :], spread(gamma[:, :], NT),
               ALU.mult, sig=affine)
        st.dve.wait(affine.at(3 * b + 1))
        st.dve(nc.vector.tensor_tensor, mid[:, :, :], mid[:, :, :], spread(beta[:, :], NT),
               ALU.add, sig=affine)
        st.dve.wait(affine.at(3 * b + 2))
        st.dve(nc.vector.tensor_tensor, x[:, tiles, :], x[:, tiles, :], mid[:, :, :], ALU.add,
               sig=affine)
        v = norm(x[:, tiles, :], x[:, tiles, :], [affine.at(3 * b + 3)])
        for n in range(b * NT, (b + 1) * NT, 4):
            turn(x[:, n:n + 4, :], xc[:, n * P:n * P + BANK], [v])
        if b + 1 < nb:
            gate_work.extend(entmax.pieces(b, lambda: turn.kept.at(HALF * (b + 1))))

    project_q(0), project_k(0), project_v(0)
    for t in range(TILES):
        maximum(0, t)
    send_maxima(0)
    FIRST_MAX, FIRST_INVERT = 3, 2
    for u in range(len(units)):
        ahead = u + 1 < len(units)
        todo = list(range(TILES)) if ahead else []
        for step in range(TILES):
            kb, a = step // 2, step % 2
            if ahead and step in (0, 1, 2):
                (project_q, project_k, project_v)[step](u + 1)
            if todo and step >= FIRST_MAX:
                maximum(u + 1, todo.pop(0))
            score(u, kb, a)
            gates_now = not FIRST_MAX <= step < FIRST_INVERT + NT
            if gate_work and gates_now:
                gate_work.pop(0)()
            if step:
                add(TILES * u + step - 1)
            if gate_work and gates_now:
                gate_work.pop(0)()
            if todo and step >= FIRST_MAX and len(todo) > TILES - 2 - step:
                maximum(u + 1, todo.pop(0))
            if ahead and step == TILES - 2:
                assert not todo
                send_maxima(u + 1)
            if a == 1 and kb:
                weigh(u, kb - 1)
            elif a == 1 and u:
                weigh(u - 1, NT - 1)
                take_sums(u - 1)
            if u and FIRST_INVERT <= step < FIRST_INVERT + NT:
                invert(u - 1, step - FIRST_INVERT)
            if u and step == FIRST_INVERT + NT:
                divide(u - 1)
            if gate_work and gates_now:
                gate_work.pop(0)()
        add(TILES * u + TILES - 1)
    for work in gate_work:
        work()
    weigh(len(units) - 1, NT - 1)
    take_sums(len(units) - 1)
    for piece in range(NT):
        invert(len(units) - 1, piece)
    divide(len(units) - 1)
    st.run()




def entmax_experts(core):
    st = Stage(core, "moe3")
    nc, inp, nb = core.nc, core.inp, core.n_batch
    x, xc, acc = core.x_tok, core.x_chn, core.x_mid
    small_banks = st.psum("small", 3)
    ring = Ring([small_banks[:, i, :] for i in range(3)])
    w1, w2, b1, b2, w_ready = load_experts(st, core, "L3_ffn", None)
    gates, gate_row = core.gates, st.sbuf("gate_row", [E2, nb * T])
    turned, kept, stored = (st.sem(n) for n in ("gates_turned", "gates_kept", "stored"))
    entmax = Entmax(st, ring)
    gate_work = entmax.pieces(nb - 1, lambda: None)
    n_pieces = len(gate_work) - 1
    PER_EXPERT = 4

    def among():
        for _ in range(min(PER_EXPERT, len(gate_work))):
            gate_work.pop(0)()

    hidden = [st.sbuf(f"hidden{i}", [P, BANK]) for i in range(8)]
    experts = Experts(st, w1, w2, b1, b2[:, :], w_ready, ACT.Relu, [h[:, :] for h in hidden],
                      among)
    norm = Norm(st)
    for b in range(nb):
        while b == nb - 1 and gate_work:
            gate_work.pop(0)()
        gates_ready = entmax.step.at(n_pieces) if b == nb - 1 else None
        for n in range(b * NT, (b + 1) * NT, 4):
            rows_ready = gate_rows_of(st, ring, gates, gate_row, range(n, n + 4), E2,
                                      [gates_ready, core.ident_ready], turned, kept)
            v = experts(xc[:, n * P:n * P + BANK], lambda e, i: gates[:, n + i, e:e + 1],
                        lambda i: gate_row[:, (n + i) * P:(n + i + 1) * P], gates_ready, rows_ready,
                        acc[:, n:n + 4, :], x[:, n:n + 4, :], [])
        tiles = slice(b * NT, (b + 1) * NT)
        v = norm(acc[:, tiles, :], x[:, tiles, :], [v])
        st.sp.wait(v)
        st.load(core.out[b].rearrange("(n p) c -> p n c", p=P), x[:, tiles, :], stored)
    st.sp.wait(stored.at(16 * nb))
    st.run()


def constants():
    bf16 = np.dtype("bfloat16")
    f = np.float32
    c = {"ident": np.eye(P, dtype=f), "ones": np.ones((P, P), f),
         "flip": np.ascontiguousarray(np.eye(P, dtype=f)[::-1])}
    tok_block = np.arange(T) // P
    rows = np.zeros((STACK - STACK_QK, GROUP, T), f)
    for s in range(SPLITS):
        for j in range(NT):
            rows[s * NT + j] = tok_block == j
    rows[STACK_FAR:] = 1.0
    c["key_rows"] = rows.astype(bf16)
    c["zero_rows"] = np.zeros((STACK_FAR, H, T), bf16)
    d = np.arange(ROW) - (P - 1)
    rp = np.maximum(d, 0)
    exact = N_BUCKETS // 2
    big = exact + (np.log(np.maximum(rp, 1).astype(f) / f(exact)) / f(np.log(MAX_DISTANCE / exact))
                   * f(N_BUCKETS - exact)).astype(np.int32)
    bucket = np.where(rp < exact, rp, np.minimum(big, N_BUCKETS - 1))
    hot = np.zeros((N_BUCKETS, 2, ROW), f)
    hot[bucket, 0, np.arange(ROW)] = 1.0
    back = np.arange(ROW)
    at = 2 * P - 1 - back + (P - 1)
    ok = at >= 0
    hot[bucket[np.maximum(at, 0)][ok], 1, back[ok]] = 1.0
    c["bucket_hot"] = hot
    part = np.arange(STACK_FAR) // NT
    key = np.arange(STACK_FAR) % NT
    c["far_level"] = np.stack([part > 0, part > 1], 1).astype(f)
    place = np.zeros((STACK_FAR, 2, NT), f)
    for n in range(NT):
        place[:, 0, n] = n < key
        place[:, 1, n] = n >= key + 2
    c["far_place"] = place
    i = np.arange(P)
    head, chan = i // HD, i % HD
    same = head[:, None] == head[None, :]
    c["same_head"] = same.astype(f)
    v = np.arange(HD)[None, :, None]
    c["pick_v"] = (same[:, None, :] & (chan[:, None, None] == v)).astype(f)
    c["place_v"] = (same[:, None, :] & (chan[None, None, :] == v)).astype(f)
    gate = np.zeros((2 * H, 2, C), f)
    for n in range(2):
        gate[n * H + head, n, i] = 1.0
    c["gate_rows"] = gate
    pair = np.zeros((E1, E1 // 2, P), f)
    for e in range(E1):
        pair[e, e // 2, (e % 2) * I1:(e % 2 + 1) * I1] = 1.0
    c["pair_rows"] = pair
    rotate = np.zeros((P, C), f)
    half = HD // 2
    low = i[chan < half]
    rotate[low + half, low] = -1.0
    rotate[low, low + half] = 1.0
    c["rotate"] = rotate
    freq = f(1.0) / f(10000.0) ** (np.arange(0, HD, 2, dtype=f) / f(HD))
    turn = np.arange(T, dtype=f)[:, None] * freq[None, :].astype(f)
    turn = np.concatenate([turn, turn], axis=-1)[:, chan].T
    c["angle"] = np.stack([np.cos(turn), np.sin(turn)], 1).astype(f)
    for n in (8, E1):
        c[f"ramp{n}"] = np.tile(np.arange(n, 0, -1, dtype=f), (P, 1))
    strip = np.zeros((P, BANK), f)
    strip[:, BANK - P:] = np.where(i[None, :] > i[:, None], f(-1e30), f(0))
    c["causal_strip"] = strip
    c["causal_mask"] = np.where(i[:, None] > i[None, :], f(-1e30), f(0)).astype(bf16)
    return c


def build(nc, inp, const, out, n_batch, upto=99):
    core = Core()
    core.nc, core.inp, core.const, core.out, core.n_batch = nc, inp, const, out, n_batch
    with ExitStack() as ctx:
        def sbuf(name, shape, dtype=F32):
            return ctx.enter_context(nc.sbuf_tensor(name, shape, dtype))

        def dram(name, shape, dtype=F32):
            return nc.dram_tensor(name, shape, dtype, kind="Internal").ap()

        names = iter(range(256))
        core.counts = []
        core.new_count = lambda: Count(ctx.enter_context(nc.semaphore(f"count{next(names)}")))
        core.x_tok = sbuf("x_tok", [P, n_batch * NT, C])
        core.x_chn = sbuf("x_chn", [P, n_batch * T])
        core.x_mid = None
        core.big = sbuf("big", [P, 2 * 4 * T])
        core.attn_w = sbuf("attn_w", [P, 4 * T])
        core.ident, core.ident_bf = sbuf("ident", [P, P]), sbuf("ident_bf", [P, P], BF16)
        core.flip, core.flip_bf = sbuf("flip", [P, P]), sbuf("flip_bf", [P, P], BF16)
        core.ones, core.eps = sbuf("ones", [P, P]), sbuf("eps", [P, 1])
        core.causal_strip = sbuf("causal_strip", [P, BANK])
        core.causal_mask = sbuf("causal_mask", [P, P], BF16)
        core.q_parts = dram("q_parts", (n_batch, SPLITS, C, T), BF16)
        core.k_parts = dram("k_parts", (n_batch, SPLITS, C, T), BF16)
        core.far_bias = dram("far_bias", (STACK_FAR, H, T), BF16)
        core.near_rev = dram("near_rev", (H, ROW))
        core.near_parts = dram("near_parts", (SPLITS, H, ROW), BF16)
        core.bias_stored = Count(ctx.enter_context(nc.semaphore("bias_stored")))

        st = Stage(core, "start")
        loaded, made = Count(ctx.enter_context(nc.semaphore("const_loaded"))), st.sem("made")
        for name, dst in (("ident", core.ident), ("ones", core.ones), ("flip", core.flip),
                          ("causal_strip", core.causal_strip), ("causal_mask", core.causal_mask)):
            t = st.load(dst[:, :], const[name][:, :], loaded)
        core.const_ready = core.ident_ready = t
        core.eps_ready = None
        st.pool(nc.gpsimd.memset, core.eps[:, :], LN_EPS, sig=made)
        st.act.wait(t)
        st.act(nc.scalar.copy, core.ident_bf[:, :], core.ident[:, :], sig=made)
        st.act.wait(t)
        st.act(nc.scalar.copy, core.flip_bf[:, :], core.flip[:, :], sig=made)
        st.run()

        stages = [position_bias, layer0, ternary_ffn, linear_attention, expert_ffn,
                  causal_attention, rotary_attention, block_experts, wide_attention,
                  entmax_experts]
        for n, stage in enumerate(stages):
            if n < upto:
                with ExitStack() as inner:
                    if stage is rotary_attention:
                        mid_ctx = ctx.enter_context(ExitStack())
                        core.x_mid = mid_ctx.enter_context(
                            nc.sbuf_tensor("x_mid", [P, n_batch * NT, C], F32))
                    if stage is wide_attention:
                        core.gates = ctx.enter_context(
                            nc.sbuf_tensor("gates", [P, n_batch * NT, E2], F32))
                    if stage is entmax_experts:
                        core.x_mid = inner.enter_context(
                            nc.sbuf_tensor("x_sum", [P, n_batch * NT, C], F32))
                    stage(core)
                    if stage is block_experts:
                        mid_ctx.close()
        if upto < len(stages):
            st = Stage(core, "end")
            stored = st.sem("stored")
            for b in range(n_batch):
                t = st.load(out[b].rearrange("(n p) c -> p n c", p=P),
                            core.x_tok[:, b * NT:(b + 1) * NT, :], stored)
            st.sp.wait(t)
            st.run()


def layout(inputs):
    out = {}
    for name, a in inputs.items():
        if name == "L0_ffn_weight":
            out["L0_ffn_weight_t"] = a.T
        elif name in ("L1_attn_W_qkv", "L1_attn_W_z", "L1_attn_W_b", "L1_attn_W_a",
                      "L1_attn_W_out", "L3_attn_Wq", "L3_attn_Wk", "L3_attn_Wv", "L3_attn_Wo"):
            out[name + "_t"] = a.T
        elif name in ("L2_attn_b_attn", "L3_attn_bq", "L3_attn_bk"):
            out[name + "_c"] = a.reshape(-1, P).T
        elif name == "L3_attn_adaptive_scale":
            out[name + "_c"] = a.reshape(-1, 2).T
        elif name in ("L2_ffn_b1", "L3_ffn_b1"):
            out[name + "_c"] = a.reshape(E2, -1, P).transpose(2, 0, 1)
        else:
            out[name] = a
    return out


def kernel(**inputs):
    from concourse import bacc
    from concourse.bass_utils import run_bass_kernel_spmd

    nc = bacc.Bacc("TRN2", target_bir_lowering=False, num_devices=1)
    n_batch = inputs["L0_attn_hidden_states"].shape[0]
    arrays, inp, const = {}, {}, {}
    for tensors, source, prefix in ((inp, layout(inputs), "in_"), (const, constants(), "const_")):
        for name, a in source.items():
            a = np.ascontiguousarray(a)
            arrays[prefix + name] = a
            tensors[name] = nc.dram_tensor(prefix + name, a.shape, mybir.dt.from_np(a.dtype),
                                           kind="ExternalInput").ap()
    out = nc.dram_tensor("out", (n_batch, T, C), F32, kind="ExternalOutput").ap()
    build(nc, inp, const, out, n_batch)
    r = run_bass_kernel_spmd(nc, [arrays], core_ids=[0])
    return r.results[0]["out"]
```
